# Optimizing a Trainium2 kernel written in Bass

```python
import numpy as np
import jax
import jax.numpy as jnp

def _softmax(x, axis=-1):
    return jax.nn.softmax(x, axis=axis)

def _gelu(x):
    return jax.nn.gelu(x, approximate=True)

def _silu(x):
    return jax.nn.silu(x)

def _sigmoid(x):
    return jax.nn.sigmoid(x)

def _layernorm(x, axis=-1, eps=1e-05):
    m = jnp.mean(x, axis=axis, keepdims=True)
    v = jnp.var(x, axis=axis, keepdims=True)
    return (x - m) / jnp.sqrt(v + eps)

def _scatter_add(tgt, idx, src, axis=0):
    return tgt.at[idx].add(src)

def _segment_sum(src, seg, n):
    return jax.ops.segment_sum(src, seg, n)
kernel_name = 'mk_adaln_ffn_d2_seqx_r8_2405c1'

def setup_inputs(seed: int=0):
    np.random.seed(seed)
    _w = jnp.asarray

    def _rec_inputs():
        import jax
        import jax.numpy as jnp
        _rk = jax.random.key(seed)
        x = -7.109e-05 + 0.9999 * jax.random.normal(jax.random.fold_in(_rk, 1), (128, 32, 512), jnp.float32)
        _lenS = 32 - jax.random.randint(jax.random.fold_in(_rk, 7), (128,), 0, max(1, 32 // 4) + 1, jnp.int32)
        _lenS2 = 32 - jax.random.randint(jax.random.fold_in(_rk, 8), (128,), 0, max(1, 32 // 4) + 1, jnp.int32)
        itok_B_0_30 = jax.random.randint(jax.random.fold_in(_rk, 11), (128,), 0, 31, jnp.int32)
        itok_B_2_6 = jax.random.randint(jax.random.fold_in(_rk, 12), (128,), 2, 7, jnp.int32)
        return (x, itok_B_0_30, itok_B_2_6)
    x, itok_B_0_30, itok_B_2_6 = _rec_inputs()

    def _L0_cond_setup():
        import jax, jax.numpy as jnp
        import numpy as np
        B, C, D, T, S = (64, 32, 32, 512, 32)
        key = jax.random.key(seed)
        k1, k2, k3 = jax.random.split(key, 3)
        x = jax.random.normal(k1, (B, C, T), dtype=jnp.float32)
        subjects = jax.random.randint(k2, (B,), 0, S, dtype=jnp.int64)
        weights = jax.random.normal(k3, (S, C, D), dtype=jnp.float32) * (1.0 / np.sqrt(C))
        return {'x': x, 'subjects': subjects, 'weights': weights}
    _L0_cond_all = _L0_cond_setup()
    _L0_cond_in = {k: v for k, v in _L0_cond_all.items() if k in ('weights',)}
    del _L0_cond_all

    def _L0_ffn_setup():
        import jax, jax.numpy as jnp
        import numpy as np
        SCALING = 32.0 / 16.0
        key = jax.random.key(seed)
        ks = jax.random.split(key, 7)
        B, T, D, O, R, E = (4, 256, 512, 512, 16, 8)
        x = jax.random.normal(ks[0], (B, T, D), dtype=jnp.float32)
        base_W = jax.random.normal(ks[1], (O, D), dtype=jnp.float32) * D ** (-0.5)
        base_b = jax.random.normal(ks[2], (O,), dtype=jnp.float32) * 0.01
        router_W = jax.random.normal(ks[3], (2 * E - 1, D), dtype=jnp.float32) * D ** (-0.5)
        router_b = jax.random.normal(ks[4], (2 * E - 1,), dtype=jnp.float32) * 0.01
        A = jax.random.normal(ks[5], (E, R, D), dtype=jnp.float32) * D ** (-0.5)
        Bm = jax.random.normal(ks[6], (E, O, R), dtype=jnp.float32) * R ** (-0.5)
        assigned_idx = 0
        others = [i for i in range(E) if i != assigned_idx]
        expert_map = jnp.array([assigned_idx] * E + others, dtype=jnp.int32)
        return {'x': x, 'base_W': base_W, 'base_b': base_b, 'router_W': router_W, 'router_b': router_b, 'A': A, 'B': Bm, 'expert_map': expert_map}
    _L0_ffn_all = _L0_ffn_setup()
    _L0_ffn_in = {k: v for k, v in _L0_ffn_all.items() if k in ('base_W', 'base_b', 'router_W', 'router_b', 'A', 'B', 'expert_map')}
    del _L0_ffn_all

    def _L1_cond_setup():
        import jax, jax.numpy as jnp
        import numpy as np
        B, N, H, F = (4, 64, 512, 1376)
        L, R, RANK = (1, 16, 16)
        SCALE = 0.5
        key = jax.random.key(seed)
        ks = jax.random.split(key, 12)
        nrm = lambda k, shape, fan: jax.random.normal(k, shape, jnp.float32) * fan ** (-0.5)
        inp = {'x': jax.random.normal(ks[0], (B, N, H), jnp.float32), 'W_gate': nrm(ks[1], (F, H), H), 'W_up': nrm(ks[2], (F, H), H), 'W_down': nrm(ks[3], (H, F), F), 'A_gate': nrm(ks[4], (L, R, RANK, H), H), 'B_gate': nrm(ks[5], (L, R, F, RANK), RANK), 'A_up': nrm(ks[6], (L, R, RANK, H), H), 'B_up': nrm(ks[7], (L, R, F, RANK), RANK), 'A_down': nrm(ks[8], (L, R, RANK, F), F), 'B_down': nrm(ks[9], (L, R, H, RANK), RANK), 'lora_indices': jax.random.randint(ks[10], (B,), 0, R), 'layer_idx': 0}
        return inp
    _L1_cond_all = _L1_cond_setup()
    _L1_cond_in = {k: v for k, v in _L1_cond_all.items() if k in ('W_gate', 'W_up', 'W_down', 'A_gate', 'B_gate', 'A_up', 'B_up', 'A_down', 'B_down')}
    del _L1_cond_all

    def _L1_ffn_setup():
        import jax, jax.numpy as jnp
        import numpy as np
        IN_F = 512
        OUT_F = 512
        N_CLUSTERS = 64
        THRESHOLD = 0.01
        TEMPERATURE = 0.1
        BATCH, SEQ = (4, 256)
        key = jax.random.key(seed)
        k1, k2, k3, k4, k5 = jax.random.split(key, 5)
        s = 1.0 / np.sqrt(IN_F)
        return {'input': jax.random.normal(k1, (BATCH, SEQ, IN_F), dtype=jnp.float32), 'weight': jax.random.normal(k2, (OUT_F, IN_F), dtype=jnp.float32) * s, 'bias': jax.random.uniform(k3, (OUT_F,), dtype=jnp.float32, minval=-s, maxval=s), 'centroids': jax.random.normal(k4, (N_CLUSTERS, IN_F), dtype=jnp.float32) * s, 'assignments': jax.random.randint(k5, (OUT_F,), 0, N_CLUSTERS, dtype=jnp.int32)}
    _L1_ffn_all = _L1_ffn_setup()
    _L1_ffn_in = {k: v for k, v in _L1_ffn_all.items() if k in ('weight', 'bias', 'centroids', 'assignments')}
    del _L1_ffn_all
    return {'x': x, 'itok_B_0_30': itok_B_0_30, 'itok_B_2_6': itok_B_2_6, 'L0_cond_weights': _L0_cond_in['weights'], 'L0_ffn_base_W': _L0_ffn_in['base_W'], 'L0_ffn_base_b': _L0_ffn_in['base_b'], 'L0_ffn_router_W': _L0_ffn_in['router_W'], 'L0_ffn_router_b': _L0_ffn_in['router_b'], 'L0_ffn_A': _L0_ffn_in['A'], 'L0_ffn_B': _L0_ffn_in['B'], 'L0_ffn_expert_map': _L0_ffn_in['expert_map'], 'L1_cond_W_gate': _L1_cond_in['W_gate'], 'L1_cond_W_up': _L1_cond_in['W_up'], 'L1_cond_W_down': _L1_cond_in['W_down'], 'L1_cond_A_gate': _L1_cond_in['A_gate'], 'L1_cond_B_gate': _L1_cond_in['B_gate'], 'L1_cond_A_up': _L1_cond_in['A_up'], 'L1_cond_B_up': _L1_cond_in['B_up'], 'L1_cond_A_down': _L1_cond_in['A_down'], 'L1_cond_B_down': _L1_cond_in['B_down'], 'L1_ffn_weight': _L1_ffn_in['weight'], 'L1_ffn_bias': _L1_ffn_in['bias'], 'L1_ffn_centroids': _L1_ffn_in['centroids'], 'L1_ffn_assignments': _L1_ffn_in['assignments']}

def reference(x, itok_B_0_30, itok_B_2_6, L0_cond_weights, L0_ffn_base_W, L0_ffn_base_b, L0_ffn_router_W, L0_ffn_router_b, L0_ffn_A, L0_ffn_B, L0_ffn_expert_map, L1_cond_W_gate, L1_cond_W_up, L1_cond_W_down, L1_cond_A_gate, L1_cond_B_gate, L1_cond_A_up, L1_cond_B_up, L1_cond_A_down, L1_cond_B_down, L1_ffn_weight, L1_ffn_bias, L1_ffn_centroids, L1_ffn_assignments):
    import jax
    import jax.numpy as jnp

    def _L0_cond_ref(x, subjects, weights):
        import jax, jax.numpy as jnp
        import numpy as np
        B, C, D, T, S = (64, 32, 32, 512, 32)
        w = weights[subjects]
        return jnp.einsum('bct,bcd->bdt', x, w)

    def _L0_ffn_ref(x, base_W, base_b, router_W, router_b, A, B, expert_map):
        import jax, jax.numpy as jnp
        import numpy as np
        SCALING = 32.0 / 16.0
        E = A.shape[0]
        base_out = jnp.einsum('btd,od->bto', x, base_W) + base_b
        logits = jnp.einsum('btd,nd->btn', x, router_W) + router_b
        probs = jax.nn.softmax(logits, axis=-1)
        topk_p, topk_i = jax.lax.top_k(probs, E)
        mapped = expert_map[topk_i]
        onehot = (mapped[..., None] == jnp.arange(E)).astype(x.dtype)
        w = jnp.einsum('btk,btke->bte', topk_p, onehot)
        h = jnp.einsum('btd,erd->bter', x, A)
        lora = jnp.einsum('bter,eor->bto', h * w[..., None], B) * SCALING
        return base_out + lora

    def _L1_cond_ref(x, W_gate, W_up, W_down, A_gate, B_gate, A_up, B_up, A_down, B_down, lora_indices, layer_idx):
        import jax, jax.numpy as jnp
        import numpy as np
        B, N, H, F = (4, 64, 512, 1376)
        L, R, RANK = (1, 16, 16)
        SCALE = 0.5

        def lora_add(base, inp, A, B):
            Ab = A[layer_idx][lora_indices]
            Bb = B[layer_idx][lora_indices]
            t = jnp.einsum('bri,bni->bnr', Ab, inp)
            return base + jnp.einsum('bor,bnr->bno', Bb, t) * SCALE
        gate = lora_add(jnp.einsum('bnh,fh->bnf', x, W_gate), x, A_gate, B_gate)
        up = lora_add(jnp.einsum('bnh,fh->bnf', x, W_up), x, A_up, B_up)
        act = jax.nn.silu(gate) * up
        down = lora_add(jnp.einsum('bnf,hf->bnh', act, W_down), act, A_down, B_down)
        return down

    def _L1_ffn_ref(input, weight, bias, centroids, assignments):
        import jax, jax.numpy as jnp
        import numpy as np
        IN_F = 512
        OUT_F = 512
        N_CLUSTERS = 64
        THRESHOLD = 0.01
        TEMPERATURE = 0.1
        BATCH, SEQ = (4, 256)
        shape = input.shape
        x = input.reshape(-1, shape[-1])
        dots = jax.nn.softmax(x @ centroids.T / TEMPERATURE, axis=-1)
        hits = dots > THRESHOLD
        query_sel = jnp.any(hits, axis=1)
        cluster_sel = jnp.any(hits, axis=0)
        row_sel = cluster_sel[assignments]
        dense = x @ weight.T + bias
        out = jnp.where(query_sel[:, None] & row_sel[None, :], dense, jnp.zeros((), dense.dtype))
        return out.reshape(*shape[:-1], -1)
    x = x + _L0_ffn_ref(_L0_cond_ref(x, itok_B_0_30, L0_cond_weights), L0_ffn_base_W, L0_ffn_base_b, L0_ffn_router_W, L0_ffn_router_b, L0_ffn_A, L0_ffn_B, L0_ffn_expert_map)
    x = x + _L1_ffn_ref(_L1_cond_ref(x, L1_cond_W_gate, L1_cond_W_up, L1_cond_W_down, L1_cond_A_gate, L1_cond_B_gate, L1_cond_A_up, L1_cond_B_up, L1_cond_A_down, L1_cond_B_down, itok_B_2_6, 0), L1_ffn_weight, L1_ffn_bias, L1_ffn_centroids, L1_ffn_assignments)
    return x

_drawn_inputs = setup_inputs


def setup_inputs(seed=0):
    import zlib

    import numpy as np

    out = dict(_drawn_inputs(seed))
    spreads = {}
    factors = {'L0_ffn_base_b': 7.811, 'L0_ffn_router_b': 4.471, 'L1_ffn_bias': 8.0}
    for name, (base, spread) in spreads.items():
        noise = np.random.default_rng([zlib.crc32(name.encode()), seed]).standard_normal(out[name].shape)
        drawn = base * np.exp(spread * noise) if base else spread * noise
        out[name] = jnp.asarray(drawn.astype(out[name].dtype))
    for name, factor in factors.items():
        out[name] = (out[name] * factor).astype(out[name].dtype)
    return out
```

```python
from contextlib import ExitStack

import numpy as np

import concourse.bass as bass
from concourse import mybir
from concourse.alu_op_type import AluOpType as ALU

F32 = mybir.dt.float32
F32R = mybir.dt.float32r
I32 = mybir.dt.int32
U32 = mybir.dt.uint32
ACT = mybir.ActivationFunctionType
AX = mybir.AxisListType

P = 128
BATCH, SEQ, D = 128, 32, 512
TOKENS = BATCH * SEQ
N = 512
TILES = TOKENS // N
KD = D // P
BLK = N // P
SPB = P // SEQ
E, R0 = 8, 16
NR = 2 * E
F = 1376
FC = -(-F // P)
RANK = 16
ADAPTERS = 16
WIN = P // RANK * SEQ
NW = N // WIN
SPW = P // RANK
SPT = N // SEQ
CL = 64
THRESHOLD = 0.01
TEMPERATURE = 0.1
SCALING = 32.0 / 16.0
SCALE = 0.5

GATE, UP, DOWN = range(3)
FRONT = 4 + 1 + 1 + 1 + 1 + KD + 2
SPARE = FRONT + 1
USE = {("cond", j): j for j in range(4)} | {("router", 0): 4, ("probs", 0): 5, ("expand", 0): 6, ("h", 0): 7} \
    | {("base", m): 8 + m for m in range(KD)} | {("lora", u): 8 + KD + u for u in range(2)}


class Tile:

    def __init__(self, i, k):
        self.i, self.k, self.par = i, k, k % 2
        self.fixed = isinstance(i, int)

    def next(self):
        return Tile(self.i, self.k + 1)

    def count(self, per_tile, n):
        if self.fixed:
            return per_tile * (2 * self.i + self.k) + n
        return 2 * per_tile * self.i + (per_tile * self.k + n)

    def index(self):
        return self.count(1, 0)

    def chunk(self, c):
        g = FC * self.k + c
        half = g // 2 + 1
        if self.fixed:
            return g % 2, FC * self.i + half
        return g % 2, FC * self.i + half

    def has_chunk(self, c):
        return not self.fixed or FC * (2 * self.i + self.k) + c < FC * TILES

    def exists(self):
        return not self.fixed or 2 * self.i + self.k < TILES


def wait(engine, semaphore, value):
    if not isinstance(value, int) or value > 0:
        engine.wait_ge(semaphore, value)


def body_steps(t, n):
    front = {
        3: ([("prep_x", 0)], [("cond", 0), ("prep_x", 1)], [("cond", 1), ("prep_x", 2)]),
        4: ([], [("cond", 2), ("prep_x", 3)], [("cond", 3)]),
        5: ([], [("router", 0)], [("prep_a", 0)]),
        6: ([], [], [("probs", 0)]),
        7: ([], [("expand", 0)], [("h", 0)]),
        8: ([], [("base", 0)], [("base", 1)]),
        9: ([], [("base", 2)], [("base", 3)]),
        10: ([], [], [("lora", 0)]),
    }
    for c in range(3, FC):
        before, mid, late = front[c] if n else ([], [], [])
        if c == 5 and not n:
            yield "prep_ffn", 0, t
        yield from ((s, j, n) for s, j in before)
        yield "gate", c, t
        if c == 6:
            yield "prep_b", 0, t
        yield from ((s, j, n) for s, j in mid)
        yield "up", c, t
        yield from ((s, j, n) for s, j in late)
        yield "down", c - 1, t
        if c == FC - 1 and n:
            yield "lora", 1, n
    yield from seam_steps(t, n)


def seam_steps(t, n):
    if n:
        yield "gate", 0, n
        yield "up", 0, n
    yield "down", FC - 1, t
    if n:
        yield "gate", 1, n
        yield "up", 1, n
    if t:
        yield "final", 0, t
    if n:
        yield "gate", 2, n
        yield "down", 0, n
    if t:
        yield "cluster", 0, t
    if n:
        yield "up", 2, n
        yield "down", 1, n


def front_steps(n):
    yield from ((s, j, n) for s, j in (
        ("prep_x", 0), ("cond", 0), ("prep_x", 1), ("cond", 1), ("prep_x", 2), ("cond", 2), ("prep_x", 3),
        ("cond", 3), ("router", 0), ("prep_a", 0), ("probs", 0), ("expand", 0), ("h", 0),
        ("base", 0), ("base", 1), ("base", 2), ("base", 3), ("lora", 0), ("lora", 1)))


def adaln_ffn_kernel(nc, x_rows, x_cols, subj_rows, lora_rows, lora_index, cond_w, base_w, base_b, router_w,
                     router_b, a0, b0, expert_map, w1, a_gu, b_gu, a_dn, b_dn, ffn_w, ffn_b, centroids,
                     assignments, out):
    ctx = ExitStack()
    with ctx:
        def sb(name, shape, dt=F32):
            return ctx.enter_context(nc.sbuf_tensor(name, shape, dt))

        def pair(name, shape):
            return sb(name + "_hi", shape, F32R), sb(name + "_lo", shape, F32R)

        def sem(name):
            return ctx.enter_context(nc.semaphore(name))

        x1_dram = nc.dram_tensor("x1_scratch", [TILES, KD, P, N], F32, kind="Internal").ap()
        d_dram = nc.dram_tensor("d_scratch", [TILES, P, KD * N], F32, kind="Internal").ap()

        w_raw = sb("w_raw", [P, 2, 3, N])
        w_hi, w_lo = zip(*[pair(f"w{q}", [P, N]) for q in ("gate", "up", "down")])
        b_raw = sb("b_raw", [P, 2, NW, 2 * P])
        b_hi, b_lo = zip(*[pair(f"b{q}", [P, NW, P]) for q in ("gate", "up")])
        ad_raw = sb("ad_raw", [P, SPT, FC, RANK])
        ad_hi, ad_lo = pair("ad", [P, SPT, RANK])
        ag_raw = sb("ag_raw", [P, SPT, KD * 2, RANK])
        da_hi, da_lo = pair("da", [P, KD * N])
        bd_hi, bd_lo = pair("bd", [P, NW, D])
        x_raw = sb("x_raw", [P, 2, D])
        x_hi, x_lo = pair("x", [P, D])
        mixw = sb("mixw", [P, 2, SPB, SEQ])
        mix = sb("mix", [P, SPB, SEQ])
        mix_hi, mix_lo = pair("mix", [P, P])
        xc_hi, xc_lo = pair("xc", [P, KD, N])
        res = sb("res", [P, 2, N])
        x1_hi, x1_lo = zip(*[pair(f"x1_{q}", [P, KD, N]) for q in range(2)])
        s = sb("s", [P, 2, N])
        act_hi, act_lo = pair("act", [P, N])
        hw = sb("hw", [P, N])
        hw_hi, hw_lo = pair("hw", [P, N])
        ranks = sb("ranks", [P, 2, N])
        probs_t = ranks[0:NR, 1, :]
        gu_hi, gu_lo = zip(*[pair(f"rank{q}", [P, N]) for q in ("gate", "up")])
        d_raw = sb("d_raw", [P, KD, N])
        bd_raw = d_raw[:, 0:NW, :]

        base_hi, base_lo = pair("base", [P, KD, D])
        a0_hi, a0_lo = pair("a0", [P, KD, P])
        b0_hi, b0_lo = pair("b0", [P, D])
        rt_hi, rt_lo = pair("rt", [P, KD, NR])
        ct_hi, ct_lo = pair("ct", [P, KD, CL])
        bias0 = sb("bias0", [P, KD])
        bias1 = sb("bias1", [P, KD])
        rbias = sb("rbias", [P, NR])
        rank_mask = sb("rank_mask", [P, SPW, SEQ])
        mix_mask = sb("mix_mask", [P, SPB, SEQ])
        ident = sb("ident", [P, P])
        e_index = sb("e_index", [NR, E, R0])
        map_i = sb("map_i", [NR, 1], I32)
        map_f = sb("map_f", [NR, 1])
        spread = sb("spread", [NR, E, R0])
        part = sb("part", [P, 1], I32)
        low5 = sb("low5", [P, 1], I32)
        low4 = sb("low4", [P, 1], I32)
        low5f = sb("low5f", [P, 1])
        low4f = sb("low4f", [P, 1])
        part_f = sb("part_f", [P, 1])
        subj_i = sb("subj_i", [P, TILES * BLK], I32)
        subj_row = sb("subj_row", [P, TILES * BLK], U32)
        lora_i = sb("lora_i", [P, TILES * NW], I32)
        lora_row = sb("lora_row", [P, TILES * NW], U32)
        subj_now = sb("subj_now", [P, 2, BLK], U32)
        lora_now = sb("lora_now", [P, 2, NW], U32)
        index_i = sb("index_i", [1, BATCH], I32)
        logit = sb("logit", [P, BLK, NR])
        chosen = sb("chosen", [P, BLK, NR])
        top = sb("top", [P, BLK, 8])
        stat = sb("stat", [P, 4, BLK])
        cl = sb("cl", [P, BLK, CL])
        cl_stat = sb("cl_stat", [P, 3, BLK])
        cl_best = sb("cl_best", [P, BLK, CL])
        hit = sb("hit", [P, TILES * BLK])

        bank = [ctx.enter_context(nc.psum_tensor(f"bank{b}", [P, N], F32)) for b in range(8)]
        p_gate, p_up, p_rank, spare = bank[0], bank[1], bank[2], bank[3]
        p_d = bank[4:8]

        in_w = [[sem(f"in_w{a}{q}") for q in range(3)] for a in range(2)]
        in_b = [sem(f"in_b{a}") for a in range(2)]
        in_ad, in_ag, in_bd = sem("in_ad"), sem("in_ag"), sem("in_bd")
        in_x = [sem(f"in_x{a}") for a in range(2)]
        in_mix = [sem(f"in_mix{a}") for a in range(2)]
        in_res = [sem(f"in_res{a}") for a in range(2)]
        out_x1 = [sem(f"out_x1{a}") for a in range(2)]
        out_d = sem("out_d")
        in_index, in_small, in_first = sem("in_index"), sem("in_small"), sem("in_first")
        in_ffn, in_assign = sem("in_ffn"), sem("in_assign")
        in_d = [sem(f"in_d{a}") for a in range(2)]
        in_x1 = [sem(f"in_x1{a}") for a in range(2 * KD)]
        out_y = [sem(f"out_y{a}") for a in range(2 * KD)]

        pe = {q: sem("pe_" + q) for q in ("gate", "up", "down", "cond", "router", "probs", "expand", "h", "base",
                                          "lora", "final", "cluster", "dense", "hits", "best", "rows")}
        spare_free = sem("spare_free")
        parts = ("wg", "wu", "wd", "bg", "bu", "ad", "act", "x", "mix", "ag", "bd", "hw", "x1", "lora", "rank", "d",
                 "const", "ffn")
        hi = {q: sem("hi_" + q) for q in (*parts, "xc")}
        lo = {q: sem("lo_" + q) for q in parts}
        silu_done, prod_done = sem("silu_done"), sem("prod_done")
        mix_made, rank_made = sem("mix_made"), sem("rank_made")
        d_act, d_dve = sem("d_act"), sem("d_dve")
        exp_ready, exp_done, chosen_done = sem("exp_ready"), sem("exp_done"), sem("chosen_done")
        cl_exp = sem("cl_exp")
        route_step, cl_step, start_step = sem("route_step"), sem("cl_step"), sem("start_step")
        pool_zero, pool_const, pool_lora, pool_mix = (
            sem(q) for q in ("pool_zero", "pool_const", "pool_lora", "pool_mix"))
        index_made, spread_made, best_cleared = sem("index_made"), sem("spread_made"), sem("best_cleared")
        waits_passed = sem("waits_passed")
        identr_made, hits_spread, hits_copied, dense_free, y_made, sel_step, rows_ready = (
            sem(q) for q in ("identr_made", "hits_spread", "hits_copied", "dense_free", "y_made", "sel_step",
                             "rows_ready"))

        d_in = [ag_raw[:].rearrange("p s g r -> p (s g r)"), d_raw[:].rearrange("p k n -> p (k n)")]
        ad_flat = ad_raw[:].rearrange("p s c r -> p (s c r)")
        y_buf = [w_raw[:, a, q, :] for a in range(2) for q in range(3)] + [ad_flat[:, 0:N], ad_flat[:, N:2 * N]]
        hit_spread = da_hi[:, 0:BLK * P].rearrange("p (b c) -> p b c", b=BLK)
        ident_r = da_lo[:, 0:P]
        dense_bank = [bank[0], bank[1], bank[4], bank[5]]
        b_flat = b_raw[0:CL].rearrange("p a w n -> p (a w n)")
        assign_i, onehot = b_flat[:, 0:D].bitcast(I32), b_flat[:, D:2 * D]
        best_1 = ad_flat[:, 2 * N:2 * N + CL]
        best_2 = ad_flat[0:CL, 2 * N + CL:2 * N + CL + 1]
        sel = ad_flat[0:CL, 2 * N + CL + 1:2 * N + CL + 2]
        row_sel = ad_flat[:, 2 * N + CL + 2:2 * N + CL + 2 + KD]
        assign_f = s[0:CL, 0, :]

        def by_window(x):
            return x[:].rearrange("p (w g s r) -> p w g s r", w=NW, g=2 * KD, s=SPW)

        ag_by_window = ag_raw[:].rearrange("p (w s) g r -> p w g s r", w=NW)

        x_blocks = x_rows.rearrange("(b p) d -> b p d", p=P)
        x_cols_t = x_cols.rearrange("(m p) n -> m p n", p=P)

        def tokens(t):
            return bass.ds(N * t.index(), N)

        def passed(engine):
            engine.sem_inc(waits_passed, 1)

        block = ctx.enter_context(nc.Block())

        @block.sync
        def _(sp):
            def load_w(t, c, q, after):
                a, n = t.chunk(c)
                if after is not None:
                    sp.wait_ge(lo[("wg", "wu", "wd")[q]], after)
                sp.dma_start(w_raw[:, a, q, :], w1[c % FC, q]).then_inc(in_w[a][q], 16)

            def load_x(t, j):
                sp.dma_start(x_raw[:, j % 2, :],
                             x_blocks[bass.ds(t.count(BLK, j), 1)].rearrange("b p d -> p (b d)")).then_inc(in_x[j % 2], 16)

            def load_res(t, m):
                sp.dma_start(res[:, m % 2, :], x_cols_t[m, :, tokens(t)]).then_inc(in_res[m % 2], 16)

            def load_adapters(t, table, dst, done):
                passed(sp)
                for j in range(SPT):
                    which = sp.value_load(index_i[0:1, bass.ds(t.count(SPT, j), 1)], min_val=0, max_val=ADAPTERS - 1)
                    sp.dma_start(dst[:, j].rearrange("p c r -> p (c r)"),
                                 table[bass.ds(which, 1)].rearrange("o p n -> p (o n)")).then_inc(done, 16)

            def serve(steps):
                for step, j, t in steps:
                    if step in ("gate", "up") and t.has_chunk(j + 3):
                        load_w(t, j + 3, GATE if step == "gate" else UP, t.count(FC, j + 2))
                    if step == "down":
                        if t is None:
                            load_w(Tile(0, 0), 2, DOWN, 1)
                        elif t.has_chunk(j + 3):
                            load_w(t, j + 3, DOWN, t.count(FC, j + 2))
                        if t is not None and j == FC - 2 and t.next().exists():
                            sp.wait_ge(lo["ad"], t.count(FC, FC))
                            load_adapters(t.next(), a_dn, ad_raw, in_ad)
                    if step == "prep_x" and (j < 2 or t.next().exists()):
                        sp.wait_ge(lo["x"], t.count(BLK, j + 1))
                        if j < 2:
                            load_x(t, j + 2)
                        else:
                            load_x(t.next(), j - 2)
                    if step == "prep_a" and t.next().exists():
                        sp.wait_ge(lo["ag"], t.count(1, 1))
                        load_adapters(t.next(), a_gu, ag_raw, in_ag)
                    if step == "base":
                        sp.wait_ge(spare_free, t.count(SPARE, USE[step, j] + 1))
                        sp.dma_start(x1_dram[bass.ds(t.index(), 1), j].rearrange("o p n -> p (o n)"),
                                     res[:, j % 2, :]).then_inc(out_x1[j % 2], 16)
                    if step == "base" and j > 0 and (j < 3 or t.next().exists()):
                        sp.wait_ge(out_x1[(j - 1) % 2], 16 * t.count(2, (j - 1) // 2 + 1))
                        sp.wait_ge(lo["x1"], t.count(KD, j))
                        if j < 3:
                            load_res(t, j + 1)
                        else:
                            load_res(t.next(), 0)
                    if step == "lora" and j == 0 and t.next().exists():
                        sp.wait_ge(out_x1[1], 16 * t.count(2, 2))
                        sp.wait_ge(lo["x1"], t.count(KD, KD))
                        load_res(t.next(), 1)
                    if step == "prep_ffn":
                        sp.wait_ge(lo["ffn"], 1)
                        sp.dma_start(d_in[0], d_dram[0]).then_inc(in_d[0], 16)
                    if step == "final":
                        sp.wait_ge(d_act, t.count(1, 1))
                        sp.wait_ge(d_dve, t.count(1, 1))
                        sp.dma_start(d_dram[bass.ds(t.index(), 1)].rearrange("o p n -> p (o n)"),
                                     d_raw[:].rearrange("p k n -> p (k n)")).then_inc(out_d, 16)

            t0 = Tile(0, 0)
            sp.dma_start(lora_i[:], lora_rows).then_inc(in_index, 16)
            sp.dma_start(subj_i[:], subj_rows).then_inc(in_index, 16)
            sp.dma_start(index_i[:], lora_index).then_inc(in_index, 16)
            load_x(t0, 0)
            load_x(t0, 1)
            sp.wait_ge(pool_zero, 2)
            sp.dma_start(rbias[:, 0:NR - 1], router_b.to_broadcast([P, NR - 1])).then_inc(in_small, 16)
            sp.dma_start(map_i[0:NR - 1], expert_map).then_inc(in_small, 16)
            sp.dma_start(bias0[:], base_b).then_inc(in_small, 16)
            sp.dma_start(bias1[:], ffn_b).then_inc(in_small, 16)
            small = d_in[0]
            at = 0
            for w in (router_w, a0, b0, centroids):
                sp.dma_start(small[:, at:at + w.shape[1]], w).then_inc(in_first, 16)
                at += w.shape[1]
            sp.dma_start(d_in[1], base_w).then_inc(out_d, 16)
            load_res(t0, 0)
            load_res(t0, 1)
            for c in range(2):
                for q in range(3):
                    load_w(t0, c, q, None)
            sp.wait_ge(lo["const"], 4)
            sp.wait_ge(in_index, 48)
            load_adapters(t0, a_gu, ag_raw, in_ag)
            load_adapters(t0, a_dn, ad_raw, in_ad)
            load_w(t0, 2, GATE, 1)
            load_w(t0, 2, UP, 1)
            serve(front_steps(t0))
            serve(seam_steps(None, t0))
            with sp.Fori(0, TILES // 2 - 1) as i:
                for k in range(2):
                    serve(body_steps(Tile(i, k), Tile(i, k + 1)))
            serve(body_steps(Tile(0, TILES - 2), Tile(0, TILES - 1)))

            sp.wait_ge(lo["ag"], TILES)
            sp.dma_start(d_in[0], ffn_w).then_inc(in_ffn, 16)
            serve(body_steps(Tile(0, TILES - 1), None))

            def load_d(t):
                sp.dma_start(d_in[t.par], d_dram[bass.ds(t.index(), 1)].rearrange("o p n -> p (o n)"))\
                    .then_inc(in_d[t.par], 16)

            def load_x1(t, m):
                b = KD * t.par + m
                sp.dma_start(y_buf[b], x1_dram[bass.ds(t.index(), 1), m].rearrange("o p n -> p (o n)"))\
                    .then_inc(in_x1[b], 16)

            def store_y(t, m):
                b = KD * t.par + m
                sp.wait_ge(y_made, t.count(KD, m + 1))
                sp.dma_start(out[m * P:(m + 1) * P, tokens(t)], y_buf[b]).then_inc(out_y[b], 16)

            for q in range(2):
                sp.wait_ge(out_x1[q], 16 * 2 * TILES)
            for q in ("wg", "wu", "wd", "ad", "bg", "bu"):
                sp.wait_ge(lo[q], FC * TILES)
            sp.dma_start(assign_i, assignments.to_broadcast([CL, D])).then_inc(in_assign, 16)
            for k in range(2):
                for m in range(KD):
                    load_x1(Tile(0, k), m)
            sp.wait_ge(out_d, 16 * (TILES + 1))
            sp.wait_ge(lo["d"], TILES + 1)
            load_d(Tile(0, 1))
            with sp.Fori(0, TILES // 2 - 1) as i:
                for k in range(2):
                    t = Tile(i, k)
                    sp.wait_ge(lo["d"], TILES + t.count(1, 2))
                    load_d(Tile(i, k + 2))
                    for m in range(KD):
                        store_y(t, m)
                    for m in range(KD):
                        sp.wait_ge(out_y[KD * k + m], 16 * (i + 1))
                        load_x1(Tile(i, k + 2), m)
            for k in range(TILES - 2, TILES):
                for m in range(KD):
                    store_y(Tile(0, k), m)
            for b in range(8):
                sp.wait_ge(out_y[b], 16 * (TILES // 2))

        @block.gpsimd
        def _(pool):
            def set_lora_rows(t):
                nc.gpsimd.tensor_copy(lora_now[:, t.par, :], lora_row[:, bass.ds(t.count(NW, 0), NW)])\
                    .then_inc(pool_lora, 1)
                pool.wait_ge(pool_lora, t.count(1, 1))

            def gather_mix(t):
                nc.gpsimd.tensor_copy(subj_now[:, t.par, :], subj_row[:, bass.ds(t.count(BLK, 0), BLK)])\
                    .then_inc(pool_mix, 1)
                pool.wait_ge(pool_mix, t.count(1, 1))
                passed(pool)
                for j in range(BLK):
                    nc.gpsimd.indirect_dma_start(
                        mixw[:, t.par, j, :], None, cond_w,
                        bass.IndirectOffsetOnAxis(subj_now[:, t.par, j:j + 1], 0)).then_inc(in_mix[t.par], 16)

            def gather_b(t, c):
                a, _ = t.chunk(c)
                rows = t if c < FC else t.next()
                passed(pool)
                for w in range(NW):
                    nc.gpsimd.indirect_dma_start(
                        b_raw[:, a, w, :], None, b_gu,
                        bass.IndirectOffsetOnAxis(lora_now[:, rows.par, w:w + 1], 0),
                        element_offset=(c % FC) * ADAPTERS * RANK * 2 * P).then_inc(in_b[a], 16)

            def serve(steps):
                for step, j, t in steps:
                    if step == "gate" and j == 3:
                        pool.wait_ge(out_d, 16 * t.count(1, 1))
                        pool.wait_ge(lo["d"], t.count(1, 1))
                        passed(pool)
                        for w in range(NW):
                            nc.gpsimd.indirect_dma_start(
                                bd_raw[:, w, :], None, b_dn,
                                bass.IndirectOffsetOnAxis(lora_now[:, t.par, w:w + 1], 0)).then_inc(in_bd, 16)
                    if step == "gate" and j == 7 and t.next().exists():
                        set_lora_rows(t.next())
                    if step == "gate" and j == 7 and t.next().next().exists():
                        pool.wait_ge(lo["mix"], t.count(BLK, BLK))
                        gather_mix(t.next().next())
                    if step == "up" and t.has_chunk(j + 3):
                        pool.wait_ge(lo["bg"], t.count(FC, j + 2))
                        pool.wait_ge(lo["bu"], t.count(FC, j + 2))
                        gather_b(t, j + 3)

            t0 = Tile(0, 0)
            nc.gpsimd.iota(part[:], [[0, 1]], base=0, channel_multiplier=1).then_inc(pool_const, 1)
            nc.gpsimd.memset(map_i[:], -1).then_inc(pool_zero, 1)
            nc.gpsimd.memset(rbias[:], -1e30).then_inc(pool_zero, 1)
            nc.gpsimd.iota(e_index[:], [[1, E], [0, R0]], base=0, channel_multiplier=0,
                           allow_small_or_imprecise_dtypes=True).then_inc(pool_const, 1)
            nc.gpsimd.memset(mix_mask[:], 1.0).then_inc(pool_zero, 1)
            nc.gpsimd.memset(rank_mask[:], SCALE).then_inc(pool_zero, 1)
            nc.gpsimd.memset(ident[:], 0.0).then_inc(pool_zero, 1)
            pool.wait_ge(pool_zero, 5)
            nc.gpsimd.affine_select(mix_mask[:], mix_mask[:], [[-SEQ, SPB], [0, SEQ]], ALU.is_ge, 0.0,
                                    base=0, channel_multiplier=1).then_inc(pool_const, 1)
            nc.gpsimd.affine_select(rank_mask[:], rank_mask[:], [[-RANK, SPW], [0, SEQ]], ALU.is_ge, 0.0,
                                    base=0, channel_multiplier=1).then_inc(pool_const, 1)
            nc.gpsimd.affine_select(ident[:], ident[:], [[-1, P]], ALU.not_equal, 1.0,
                                    base=0, channel_multiplier=1).then_inc(pool_const, 1)
            pool.wait_ge(pool_const, 5)
            nc.gpsimd.affine_select(mix_mask[:], mix_mask[:], [[SEQ, SPB], [0, SEQ]], ALU.is_ge, 0.0,
                                    base=SEQ - 1, channel_multiplier=-1).then_inc(pool_const, 1)
            nc.gpsimd.affine_select(rank_mask[:], rank_mask[:], [[RANK, SPW], [0, SEQ]], ALU.is_ge, 0.0,
                                    base=RANK - 1, channel_multiplier=-1).then_inc(pool_const, 1)
            pool.wait_ge(index_made, 2)
            gather_mix(t0)
            set_lora_rows(t0)
            for c in range(2):
                gather_b(t0, c)
            gather_mix(t0.next())
            pool.wait_ge(lo["bg"], 1)
            pool.wait_ge(lo["bu"], 1)
            gather_b(t0, 2)
            serve(seam_steps(None, t0))
            with pool.Fori(0, TILES // 2 - 1) as i:
                for k in range(2):
                    serve(body_steps(Tile(i, k), Tile(i, k + 1)))
            serve(body_steps(Tile(0, TILES - 2), Tile(0, TILES - 1)))
            serve(body_steps(Tile(0, TILES - 1), None))

        @block.scalar
        def _(act):
            def copy(out, in_):
                return nc.scalar.activation(out, in_, ACT.Copy)

            def round_w(t, c, q):
                name = ("wg", "wu", "wd")[q]
                a, fill = t.chunk(c)
                act.wait_ge(in_w[a][q], 16 * fill)
                copy(w_hi[q][:], w_raw[:, a, q, :]).then_inc(hi[name], 1)
                if q == DOWN:
                    rows = t if c < FC else t.next()
                    act.wait_ge(in_ad, 16 * SPT * rows.count(1, 1))
                    copy(ad_hi[:], ad_raw[:, :, c % FC, :]).then_inc(hi["ad"], 1)
                else:
                    act.wait_ge(in_b[a], 16 * NW * fill)
                    copy(b_hi[q][:], b_raw[:, a, :, q * P:(q + 1) * P]).then_inc(hi[("bg", "bu")[q]], 1)

            def serve(steps):
                for step, j, t in steps:
                    if step == "prep_x":
                        act.wait_ge(in_x[j % 2], 16 * t.count(2, j // 2 + 1))
                        wait(act, pe["cond"], t.count(BLK, j))
                        wait(act, pe["gate"], t.count(FC, 3 - FC))
                        copy(x_hi[:], x_raw[:, j % 2, :]).then_inc(hi["x"], 1)
                        act.wait_ge(mix_made, t.count(BLK, j + 1))
                        copy(mix_hi[:], mix[:].rearrange("p s c -> p (s c)")).then_inc(hi["mix"], 1)
                    elif step == "prep_a":
                        act.wait_ge(in_ag, 16 * SPT * t.count(1, 1))
                        act.wait_ge(pe["cond"], t.count(BLK, BLK))
                        for w in range(NW):
                            last = copy(by_window(da_hi)[:, w], ag_by_window[:, w])
                        last.then_inc(hi["ag"], 1)
                    elif step == "prep_b":
                        act.wait_ge(in_bd, 16 * NW * t.count(1, 1))
                        act.wait_ge(pe["gate"], t.count(FC, 3))
                        copy(bd_hi[:], bd_raw).then_inc(hi["bd"], 1)
                    elif step == "prep_ffn":
                        act.wait_ge(in_ffn, 16)
                        act.wait_ge(pe["base"], KD * TILES)
                        copy(base_hi[:].rearrange("p k n -> p (k n)"), d_in[0]).then_inc(hi["ffn"], 1)
                    elif step == "cond":
                        act.wait_ge(pe["cond"], t.count(BLK, j + 1))
                        copy(xc_hi[:, :, j * P:(j + 1) * P],
                             spare[:].rearrange("p (k n) -> p k n", k=KD)).then_inc(hi["xc"], 1)
                    elif step == "router":
                        act.wait_ge(exp_ready, t.count(1, 1))
                        nc.scalar.activation(logit[:], logit[:], ACT.Exp).then_inc(exp_done, 1)
                    elif step == "probs":
                        act.wait_ge(pe["probs"], t.count(1, 1))
                        copy(probs_t, spare[0:NR, :]).then_inc(spare_free, 1)
                    elif step == "expand":
                        act.wait_ge(pe["expand"], t.count(1, 1))
                        copy(hw[:], spare[:]).then_inc(spare_free, 1)
                    elif step == "h":
                        act.wait_ge(spare_free, t.count(SPARE, USE[step, j] + 1))
                        copy(hw_hi[:], hw[:]).then_inc(hi["hw"], 1)
                    elif step == "base":
                        act.wait_ge(spare_free, t.count(SPARE, USE[step, j] + 1))
                        copy(x1_hi[t.par][:, j, :], res[:, j % 2, :]).then_inc(hi["x1"], 1)
                    elif step == "lora":
                        act.wait_ge(spare_free, t.count(SPARE, USE[step, j] + 1))
                        wait(act, pe[("gate", "up")[j]], t.count(FC, 0))
                        copy(gu_hi[j][:], ranks[:, j, :]).then_inc(hi["lora"], 1)
                    elif step in ("gate", "up"):
                        act.wait_ge(pe[step], t.count(FC, j + 1))
                        if step == "gate":
                            wait(act, lo["act"], t.count(FC, j - 1))
                            nc.scalar.activation(s[:, t.chunk(j)[0], :], p_gate[:], ACT.Silu).then_inc(silu_done, 1)
                        if t.has_chunk(j + 1):
                            round_w(t, j + 1, GATE if step == "gate" else UP)
                    elif step == "down":
                        if t is None:
                            t, j = Tile(0, -1), FC - 1
                            round_act(Tile(0, 0), 0)
                            round_w(Tile(0, 0), 0, DOWN)
                            continue
                        act.wait_ge(pe["down"], t.count(FC, j + 1))
                        if j == FC - 1:
                            act.wait_ge(rank_made, t.count(1, 1))
                            copy(x_hi[:], ranks[:, 0, :]).then_inc(hi["rank"], 1)
                        if t.has_chunk(j + 1):
                            round_act(t, j + 1)
                            round_w(t, j + 1, DOWN)
                    elif step == "final":
                        act.wait_ge(pe["final"], t.count(1, 1))
                        act.wait_ge(lo["bd"], t.count(1, 1))
                        for m in range(0, KD, 2):
                            last = copy(d_raw[:, m, :], p_d[m][:])
                        last.then_inc(d_act, 1)
                        act.wait_ge(d_dve, t.count(1, 1))
                        act.wait_ge(d_act, t.count(1, 1))
                        copy(da_hi[:], d_raw[:].rearrange("p k n -> p (k n)")).then_inc(hi["d"], 1)
                    elif step == "cluster":
                        act.wait_ge(spare_free, t.next().count(SPARE, 0) + (FRONT + 1 if t.next().exists() else 1))
                        nc.scalar.activation(cl[:], cl[:], ACT.Exp, scale=1.0 / TEMPERATURE).then_inc(cl_exp, 1)

            def round_act(t, c):
                act.wait_ge(prod_done, t.count(FC, c + 1))
                copy(act_hi[:], s[:, t.chunk(c)[0], :]).then_inc(hi["act"], 1)

            t0 = Tile(0, 0)
            act.wait_ge(in_first, 64)
            at = 0
            for part_hi in (rt_hi, a0_hi, b0_hi, ct_hi):
                flat = part_hi[:] if len(part_hi.shape) == 2 else part_hi[:].rearrange("p k n -> p (k n)")
                copy(flat, d_in[0][:, at:at + flat.shape[1]]).then_inc(hi["const"], 1)
                at += flat.shape[1]
            act.wait_ge(out_d, 16)
            copy(base_hi[:].rearrange("p k n -> p (k n)"), d_in[1]).then_inc(hi["d"], 1)
            round_w(t0, 0, GATE)
            round_w(t0, 0, UP)
            serve(front_steps(t0))
            serve(seam_steps(None, t0))
            with act.Fori(0, TILES // 2 - 1) as i:
                for k in range(2):
                    serve(body_steps(Tile(i, k), Tile(i, k + 1)))
            serve(body_steps(Tile(0, TILES - 2), Tile(0, TILES - 1)))
            serve(body_steps(Tile(0, TILES - 1), None))

            with act.Fori(0, TILES // 2) as i:
                for k in range(2):
                    t = Tile(i, k)
                    act.wait_ge(in_d[k], 16 * (i + 1))
                    act.wait_ge(pe["up"], FC * TILES)
                    act.wait_ge(dense_free, t.count(KD, 1))
                    copy(x1_hi[k][:].rearrange("p k n -> p (k n)"), d_in[k]).then_inc(hi["d"], 1)
                    act.wait_ge(pe["hits"], t.count(1, 1))
                    copy(ranks[:, k, :], spare[:]).then_inc(hits_copied, 1)

        @block.vector
        def _(dve):
            def minus(out, a, b):
                return nc.vector.tensor_tensor(out, a, b.bitcast(F32), ALU.subtract)

            def rest_w(t, c, q):
                name = ("wg", "wu", "wd")[q]
                a, _ = t.chunk(c)
                dve.wait_ge(hi[name], t.count(FC, c + 1))
                minus(w_lo[q][:], w_raw[:, a, q, :], w_hi[q][:]).then_inc(lo[name], 1)
                other = ("bg", "bu", "ad")[q]
                dve.wait_ge(hi[other], t.count(FC, c + 1))
                if q == DOWN:
                    minus(ad_lo[:], ad_raw[:, :, c % FC, :], ad_hi[:]).then_inc(lo["ad"], 1)
                else:
                    minus(b_lo[q][:], b_raw[:, a, :, q * P:(q + 1) * P], b_hi[q][:]).then_inc(lo[other], 1)

            def rest_act(t, c):
                dve.wait_ge(hi["act"], t.count(FC, c + 1))
                minus(act_lo[:], s[:, t.chunk(c)[0], :], act_hi[:]).then_inc(lo["act"], 1)

            def masked(out, psum):
                return nc.vector.tensor_tensor(
                    out.rearrange("p (w n) -> p w n", w=NW), psum[:].rearrange("p (w n) -> p w n", w=NW),
                    rank_mask[:].rearrange("p s c -> p (s c)").unsqueeze(1).to_broadcast([P, NW, WIN]), ALU.mult)

            def route(t):
                def link(ins, n, before_max=False):
                    ins.then_inc(route_step, 1)
                    dve.wait_ge(route_step, t.count(6, n))
                    if before_max:
                        passed(dve)

                def wide(x):
                    return x.unsqueeze(2).to_broadcast([P, BLK, NR])

                dve.wait_ge(pe["router"], t.count(1, 1))
                nc.vector.tensor_tensor(logit[:], spare[:, 0:BLK * NR].rearrange("p (b n) -> p b n", b=BLK),
                                        rbias[:].unsqueeze(1).to_broadcast([P, BLK, NR]), ALU.add)\
                    .then_inc(spare_free, 1)
                dve.wait_ge(spare_free, t.count(SPARE, USE["router", 0] + 1))
                link(nc.vector.tensor_reduce(stat[:, 0, :], logit[:], AX.X, ALU.max), 1)
                nc.vector.tensor_tensor(logit[:], logit[:], wide(stat[:, 0, :]), ALU.subtract).then_inc(exp_ready, 1)
                dve.wait_ge(exp_done, t.count(1, 1))
                link(nc.vector.tensor_reduce(stat[:, 1, :], logit[:], AX.X, ALU.add), 2)
                link(nc.vector.reciprocal(stat[:, 2, :], stat[:, 1, :]), 3)
                link(nc.vector.tensor_tensor(logit[:], logit[:], wide(stat[:, 2, :]), ALU.mult), 4, True)
                for b in range(BLK):
                    last = nc.vector.max(top[:, b, :], logit[:, b, :])
                link(last, 5, True)
                for b in range(BLK):
                    last = nc.vector.match_replace(chosen[:, b, :], top[:, b, :], logit[:, b, :], 0.0)
                link(last, 6)
                nc.vector.tensor_tensor(chosen[:], logit[:], chosen[:], ALU.subtract).then_inc(chosen_done, 1)

            def clusters(t):
                def link(ins, n):
                    ins.then_inc(cl_step, 1)
                    dve.wait_ge(cl_step, t.count(6, n))

                def wide(x):
                    return x.unsqueeze(2).to_broadcast([P, BLK, CL])

                logits = spare[:, 0:BLK * CL].rearrange("p (b n) -> p b n", b=BLK)
                dve.wait_ge(pe["cluster"], t.count(1, 1))
                link(nc.vector.tensor_reduce(cl_stat[:, 0, :], logits, AX.X, ALU.max), 1)
                nc.vector.tensor_tensor(cl[:], logits, wide(cl_stat[:, 0, :]), ALU.subtract).then_inc(spare_free, 1)
                dve.wait_ge(cl_exp, t.count(1, 1))
                link(nc.vector.tensor_reduce(cl_stat[:, 1, :], cl[:], AX.X, ALU.add), 2)
                link(nc.vector.reciprocal(cl_stat[:, 2, :], cl_stat[:, 1, :]), 3)
                link(nc.vector.tensor_tensor(cl[:], cl[:], wide(cl_stat[:, 2, :]), ALU.mult), 4)
                link(nc.vector.tensor_reduce(cl_stat[:, 0, :], cl[:], AX.X, ALU.max), 5)
                nc.vector.tensor_tensor(cl_best[:], cl_best[:], cl[:], ALU.max)
                link(nc.vector.tensor_scalar(hit[:, bass.ds(t.count(BLK, 0), BLK)], cl_stat[:, 0, :], THRESHOLD, None,
                                             ALU.is_gt), 6)

            def serve(steps):
                for step, j, t in steps:
                    if step == "prep_x":
                        dve.wait_ge(in_mix[t.par], 16 * BLK * (t.i + t.k // 2 + 1))
                        nc.vector.tensor_tensor(mix[:], mixw[:, t.par, j:j + 1, :].to_broadcast([P, SPB, SEQ]),
                                                mix_mask[:], ALU.mult).then_inc(mix_made, 1)
                        dve.wait_ge(hi["x"], t.count(BLK, j + 1))
                        minus(x_lo[:], x_raw[:, j % 2, :], x_hi[:]).then_inc(lo["x"], 1)
                        dve.wait_ge(hi["mix"], t.count(BLK, j + 1))
                        minus(mix_lo[:], mix[:].rearrange("p s c -> p (s c)"), mix_hi[:]).then_inc(lo["mix"], 1)
                    elif step == "prep_a":
                        dve.wait_ge(hi["ag"], t.count(1, 1))
                        for w in range(NW):
                            last = minus(by_window(da_lo)[:, w], ag_by_window[:, w], by_window(da_hi)[:, w])
                        last.then_inc(lo["ag"], 1)
                    elif step == "prep_b":
                        dve.wait_ge(hi["bd"], t.count(1, 1))
                        minus(bd_lo[:], bd_raw, bd_hi[:]).then_inc(lo["bd"], 1)
                    elif step == "prep_ffn":
                        dve.wait_ge(hi["ffn"], 1)
                        minus(base_lo[:].rearrange("p k n -> p (k n)"), d_in[0],
                              base_hi[:].rearrange("p k n -> p (k n)")).then_inc(lo["ffn"], 1)
                    elif step == "cond":
                        dve.wait_ge(hi["xc"], t.count(BLK, j + 1))
                        cols = slice(j * P, (j + 1) * P)
                        minus(xc_lo[:, :, cols], spare[:].rearrange("p (k n) -> p k n", k=KD), xc_hi[:, :, cols])\
                            .then_inc(spare_free, 1)
                    elif step == "router":
                        route(t)
                    elif step == "h":
                        dve.wait_ge(pe["h"], t.count(1, 1))
                        nc.vector.tensor_tensor(hw[:], spare[:], hw[:], ALU.mult).then_inc(spare_free, 1)
                        dve.wait_ge(hi["hw"], t.count(1, 1))
                        minus(hw_lo[:], hw[:], hw_hi[:]).then_inc(lo["hw"], 1)
                    elif step == "base":
                        dve.wait_ge(pe["base"], t.count(KD, j + 1))
                        dve.wait_ge(in_res[j % 2], 16 * t.count(2, j // 2 + 1))
                        r = res[:, j % 2, :]
                        nc.vector.scalar_tensor_tensor(r, spare[:], bias0[:, j:j + 1], r, ALU.add, ALU.add)\
                            .then_inc(spare_free, 1)
                        dve.wait_ge(hi["x1"], t.count(KD, j + 1))
                        minus(x1_lo[t.par][:, j, :], r, x1_hi[t.par][:, j, :]).then_inc(lo["x1"], 1)
                    elif step == "lora":
                        dve.wait_ge(pe["lora"], t.count(2, j + 1))
                        masked(ranks[:, j, :], spare)\
                            .then_inc(spare_free, 2 if t.fixed and t.k == 0 and j == 1 else 1)
                        dve.wait_ge(hi["lora"], t.count(2, j + 1))
                        minus(gu_lo[j][:], ranks[:, j, :], gu_hi[j][:]).then_inc(lo["lora"], 1)
                    elif step == "gate":
                        if t.has_chunk(j + 1):
                            rest_w(t, j + 1, GATE)
                    elif step == "up":
                        dve.wait_ge(pe["up"], t.count(FC, j + 1))
                        dve.wait_ge(silu_done, t.count(FC, j + 1))
                        chunk = s[:, t.chunk(j)[0], :]
                        nc.vector.tensor_tensor(chunk, chunk, p_up[:], ALU.mult).then_inc(prod_done, 1)
                        if t.has_chunk(j + 1):
                            rest_w(t, j + 1, UP)
                    elif step == "down":
                        if t is None:
                            rest_act(Tile(0, 0), 0)
                            rest_w(Tile(0, 0), 0, DOWN)
                            continue
                        if j == FC - 1:
                            dve.wait_ge(pe["down"], t.count(FC, FC))
                            masked(ranks[:, 0, :], p_rank).then_inc(rank_made, 1)
                            dve.wait_ge(hi["rank"], t.count(1, 1))
                            minus(x_lo[:], ranks[:, 0, :], x_hi[:]).then_inc(lo["rank"], 1)
                        if t.has_chunk(j + 1):
                            rest_act(t, j + 1)
                            rest_w(t, j + 1, DOWN)
                    elif step == "final":
                        dve.wait_ge(pe["final"], t.count(1, 1))
                        for m in range(1, KD, 2):
                            last = nc.vector.tensor_copy(d_raw[:, m, :], p_d[m][:])
                        last.then_inc(d_dve, 1)
                        dve.wait_ge(hi["d"], t.count(1, 2))
                        minus(da_lo[:], d_raw[:].rearrange("p k n -> p (k n)"), da_hi[:]).then_inc(lo["d"], 1)
                    elif step == "cluster":
                        clusters(t)

            t0 = Tile(0, 0)

            def start(ins, n):
                ins.then_inc(start_step, 1)
                dve.wait_ge(start_step, n)

            dve.wait_ge(pool_const, 1)
            nc.vector.tensor_scalar(low5[:], part[:], SEQ - 1, None, ALU.bitwise_and)
            start(nc.vector.tensor_scalar(low4[:], part[:], RANK - 1, None, ALU.bitwise_and), 1)
            nc.vector.tensor_copy(low5f[:], low5[:])
            nc.vector.tensor_copy(part_f[:], part[:])
            start(nc.vector.tensor_copy(low4f[:], low4[:]), 2)
            dve.wait_ge(in_index, 48)
            nc.vector.tensor_scalar(subj_row[:], subj_i[:], float(SEQ), low5f[:], ALU.mult, ALU.add)\
                .then_inc(index_made, 1)
            nc.vector.tensor_scalar(lora_row[:], lora_i[:], float(RANK), low4f[:], ALU.mult, ALU.add)\
                .then_inc(index_made, 1)
            nc.vector.memset(cl_best[:], 0.0)
            dve.wait_ge(in_small, 64)
            start(nc.vector.tensor_copy(map_f[:], map_i[:]), 3)
            dve.wait_ge(pool_const, 2)
            nc.vector.tensor_scalar(spread[:], e_index[:], map_f[:], SCALING, ALU.is_equal, ALU.mult)\
                .then_inc(spread_made, 1)
            at = 0
            for n, (part_hi, part_lo) in enumerate(((rt_hi, rt_lo), (a0_hi, a0_lo), (b0_hi, b0_lo), (ct_hi, ct_lo))):
                flat_hi, flat_lo = (x[:] if len(x.shape) == 2 else x[:].rearrange("p k n -> p (k n)")
                                    for x in (part_hi, part_lo))
                dve.wait_ge(hi["const"], n + 1)
                minus(flat_lo, d_in[0][:, at:at + flat_hi.shape[1]], flat_hi).then_inc(lo["const"], 1)
                at += flat_hi.shape[1]
            dve.wait_ge(hi["d"], 1)
            minus(base_lo[:].rearrange("p k n -> p (k n)"), d_in[1],
                  base_hi[:].rearrange("p k n -> p (k n)")).then_inc(lo["d"], 1)
            rest_w(t0, 0, GATE)
            rest_w(t0, 0, UP)
            dve.wait_ge(pool_const, 7)
            serve(front_steps(t0))
            serve(seam_steps(None, t0))
            with dve.Fori(0, TILES // 2 - 1) as i:
                for k in range(2):
                    serve(body_steps(Tile(i, k), Tile(i, k + 1)))
            serve(body_steps(Tile(0, TILES - 2), Tile(0, TILES - 1)))
            serve(body_steps(Tile(0, TILES - 1), None))

            dve.wait_ge(cl_step, 6 * TILES)
            nc.vector.tensor_reduce(best_1, cl_best[:].rearrange("p b c -> p c b"), AX.X, ALU.max).then_inc(sel_step, 1)
            nc.vector.tensor_copy(ident_r, ident[:]).then_inc(identr_made, 1)
            dve.wait_ge(in_assign, 16)
            nc.vector.tensor_copy(assign_f, assign_i).then_inc(sel_step, 1)
            dve.wait_ge(sel_step, 2)
            nc.vector.tensor_scalar(onehot, assign_f, part_f[0:CL], None, ALU.is_equal).then_inc(sel_step, 1)
            dve.wait_ge(pe["best"], 1)
            nc.vector.tensor_reduce(best_2, spare[0:CL, 0:P], AX.X, ALU.max).then_inc(sel_step, 1)
            dve.wait_ge(sel_step, 4)
            nc.vector.tensor_scalar(sel, best_2, THRESHOLD, None, ALU.is_gt).then_inc(sel_step, 1)
            dve.wait_ge(pe["rows"], 1)
            nc.vector.tensor_copy(row_sel, spare[:, 0:KD]).then_inc(rows_ready, 1)
            dve.wait_ge(rows_ready, 1)
            dve.wait_ge(d_act, TILES)
            dve.wait_ge(d_dve, TILES)
            nc.vector.memset(stat[:], 0.0).then_inc(dense_free, KD)
            with dve.Fori(0, TILES // 2) as i:
                for k in range(2):
                    t = Tile(i, k)
                    nc.vector.tensor_copy(
                        hit_spread, hit[:, bass.ds(t.count(BLK, 0), BLK)].unsqueeze(2).to_broadcast([P, BLK, P]))\
                        .then_inc(hits_spread, 1)
                    dve.wait_ge(hi["d"], TILES + t.count(1, 2))
                    minus(x1_lo[k][:].rearrange("p k n -> p (k n)"), d_in[k],
                          x1_hi[k][:].rearrange("p k n -> p (k n)")).then_inc(lo["d"], 1)
                    dve.wait_ge(hits_copied, t.count(1, 1))
                    for m in range(KD):
                        b = KD * k + m
                        dve.wait_ge(pe["dense"], t.count(KD, m + 1))
                        nc.vector.scalar_tensor_tensor(s[:, m % 2, :], dense_bank[m][:], bias1[:, m:m + 1],
                                                       ranks[:, k, :], ALU.add, ALU.mult).then_inc(dense_free, 1)
                        dve.wait_ge(dense_free, KD + t.count(KD, m + 1))
                        dve.wait_ge(in_x1[b], 16 * (i + 1))
                        nc.vector.scalar_tensor_tensor(y_buf[b], s[:, m % 2, :], row_sel[:, m:m + 1], y_buf[b],
                                                       ALU.mult, ALU.add).then_inc(y_made, 1)

        @block.tensor
        def _(ten):
            def product(out, w, x, first=True, last=True):
                nc.tensor.matmul(out, w[0], x[0], start=first, stop=False, skip_group_check=True)
                nc.tensor.matmul(out, w[0], x[1], start=False, stop=False, skip_group_check=True)
                return nc.tensor.matmul(out, w[1], x[0], start=False, stop=last, skip_group_check=True)

            def cols(pr, a, b):
                return pr[0][:, a:b], pr[1][:, a:b]

            def chunk3(pr, k, a, b):
                return pr[0][:, k, a:b], pr[1][:, k, a:b]

            da, bd, act_p, x_p, mix_p = (da_hi, da_lo), (bd_hi, bd_lo), (act_hi, act_lo), (x_hi, x_lo), (mix_hi, mix_lo)
            xc, hw_p, base_p, a0_p, b0_p = (xc_hi, xc_lo), (hw_hi, hw_lo), (base_hi, base_lo), (a0_hi, a0_lo), (b0_hi, b0_lo)
            rt, ct, ad = (rt_hi, rt_lo), (ct_hi, ct_lo), (ad_hi, ad_lo)

            def gate_up(t, c, q):
                ten.wait_ge(lo[("wg", "wu")[q]], t.count(FC, c + 1))
                wait(ten, (silu_done, prod_done)[q], t.count(FC, c))
                if c == 0 and q == 0:
                    ten.wait_ge(lo["x1"], t.count(KD, KD))
                bank_ = (p_gate, p_up)[q]
                w, x1 = (w_hi[q], w_lo[q]), (x1_hi[t.par], x1_lo[t.par])
                for k in range(KD):
                    product(bank_[:], cols(w, k * P, (k + 1) * P), chunk3(x1, k, 0, N), first=k == 0, last=False)
                ten.wait_ge(lo[("bg", "bu")[q]], t.count(FC, c + 1))
                if c == 0:
                    ten.wait_ge(lo["lora"], t.count(2, q + 1))
                for v in range(NW):
                    at = slice(v * WIN, (v + 1) * WIN)
                    mm = product(bank_[:, at], (b_hi[q][:, v, :], b_lo[q][:, v, :]),
                                 cols((gu_hi[q], gu_lo[q]), v * WIN, (v + 1) * WIN), first=False)
                mm.then_inc(pe[("gate", "up")[q]], 1)

            def down(t, c):
                ten.wait_ge(lo["act"], t.count(FC, c + 1))
                ten.wait_ge(lo["wd"], t.count(FC, c + 1))
                if c == 0:
                    wait(ten, d_act, t.count(1, 0))
                    wait(ten, d_dve, t.count(1, 0))
                    wait(ten, rank_made, t.count(1, 0))
                for m in range(KD):
                    product(p_d[m][:], cols((w_hi[DOWN], w_lo[DOWN]), m * P, (m + 1) * P), cols(act_p, 0, N),
                            first=c == 0, last=False)
                ten.wait_ge(lo["ad"], t.count(FC, c + 1))
                for v in range(NW):
                    w = [x[:, v * SPW:(v + 1) * SPW, :].rearrange("p s r -> p (s r)") for x in ad]
                    mm = product(p_rank[:, v * WIN:(v + 1) * WIN], w, cols(act_p, v * WIN, (v + 1) * WIN),
                                 first=c == 0 and v == 0, last=c == FC - 1)
                mm.then_inc(pe["down"], 1)

            def front(step, j, t):
                wait(ten, spare_free, t.count(SPARE, USE[step, j]))
                if step == "cond":
                    ten.wait_ge(lo["x"], t.count(BLK, j + 1))
                    ten.wait_ge(lo["mix"], t.count(BLK, j + 1))
                    for k in range(KD):
                        mm = product(spare[:, k * P:(k + 1) * P], cols(x_p, k * P, (k + 1) * P), cols(mix_p, 0, P))
                elif step == "router":
                    for b in range(BLK):
                        for k in range(KD):
                            mm = product(spare[:, b * NR:(b + 1) * NR], chunk3(xc, k, b * P, (b + 1) * P),
                                         chunk3(rt, k, 0, NR), k == 0, k == KD - 1)
                elif step == "probs":
                    ten.wait_ge(chosen_done, t.count(1, 1))
                    for b in range(BLK):
                        mm = nc.tensor.transpose(spare[0:NR, b * P:(b + 1) * P], chosen[:, b, :], ident[:])
                elif step == "expand":
                    mm = nc.tensor.matmul(spare[:], spread[:].rearrange("n e r -> n (e r)"), probs_t,
                                          start=True, stop=True)
                elif step == "h":
                    for k in range(KD):
                        mm = product(spare[:], chunk3(a0_p, k, 0, P), chunk3(xc, k, 0, N), k == 0, k == KD - 1)
                elif step == "base":
                    for k in range(KD):
                        product(spare[:], chunk3(base_p, k, j * P, (j + 1) * P), chunk3(xc, k, 0, N), k == 0, False)
                    ten.wait_ge(lo["hw"], t.count(1, 1))
                    mm = product(spare[:], cols(b0_p, j * P, (j + 1) * P), cols(hw_p, 0, N), False, True)
                elif step == "lora":
                    ten.wait_ge(lo["ag"], t.count(1, 1))
                    ten.wait_ge(lo["x1"], t.count(KD, KD))
                    for v in range(NW):
                        for k in range(KD):
                            at = (v * 2 * KD + 2 * k + j) * P
                            mm = product(spare[:, v * WIN:(v + 1) * WIN], cols(da, at, at + P),
                                         chunk3((x1_hi[t.par], x1_lo[t.par]), k, v * WIN, (v + 1) * WIN),
                                         k == 0, k == KD - 1)
                mm.then_inc(pe[step], 1)

            def serve(steps):
                for step, j, t in steps:
                    if step in ("gate", "up"):
                        gate_up(t, j, GATE if step == "gate" else UP)
                    elif step == "down" and t is not None:
                        down(t, j)
                    elif (step, j) in USE:
                        front(step, j, t)
                    elif step == "final":
                        ten.wait_ge(lo["rank"], t.count(1, 1))
                        ten.wait_ge(lo["bd"], t.count(1, 1))
                        for m in range(KD):
                            for v in range(NW):
                                w = [x[:, v, m * P:(m + 1) * P] for x in bd]
                                mm = product(p_d[m][:, v * WIN:(v + 1) * WIN], w,
                                             cols(x_p, v * WIN, (v + 1) * WIN), False, True)
                        mm.then_inc(pe["final"], 1)
                    elif step == "cluster":
                        ten.wait_ge(lo["d"], t.count(1, 2))
                        ten.wait_ge(spare_free, t.next().count(SPARE, 0) + (FRONT if t.next().exists() else 0))
                        for b in range(BLK):
                            for k in range(KD):
                                at = k * N + b * P
                                mm = product(spare[:, b * CL:(b + 1) * CL], cols(da, at, at + P),
                                             chunk3(ct, k, 0, CL), k == 0, k == KD - 1)
                        mm.then_inc(pe["cluster"], 1)

            t0 = Tile(0, 0)
            ten.wait_ge(lo["const"], 4)
            ten.wait_ge(lo["d"], 1)
            ten.wait_ge(spread_made, 1)
            ten.wait_ge(pool_const, 5)
            serve(front_steps(t0))
            serve(seam_steps(None, t0))
            with ten.Fori(0, TILES // 2 - 1) as i:
                for k in range(2):
                    serve(body_steps(Tile(i, k), Tile(i, k + 1)))
            serve(body_steps(Tile(0, TILES - 2), Tile(0, TILES - 1)))
            serve(body_steps(Tile(0, TILES - 1), None))

            ten.wait_ge(sel_step, 1)
            ten.wait_ge(spare_free, SPARE * TILES + 1)
            nc.tensor.transpose(spare[0:CL, 0:P], best_1, ident[:]).then_inc(pe["best"], 1)
            ten.wait_ge(sel_step, 5)
            for m in range(KD):
                mm = nc.tensor.matmul(spare[:, m:m + 1], onehot[:, m * P:(m + 1) * P], sel, start=True, stop=True)
            mm.then_inc(pe["rows"], 1)
            ten.wait_ge(rows_ready, 1)
            ten.wait_ge(identr_made, 1)
            ten.wait_ge(lo["ffn"], 1)
            ten.wait_ge(silu_done, FC * TILES)
            ten.wait_ge(prod_done, FC * TILES)
            with ten.Fori(0, TILES // 2) as i:
                for k in range(2):
                    t = Tile(i, k)
                    ten.wait_ge(hits_spread, t.count(1, 1))
                    ten.wait_ge(dense_free, t.count(KD, 1))
                    for b in range(BLK):
                        mm = nc.tensor.matmul(spare[:, b * P:(b + 1) * P], hit_spread[:, b, :], ident_r,
                                              start=True, stop=True)
                    mm.then_inc(pe["hits"], 1)
                    ten.wait_ge(lo["d"], TILES + t.count(1, 2))
                    for m in range(KD):
                        ten.wait_ge(dense_free, t.count(KD, m + 1))
                        for kk in range(KD):
                            mm = product(dense_bank[m][:], chunk3(base_p, kk, m * P, (m + 1) * P),
                                         chunk3((x1_hi[k], x1_lo[k]), kk, 0, N), kk == 0, kk == KD - 1)
                        mm.then_inc(pe["dense"], 1)


def kernel(**inputs):
    import concourse.bacc as bacc
    from concourse.bass_utils import run_bass_kernel_spmd as run

    a = {k: np.asarray(v) for k, v in inputs.items()}

    def kmajor(w):
        return w.T.reshape(KD, P, -1).transpose(1, 0, 2).reshape(P, -1)

    def pad_f(w, axis):
        shape = list(w.shape)
        shape[axis] = FC * P
        full = np.zeros(shape, w.dtype)
        full[tuple(slice(0, n) for n in w.shape)] = w
        return full

    x = a["x"].reshape(TOKENS, D)
    router = np.zeros((NR, D), x.dtype)
    router[:NR - 1] = a["L0_ffn_router_W"]
    gate, up = (pad_f(a[n], 0).reshape(FC, P, KD, P).transpose(0, 3, 2, 1).reshape(FC, P, D)
                for n in ("L1_cond_W_gate", "L1_cond_W_up"))
    down = pad_f(a["L1_cond_W_down"], 1).reshape(D, FC, P).transpose(1, 2, 0)
    a_gu = np.stack([a["L1_cond_A_gate"][0], a["L1_cond_A_up"][0]])
    a_gu = a_gu.reshape(2, ADAPTERS, RANK, KD, P).transpose(1, 4, 3, 0, 2).reshape(ADAPTERS, P, -1)
    b_gu = pad_f(np.stack([a["L1_cond_B_gate"][0], a["L1_cond_B_up"][0]]), 2)
    b_gu = b_gu.reshape(2, ADAPTERS, FC, P, RANK).transpose(2, 1, 4, 0, 3).reshape(FC * ADAPTERS * RANK, 2 * P)
    a_dn = pad_f(a["L1_cond_A_down"][0], 2).reshape(ADAPTERS, RANK, FC, P).transpose(0, 3, 2, 1)
    subjects, loras = a["itok_B_0_30"], a["itok_B_2_6"]
    arrays = {
        "x_rows": x, "x_cols": x.T,
        "subj_rows": np.repeat(subjects.reshape(-1, SPB), SEQ, axis=1).T,
        "lora_rows": np.repeat(loras.reshape(-1, SPW), RANK, axis=1).T,
        "lora_index": loras.reshape(1, -1),
        "cond_w": a["L0_cond_weights"].reshape(-1, SEQ),
        "base_w": kmajor(a["L0_ffn_base_W"]), "base_b": a["L0_ffn_base_b"].reshape(KD, P).T,
        "router_w": kmajor(router), "router_b": a["L0_ffn_router_b"].reshape(1, -1),
        "a0": kmajor(a["L0_ffn_A"].reshape(-1, D)), "b0": a["L0_ffn_B"].transpose(0, 2, 1).reshape(-1, D),
        "expert_map": a["L0_ffn_expert_map"].reshape(-1, 1),
        "w1": np.stack([gate, up, down], axis=1),
        "a_gu": a_gu, "b_gu": b_gu, "a_dn": a_dn.reshape(ADAPTERS, P, -1),
        "b_dn": a["L1_cond_B_down"][0].transpose(0, 2, 1).reshape(-1, D),
        "ffn_w": kmajor(a["L1_ffn_weight"]), "ffn_b": a["L1_ffn_bias"].reshape(KD, P).T,
        "centroids": kmajor(a["L1_ffn_centroids"]), "assignments": a["L1_ffn_assignments"].reshape(1, -1),
    }
    arrays = {n: np.ascontiguousarray(v) for n, v in arrays.items()}
    nc = bacc.Bacc("TRN2", target_bir_lowering=False, num_devices=1)
    args = [nc.dram_tensor(n, v.shape, mybir.dt.from_np(v.dtype), kind="ExternalInput").ap() for n, v in arrays.items()]
    out = nc.dram_tensor("out_cols", (D, TOKENS), F32, kind="ExternalOutput").ap()
    adaln_ffn_kernel(nc, *args, out)
    got = run(nc, [arrays], core_ids=[0]).results[0]["out_cols"]
    return np.ascontiguousarray(got.T).reshape(BATCH, SEQ, D)
```

```python
from contextlib import ExitStack

import numpy as np

import concourse.bass as bass
from concourse import mybir
from concourse.alu_op_type import AluOpType as ALU

F32 = mybir.dt.float32
F32R = mybir.dt.float32r
I32 = mybir.dt.int32
U32 = mybir.dt.uint32
ACT = mybir.ActivationFunctionType
AX = mybir.AxisListType

P = 128
BATCH, SEQ, D = 128, 32, 512
TOKENS = BATCH * SEQ
N = 512
TILES = TOKENS // N
KD = D // P
BLK = N // P
SPB = P // SEQ
E, R0 = 8, 16
NR = 2 * E
F = 1376
FC = -(-F // P)
RANK = 16
ADAPTERS = 16
WIN = P // RANK * SEQ
NW = N // WIN
SPW = P // RANK
SPT = N // SEQ
CL = 64
THRESHOLD = 0.01
TEMPERATURE = 0.1
SCALING = 32.0 / 16.0
SCALE = 0.5

GATE, UP, DOWN = range(3)
FRONT_STEPS = [("cond", j) for j in range(BLK)] + [("router", 0), ("turn", 0), ("probs", 0), ("expand", 0), ("h", 0)] \
    + [("base", m) for m in range(KD)] + [("lora", u) for u in range(2)]
USE = {step: n for n, step in enumerate(FRONT_STEPS)}
FRONT = len(FRONT_STEPS)
SPARE = FRONT + 2
HALF = 6
PART = 4


class Tile:

    def __init__(self, i, k):
        self.i, self.k, self.par = i, k, k % 2
        self.fixed = isinstance(i, int)

    def next(self):
        return Tile(self.i, self.k + 1)

    def count(self, per_tile, n):
        if self.fixed:
            return per_tile * (2 * self.i + self.k) + n
        return 2 * per_tile * self.i + (per_tile * self.k + n)

    def index(self):
        return self.count(1, 0)

    def chunk(self, c):
        g = FC * self.k + c
        half = g // 2 + 1
        if self.fixed:
            return g % 2, FC * self.i + half
        return g % 2, FC * self.i + half

    def has_chunk(self, c):
        return not self.fixed or FC * (2 * self.i + self.k) + c < FC * TILES

    def first(self):
        return self.fixed and 2 * self.i + self.k == 0

    def exists(self):
        return not self.fixed or 2 * self.i + self.k < TILES


def wait(engine, semaphore, value):
    if not isinstance(value, int) or value > 0:
        engine.wait_ge(semaphore, value)


def after_front(t):
    return t.next().count(SPARE, FRONT if t.next().exists() else 0)


def body_steps(t, n):
    front = {
        3: ([("prep_x", 0)], [], [("cond", 0), ("prep_x", 1)]),
        4: ([], [("cond", 1), ("prep_x", 2)], [("cond", 2), ("prep_x", 3)]),
        5: ([], [("cond", 3)], [("router", 0)]),
        6: ([("turn", 0)], [("prep_a", 0)], [("probs", 0)]),
        7: ([], [("expand", 0)], [("h", 0)]),
        8: ([], [("base", 0)], [("base", 1)]),
        9: ([], [("base", 2)], [("base", 3)]),
        10: ([], [], [("lora", 0)]),
    }
    for c in range(3, FC):
        before, mid, late = front[c] if n else ([], [], [])
        if c == 5 and not n:
            yield "prep_ffn", 0, t
        if c == 8 and not n:
            yield "prep_dense", 0, t
        yield from ((s, j, n) for s, j in before)
        yield "gate", c, t
        if c == 6:
            yield "prep_b", 0, t
        yield from ((s, j, n) for s, j in mid)
        yield "up", c, t
        yield from ((s, j, n) for s, j in late)
        yield "down", c - 1, t
        if c == FC - 1 and n:
            yield "lora", 1, n
    yield from seam_steps(t, n)


def seam_steps(t, n):
    if n:
        yield "gate", 0, n
        yield "up", 0, n
    else:
        yield "dense", 0, t
    yield "down", FC - 1, t
    if n:
        yield "gate", 1, n
        yield "up", 1, n
    else:
        yield "dense", 1, t
    if t:
        yield "final", 0, t
    if n:
        yield "gate", 2, n
        yield "down", 0, n
    else:
        yield "dense", 2, t
        yield "dense", 3, t
    if t:
        yield "cluster", 0, t
    if n:
        yield "up", 2, n
    if t:
        yield "cl_turn", 0, t
    if n:
        yield "down", 1, n


def front_steps(n):
    yield from ((s, j, n) for s, j in (
        ("prep_x", 0), ("prep_x", 1), ("cond", 0), ("prep_x", 2), ("small", 0), ("cond", 1), ("prep_x", 3),
        ("cond", 2), ("cond", 3), ("first_base", 0), ("router", 0), ("early_h", 0), ("turn", 0), ("early_base", 0),
        ("early_base", 1), ("prep_a", 0), ("probs", 0), ("early_base", 2), ("expand", 0), ("early_base", 3), ("h", 0),
        ("base", 0), ("base", 1), ("base", 2), ("base", 3), ("first_w", GATE), ("lora", 0), ("first_w", UP),
        ("lora", 1)))


def adaln_ffn_kernel(nc, x_rows, x_cols, subj_rows, lora_rows, lora_index, cond_w, base_w, base_b, router_w,
                     router_b, a0, b0, expert_map, w1, a_gu, b_gu, a_dn, b_dn, ffn_w, ffn_b, centroids,
                     assignments, out):
    ctx = ExitStack()
    with ctx:
        def sb(name, shape, dt=F32):
            return ctx.enter_context(nc.sbuf_tensor(name, shape, dt))

        def pair(name, shape):
            return sb(name + "_hi", shape, F32R), sb(name + "_lo", shape, F32R)

        def sem(name):
            return ctx.enter_context(nc.semaphore(name))

        x1_dram = nc.dram_tensor("x1_scratch", [TILES, KD, P, N], F32, kind="Internal").ap()
        d_dram = nc.dram_tensor("d_scratch", [TILES, P, KD * N], F32, kind="Internal").ap()

        w_raw = sb("w_raw", [P, 2, 3, N])
        w_hi, w_lo = zip(*[pair(f"w{q}", [P, N]) for q in ("gate", "up", "down")])
        b_raw = sb("b_raw", [P, 2, NW, 2 * P])
        b_hi, b_lo = zip(*[pair(f"b{q}", [P, NW, P]) for q in ("gate", "up")])
        ad_raw = sb("ad_raw", [P, SPT, FC, RANK])
        ad_hi, ad_lo = pair("ad", [P, SPT, RANK])
        ag_raw = sb("ag_raw", [P, SPT, KD * 2, RANK])
        da_hi, da_lo = pair("da", [P, KD * N])
        bd_hi, bd_lo = pair("bd", [P, NW, D])
        x_raw = sb("x_raw", [P, 2, D])
        x_hi, x_lo = pair("x", [P, D])
        mixw = sb("mixw", [P, 2, SPB, SEQ])
        mix = sb("mix", [P, SPB, SEQ])
        mix_hi, mix_lo = pair("mix", [P, P])
        xc_hi, xc_lo = pair("xc", [P, KD, N])
        res = sb("res", [P, 2, N])
        x1_hi, x1_lo = zip(*[pair(f"x1_{q}", [P, KD, N]) for q in range(2)])
        s = sb("s", [P, 2, N])
        act_hi, act_lo = pair("act", [P, N])
        hw = sb("hw", [P, N])
        hw_hi, hw_lo = pair("hw", [P, N])
        ranks = sb("ranks", [P, 2, N])
        logit_t, probs_t = ranks[0:2 * NR, 1, :], ranks[0:NR, 1, :]
        cl_t = ranks[:, 0, :]
        gu_hi, gu_lo = zip(*[pair(f"rank{q}", [P, N]) for q in ("gate", "up")])
        d_raw = sb("d_raw", [P, KD, N])
        bd_raw = d_raw[:, 0:NW, :]

        base_hi, base_lo = pair("base", [P, KD, D])
        a0_hi, a0_lo = pair("a0", [P, KD, P])
        b0_hi, b0_lo = pair("b0", [P, D])
        rt = sb("rt", [P, KD, 2 * NR], F32R)
        ct = sb("ct", [P, KD, 2 * CL], F32R)
        rt_hi, rt_lo, ct_hi, ct_lo = rt[:, :, 0:NR], rt[:, :, NR:], ct[:, :, 0:CL], ct[:, :, CL:]
        bias0 = sb("bias0", [P, KD])
        bias1 = sb("bias1", [P, KD])
        rbias = sb("rbias", [P, NR])
        rank_mask = sb("rank_mask", [P, SPW, SEQ])
        mix_mask = sb("mix_mask", [P, SPB, SEQ])
        ident = sb("ident", [P, P])
        fold_rt = sb("fold_rt", [2 * NR, NR])
        fold_ct = sb("fold_ct", [2 * CL, CL])
        e_index = sb("e_index", [NR, E, R0])
        map_i = sb("map_i", [NR, 1], I32)
        map_f = sb("map_f", [NR, 1])
        spread = sb("spread", [NR, E, R0])
        part = sb("part", [P, 1], I32)
        low5 = sb("low5", [P, 1], I32)
        low4 = sb("low4", [P, 1], I32)
        low5f = sb("low5f", [P, 1])
        low4f = sb("low4f", [P, 1])
        part_f = sb("part_f", [P, 1])
        subj_i = sb("subj_i", [P, TILES * BLK], I32)
        subj_row = sb("subj_row", [P, TILES * BLK], U32)
        lora_i = sb("lora_i", [P, TILES * NW], I32)
        lora_row = sb("lora_row", [P, TILES * NW], U32)
        subj_now = sb("subj_now", [P, 2, BLK], U32)
        lora_now = sb("lora_now", [P, 2, NW], U32)
        index_i = sb("index_i", [1, BATCH], I32)
        logit = sb("logit", [P, BLK, NR])
        chosen = sb("chosen", [P, BLK, NR])
        top = sb("top", [P, BLK, 8])
        stat = sb("stat", [P, 4, BLK])
        cl = sb("cl", [P, BLK, CL])
        cl_stat = sb("cl_stat", [P, 3, BLK])
        cl_best = sb("cl_best", [P, BLK, CL])
        hit = sb("hit", [P, TILES * BLK])

        bank = [ctx.enter_context(nc.psum_tensor(f"bank{b}", [P, N], F32)) for b in range(8)]
        p_gate, p_up, p_rank, spare = bank[0], bank[1], bank[2], bank[3]
        p_d = bank[4:8]

        in_w = [[sem(f"in_w{a}{q}") for q in range(3)] for a in range(2)]
        in_b = [sem(f"in_b{a}") for a in range(2)]
        in_ad = [sem(f"in_ad{a}") for a in range(2)]
        in_ag, in_bd = sem("in_ag"), sem("in_bd")
        in_x = [sem(f"in_x{a}") for a in range(2)]
        in_mix = [sem(f"in_mix{a}") for a in range(2)]
        in_res = [sem(f"in_res{a}") for a in range(2)]
        out_x1 = [sem(f"out_x1{a}") for a in range(2)]
        out_d = sem("out_d")
        in_mix_first = sem("in_mix_first")
        in_index, in_ids, in_small, in_first = sem("in_index"), sem("in_ids"), sem("in_small"), sem("in_first")
        in_ffn, in_assign = sem("in_ffn"), sem("in_assign")
        in_d = [sem(f"in_d{a}") for a in range(2)]
        in_x1 = [sem(f"in_x1{a}") for a in range(2 * KD)]
        out_y = [sem(f"out_y{a}") for a in range(2 * KD)]

        pe = {q: sem("pe_" + q) for q in ("gate", "up", "down", "cond", "router", "turn", "probs", "expand", "h",
                                          "base", "lora", "final", "cluster", "cl_turn", "dense", "hits", "best",
                                          "rows")}
        spare_free = sem("spare_free")
        parts = ("wg", "wu", "wd", "bg", "bu", "ad", "act", "x", "mix", "ag", "bd", "hw", "x1", "lora", "rank", "d",
                 "const", "ffn", "dense")
        hi = {q: sem("hi_" + q) for q in (*parts, "xc")}
        lo = {q: sem("lo_" + q) for q in parts}
        silu_done, prod_done = sem("silu_done"), sem("prod_done")
        mix_made, rank_made = sem("mix_made"), sem("rank_made")
        d_act, d_dve = sem("d_act"), sem("d_dve")
        exp_ready, exp_done, chosen_done = sem("exp_ready"), sem("exp_done"), sem("chosen_done")
        cl_exp = sem("cl_exp")
        route_step, cl_step, start_step = sem("route_step"), sem("cl_step"), sem("start_step")
        pool_zero, pool_const, pool_lora, pool_mix = (
            sem(q) for q in ("pool_zero", "pool_const", "pool_lora", "pool_mix"))
        index_made, spread_made, best_cleared = sem("index_made"), sem("spread_made"), sem("best_cleared")
        waits_passed = sem("waits_passed")
        identr_made, hits_spread, hits_copied, dense_free, y_made, sel_step, rows_ready = (
            sem(q) for q in ("identr_made", "hits_spread", "hits_copied", "dense_free", "y_made", "sel_step",
                             "rows_ready"))

        d_in = [ag_raw[:].rearrange("p s g r -> p (s g r)"), d_raw[:].rearrange("p k n -> p (k n)")]
        ad_flat = ad_raw[:].rearrange("p s c r -> p (s c r)")
        y_buf = [w_raw[:, a, q, :] for a in range(2) for q in range(3)] + [ad_flat[:, 0:N], ad_flat[:, N:2 * N]]
        hit_spread = da_hi[:, 0:BLK * P].rearrange("p (b c) -> p b c", b=BLK)
        ident_r = da_lo[:, 0:P]
        dense_bank = [(p_gate, p_up, p_rank, p_d[0]), (p_d[1], p_d[2], p_d[3], p_d[0])]
        b_flat = b_raw[0:CL].rearrange("p a w n -> p (a w n)")
        assign_i, onehot = b_flat[:, 0:D].bitcast(I32), b_flat[:, D:2 * D]
        best_1 = ad_flat[:, 2 * N:2 * N + CL]
        best_2 = ad_flat[0:CL, 2 * N + CL:2 * N + CL + 1]
        sel = ad_flat[0:CL, 2 * N + CL + 1:2 * N + CL + 2]
        row_sel = ad_flat[:, 2 * N + CL + 2:2 * N + CL + 2 + KD]
        assign_f = s[0:CL, 0, :]

        def by_window(x):
            return x[:].rearrange("p (w g s r) -> p w g s r", w=NW, g=2 * KD, s=SPW)

        ag_by_window = ag_raw[:].rearrange("p (w s) g r -> p w g s r", w=NW)

        x_blocks = x_rows.rearrange("(b p) d -> b p d", p=P)
        x_cols_t = x_cols.rearrange("(m p) n -> m p n", p=P)

        def tokens(t):
            return bass.ds(N * t.index(), N)

        def passed(engine):
            engine.sem_inc(waits_passed, 1)

        def x_part(t, j):
            return (act_hi, act_lo) if t.first() and j % 2 else (x_hi, x_lo)

        def mix_part(t, j):
            return (hw_hi[:, 0:P], hw_lo[:, 0:P]) if t.first() and j % 2 else (mix_hi[:], mix_lo[:])

        def res_place(t, m):
            return d_raw[:, m, :] if t.first() and m >= 2 else res[:, m % 2, :]

        def res_loads(t, m):
            return 2 if t.first() else t.count(2, m // 2 + 1)

        def front_bank(t, step, j):
            if t.first() and step in ("cond", "base", "lora"):
                return p_d[j]
            return p_gate if t.first() and step == "h" else spare

        block = ctx.enter_context(nc.Block())

        @block.sync
        def _(sp):
            def load_w(t, c, q, after):
                a, n = t.chunk(c)
                if after is not None:
                    sp.wait_ge(lo[("wg", "wu", "wd")[q]], after)
                sp.dma_start(w_raw[:, a, q, :], w1[c % FC, q]).then_inc(in_w[a][q], 16)

            def load_x(t, j):
                sp.dma_start(x_raw[:, j % 2, :],
                             x_blocks[bass.ds(t.count(BLK, j), 1)].rearrange("b p d -> p (b d)")).then_inc(in_x[j % 2], 16)

            def load_res(t, m):
                sp.dma_start(res_place(t, m), x_cols_t[m, :, tokens(t)]).then_inc(in_res[m % 2], 16)

            def load_adapters(t, table, dst, first, last, done, samples=range(SPT)):
                passed(sp)
                for j in samples:
                    which = sp.value_load(index_i[0:1, bass.ds(t.count(SPT, j), 1)], min_val=0, max_val=ADAPTERS - 1)
                    sp.dma_start(dst[:, j, first:last].rearrange("p c r -> p (c r)"),
                                 table[bass.ds(which, 1), :, first * RANK:last * RANK]
                                 .rearrange("o p n -> p (o n)")).then_inc(done, 16)

            def serve(steps):
                for step, j, t in steps:
                    if step in ("gate", "up") and t.has_chunk(j + 3):
                        load_w(t, j + 3, GATE if step == "gate" else UP, t.count(FC, j + 2))
                    if step == "down":
                        if t is None:
                            load_w(Tile(0, 0), 2, DOWN, 1)
                        elif t.has_chunk(j + 3):
                            load_w(t, j + 3, DOWN, t.count(FC, j + 2))
                        if t is not None and j in range(SPT // PART):
                            if j == 0:
                                wait(sp, lo["ad"], t.count(FC, 0))
                            load_adapters(t, a_dn, ad_raw, HALF, FC, in_ad[1], range(PART * j, PART * (j + 1)))
                        if t is not None and j in range(HALF, HALF + SPT // PART) and t.next().exists():
                            if j == HALF:
                                sp.wait_ge(lo["ad"], t.count(FC, HALF))
                            q = j - HALF
                            load_adapters(t.next(), a_dn, ad_raw, 0, HALF, in_ad[0], range(PART * q, PART * (q + 1)))
                    if step == "prep_x" and (j < 2 or t.next().exists()):
                        sp.wait_ge(lo["x"], t.count(BLK, j + 1))
                        if j < 2:
                            load_x(t, j + 2)
                        else:
                            load_x(t.next(), j - 2)
                    if step == "gate" and j in range(SPT // PART) and t.next().exists():
                        if j == 0:
                            sp.wait_ge(lo["ag"], t.count(1, 1))
                        load_adapters(t.next(), a_gu, ag_raw, 0, 2 * KD, in_ag, range(PART * j, PART * (j + 1)))
                    if step == "base":
                        sp.wait_ge(spare_free, t.count(SPARE, USE[step, j] + 1))
                        sp.dma_start(x1_dram[bass.ds(t.index(), 1), j].rearrange("o p n -> p (o n)"),
                                     res_place(t, j)).then_inc(out_x1[j % 2], 16)
                    if step == "base" and j > 0 and not (j < 3 and t.first()) and (j < 3 or t.next().exists()):
                        sp.wait_ge(out_x1[(j - 1) % 2], 16 * t.count(2, (j - 1) // 2 + 1))
                        sp.wait_ge(lo["x1"], t.count(KD, j))
                        if j < 3:
                            load_res(t, j + 1)
                        else:
                            load_res(t.next(), 0)
                    if step == "lora" and j == 0 and t.next().exists():
                        sp.wait_ge(out_x1[1], 16 * t.count(2, 2))
                        sp.wait_ge(lo["x1"], t.count(KD, KD))
                        load_res(t.next(), 1)
                    if step == "prep_ffn":
                        sp.wait_ge(lo["ffn"], 1)
                        sp.dma_start(d_in[0], d_dram[0]).then_inc(in_d[0], 16)
                    if step == "final":
                        sp.wait_ge(d_act, t.count(1, 1))
                        sp.wait_ge(d_dve, t.count(1, 1))
                        sp.dma_start(d_dram[bass.ds(t.index(), 1)].rearrange("o p n -> p (o n)"),
                                     d_raw[:].rearrange("p k n -> p (k n)")).then_inc(out_d, 16)

            t0 = Tile(0, 0)
            sp.dma_start(subj_i[:], subj_rows).then_inc(in_index, 16)
            sp.dma_start(lora_i[:], lora_rows).then_inc(in_index, 16)
            load_x(t0, 0)
            load_x(t0, 1)
            small = d_in[0]
            at = 0
            for w in (router_w, a0, b0, centroids):
                sp.dma_start(small[:, at:at + w.shape[1]], w).then_inc(in_first, 16)
                at += w.shape[1]
            sp.wait_ge(pool_zero, 2)
            sp.dma_start(rbias[:, 0:NR - 1], router_b.to_broadcast([P, NR - 1])).then_inc(in_small, 16)
            sp.dma_start(map_i[0:NR - 1], expert_map).then_inc(in_small, 16)
            sp.dma_start(bias0[:], base_b).then_inc(in_small, 16)
            sp.dma_start(bias1[:], ffn_b).then_inc(in_small, 16)
            sp.dma_start(index_i[:], lora_index).then_inc(in_ids, 16)
            serve([("prep_x", 0, t0)])
            sp.dma_start(d_in[1], base_w).then_inc(out_d, 16)
            serve([("prep_x", 1, t0)])
            sp.wait_ge(in_ids, 16)
            sp.wait_ge(lo["const"], 4)
            load_adapters(t0, a_gu, ag_raw, 0, 2 * KD, in_ag, range(0, SPT // 2))
            serve([("prep_x", 2, t0), ("prep_x", 3, t0)])
            load_adapters(t0, a_gu, ag_raw, 0, 2 * KD, in_ag, range(SPT // 2, SPT))
            load_res(t0, 0)
            load_res(t0, 1)
            sp.wait_ge(lo["d"], 1)
            load_res(t0, 2)
            load_res(t0, 3)
            for c in range(2):
                for q in range(3):
                    load_w(t0, c, q, None)
            load_adapters(t0, a_dn, ad_raw, 0, HALF, in_ad[0])
            serve(s for s in front_steps(t0) if s[0] == "base")
            serve(s for s in front_steps(t0) if s[0] == "lora")
            load_w(t0, 2, GATE, 1)
            load_w(t0, 2, UP, 1)
            serve(seam_steps(None, t0))
            with sp.Fori(0, TILES // 2 - 1) as i:
                for k in range(2):
                    serve(body_steps(Tile(i, k), Tile(i, k + 1)))
            serve(body_steps(Tile(0, TILES - 2), Tile(0, TILES - 1)))

            sp.wait_ge(lo["ag"], TILES)
            sp.dma_start(d_in[0], ffn_w).then_inc(in_ffn, 16)
            serve(body_steps(Tile(0, TILES - 1), None))

            def load_d(t):
                sp.dma_start(d_in[t.par], d_dram[bass.ds(t.index(), 1)].rearrange("o p n -> p (o n)"))\
                    .then_inc(in_d[t.par], 16)

            def load_x1(t, m):
                b = KD * t.par + m
                sp.dma_start(y_buf[b], x1_dram[bass.ds(t.index(), 1), m].rearrange("o p n -> p (o n)"))\
                    .then_inc(in_x1[b], 16)

            def store_y(t, m):
                b = KD * t.par + m
                sp.wait_ge(y_made, t.count(KD, m + 1))
                sp.dma_start(out[m * P:(m + 1) * P, tokens(t)], y_buf[b]).then_inc(out_y[b], 16)

            sp.wait_ge(out_d, 16 * (TILES + 1))
            sp.wait_ge(lo["d"], TILES + 1)
            load_d(Tile(0, 1))
            for q in range(2):
                sp.wait_ge(out_x1[q], 16 * 2 * TILES)
            for q in ("wg", "wu", "wd", "ad", "bg", "bu"):
                sp.wait_ge(lo[q], FC * TILES)
            sp.dma_start(assign_i, assignments.to_broadcast([CL, D])).then_inc(in_assign, 16)
            for k in range(2):
                for m in range(KD):
                    load_x1(Tile(0, k), m)
            with sp.Fori(0, TILES // 2 - 1) as i:
                for k in range(2):
                    t = Tile(i, k)
                    sp.wait_ge(lo["dense"], t.count(1, 1))
                    load_d(Tile(i, k + 2))
                    for m in range(KD):
                        store_y(t, m)
                    for m in range(KD):
                        sp.wait_ge(out_y[KD * k + m], 16 * (i + 1))
                        load_x1(Tile(i, k + 2), m)
            for k in range(TILES - 2, TILES):
                for m in range(KD):
                    store_y(Tile(0, k), m)
            for b in range(8):
                sp.wait_ge(out_y[b], 16 * (TILES // 2))

        @block.gpsimd
        def _(pool):
            def set_lora_rows(t):
                nc.gpsimd.tensor_copy(lora_now[:, t.par, :], lora_row[:, bass.ds(t.count(NW, 0), NW)])\
                    .then_inc(pool_lora, 1)
                pool.wait_ge(pool_lora, t.count(1, 1))

            def gather_mix(t):
                nc.gpsimd.tensor_copy(subj_now[:, t.par, :], subj_row[:, bass.ds(t.count(BLK, 0), BLK)])\
                    .then_inc(pool_mix, 1)
                pool.wait_ge(pool_mix, t.count(1, 1))
                passed(pool)
                for j in range(BLK):
                    nc.gpsimd.indirect_dma_start(
                        mixw[:, t.par, j, :], None, cond_w,
                        bass.IndirectOffsetOnAxis(subj_now[:, t.par, j:j + 1], 0))\
                        .then_inc(in_mix_first if t.first() and j == 0 else in_mix[t.par], 16)

            def gather_b(t, c):
                a, _ = t.chunk(c)
                rows = t if c < FC else t.next()
                passed(pool)
                for w in range(NW):
                    nc.gpsimd.indirect_dma_start(
                        b_raw[:, a, w, :], None, b_gu,
                        bass.IndirectOffsetOnAxis(lora_now[:, rows.par, w:w + 1], 0),
                        element_offset=(c % FC) * ADAPTERS * RANK * 2 * P).then_inc(in_b[a], 16)

            def serve(steps):
                for step, j, t in steps:
                    if step == "gate" and j == 3:
                        pool.wait_ge(out_d, 16 * t.count(1, 1))
                        pool.wait_ge(lo["d"], t.count(1, 1))
                        for q in range(2):
                            pool.wait_ge(out_x1[q], 16 * t.count(2, 2))
                        passed(pool)
                        for w in range(NW):
                            nc.gpsimd.indirect_dma_start(
                                bd_raw[:, w, :], None, b_dn,
                                bass.IndirectOffsetOnAxis(lora_now[:, t.par, w:w + 1], 0)).then_inc(in_bd, 16)
                    if step == "gate" and j == 7 and t.next().exists():
                        set_lora_rows(t.next())
                    if step == "gate" and j == 7 and t.next().next().exists():
                        pool.wait_ge(lo["mix"], t.count(BLK, BLK))
                        gather_mix(t.next().next())
                    if step == "up" and t.has_chunk(j + 3):
                        pool.wait_ge(lo["bg"], t.count(FC, j + 2))
                        pool.wait_ge(lo["bu"], t.count(FC, j + 2))
                        gather_b(t, j + 3)

            t0 = Tile(0, 0)
            nc.gpsimd.iota(part[:], [[0, 1]], base=0, channel_multiplier=1).then_inc(pool_const, 1)
            nc.gpsimd.memset(map_i[:], -1).then_inc(pool_zero, 1)
            nc.gpsimd.memset(rbias[:], -1e30).then_inc(pool_zero, 1)
            nc.gpsimd.iota(e_index[:], [[1, E], [0, R0]], base=0, channel_multiplier=0,
                           allow_small_or_imprecise_dtypes=True).then_inc(pool_const, 1)
            nc.gpsimd.memset(mix_mask[:], 1.0).then_inc(pool_zero, 1)
            nc.gpsimd.memset(rank_mask[:], SCALE).then_inc(pool_zero, 1)
            nc.gpsimd.memset(ident[:], 0.0).then_inc(pool_zero, 1)
            pool.wait_ge(pool_zero, 5)
            nc.gpsimd.affine_select(mix_mask[:], mix_mask[:], [[-SEQ, SPB], [0, SEQ]], ALU.is_ge, 0.0,
                                    base=0, channel_multiplier=1).then_inc(pool_const, 1)
            nc.gpsimd.affine_select(rank_mask[:], rank_mask[:], [[-RANK, SPW], [0, SEQ]], ALU.is_ge, 0.0,
                                    base=0, channel_multiplier=1).then_inc(pool_const, 1)
            nc.gpsimd.affine_select(ident[:], ident[:], [[-1, P]], ALU.not_equal, 1.0,
                                    base=0, channel_multiplier=1).then_inc(pool_const, 1)
            pool.wait_ge(pool_const, 5)
            nc.gpsimd.affine_select(mix_mask[:], mix_mask[:], [[SEQ, SPB], [0, SEQ]], ALU.is_ge, 0.0,
                                    base=SEQ - 1, channel_multiplier=-1).then_inc(pool_const, 1)
            nc.gpsimd.affine_select(rank_mask[:], rank_mask[:], [[RANK, SPW], [0, SEQ]], ALU.is_ge, 0.0,
                                    base=RANK - 1, channel_multiplier=-1).then_inc(pool_const, 1)
            pool.wait_ge(index_made, 2)
            gather_mix(t0)
            set_lora_rows(t0)
            for c in range(2):
                gather_b(t0, c)
            gather_mix(t0.next())
            pool.wait_ge(lo["bg"], 1)
            pool.wait_ge(lo["bu"], 1)
            gather_b(t0, 2)
            serve(seam_steps(None, t0))
            with pool.Fori(0, TILES // 2 - 1) as i:
                for k in range(2):
                    serve(body_steps(Tile(i, k), Tile(i, k + 1)))
            serve(body_steps(Tile(0, TILES - 2), Tile(0, TILES - 1)))
            serve(body_steps(Tile(0, TILES - 1), None))

        @block.scalar
        def _(act):
            def copy(out, in_):
                return nc.scalar.activation(out, in_, ACT.Copy)

            def round_w(t, c, q):
                name = ("wg", "wu", "wd")[q]
                a, fill = t.chunk(c)
                act.wait_ge(in_w[a][q], 16 * fill)
                copy(w_hi[q][:], w_raw[:, a, q, :]).then_inc(hi[name], 1)
                if q == DOWN:
                    rows = t if c < FC else t.next()
                    act.wait_ge(in_ad[c % FC >= HALF], 16 * SPT * rows.count(1, 1))
                    copy(ad_hi[:], ad_raw[:, :, c % FC, :]).then_inc(hi["ad"], 1)
                else:
                    act.wait_ge(in_b[a], 16 * NW * fill)
                    copy(b_hi[q][:], b_raw[:, a, :, q * P:(q + 1) * P]).then_inc(hi[("bg", "bu")[q]], 1)

            def serve(steps):
                for step, j, t in steps:
                    if step == "prep_x":
                        act.wait_ge(in_x[j % 2], 16 * t.count(2, j // 2 + 1))
                        wait(act, pe["cond"], t.count(BLK, j - 1 if t.first() else j))
                        wait(act, pe["gate"], t.count(FC, 3 - FC))
                        copy(x_part(t, j)[0][:], x_raw[:, j % 2, :]).then_inc(hi["x"], 1)
                        act.wait_ge(mix_made, t.count(BLK, j + 1))
                        copy(mix_part(t, j)[0], mix[:].rearrange("p s c -> p (s c)")).then_inc(hi["mix"], 1)
                    elif step == "prep_a":
                        act.wait_ge(in_ag, 16 * SPT * t.count(1, 1))
                        act.wait_ge(pe["cond"], t.count(BLK, BLK))
                        for w in range(NW):
                            last = copy(by_window(da_hi)[:, w], ag_by_window[:, w])
                        last.then_inc(hi["ag"], 1)
                    elif step == "prep_b":
                        act.wait_ge(in_bd, 16 * NW * t.count(1, 1))
                        act.wait_ge(pe["gate"], t.count(FC, 3))
                        copy(bd_hi[:], bd_raw).then_inc(hi["bd"], 1)
                    elif step == "small":
                        act.wait_ge(in_first, 64)
                        at = 0
                        for part_hi in (rt_hi, a0_hi[:], b0_hi[:].unsqueeze(1), ct_hi):
                            _, groups, n = part_hi.shape
                            copy(part_hi, d_in[0][:, at:at + groups * n].rearrange("p (k n) -> p k n", k=groups))\
                                .then_inc(hi["const"], 1)
                            at += groups * n
                    elif step == "first_base":
                        act.wait_ge(out_d, 16)
                        copy(base_hi[:].rearrange("p k n -> p (k n)"), d_in[1]).then_inc(hi["d"], 1)
                    elif step == "first_w":
                        round_w(t, 0, j)
                    elif step == "prep_dense":
                        prepare(Tile(0, 0))
                    elif step == "prep_ffn":
                        act.wait_ge(in_ffn, 16)
                        act.wait_ge(pe["base"], KD * TILES)
                        copy(base_hi[:].rearrange("p k n -> p (k n)"), d_in[0]).then_inc(hi["ffn"], 1)
                    elif step == "cond":
                        act.wait_ge(pe["cond"], t.count(BLK, j + 1))
                        copy(xc_hi[:, :, j * P:(j + 1) * P],
                             front_bank(t, step, j)[:].rearrange("p (k n) -> p k n", k=KD)).then_inc(hi["xc"], 1)
                    elif step == "router":
                        act.wait_ge(pe["router"], t.count(1, 1))
                        copy(logit_t, spare[0:2 * NR, :]).then_inc(spare_free, 1)
                    elif step == "turn":
                        act.wait_ge(exp_ready, t.count(1, 1))
                        nc.scalar.activation(logit[:], logit[:], ACT.Exp).then_inc(exp_done, 1)
                    elif step == "probs":
                        act.wait_ge(pe["probs"], t.count(1, 1))
                        copy(probs_t, spare[0:NR, :]).then_inc(spare_free, 1)
                    elif step == "expand":
                        act.wait_ge(pe["expand"], t.count(1, 1))
                        copy(hw[:], spare[:]).then_inc(spare_free, 1)
                    elif step == "h":
                        act.wait_ge(spare_free, t.count(SPARE, USE[step, j] + 1))
                        copy(hw_hi[:], hw[:]).then_inc(hi["hw"], 1)
                    elif step == "base":
                        act.wait_ge(spare_free, t.count(SPARE, USE[step, j] + 1))
                        copy(x1_hi[t.par][:, j, :], res_place(t, j)).then_inc(hi["x1"], 1)
                    elif step == "lora":
                        act.wait_ge(spare_free, t.count(SPARE, USE[step, j] + 1))
                        wait(act, pe[("gate", "up")[j]], t.count(FC, 0))
                        copy(gu_hi[j][:], ranks[:, j, :]).then_inc(hi["lora"], 1)
                    elif step in ("gate", "up"):
                        act.wait_ge(pe[step], t.count(FC, j + 1))
                        if step == "gate":
                            wait(act, lo["act"], t.count(FC, j - 1))
                            nc.scalar.activation(s[:, t.chunk(j)[0], :], p_gate[:], ACT.Silu).then_inc(silu_done, 1)
                        if t.has_chunk(j + 1):
                            round_w(t, j + 1, GATE if step == "gate" else UP)
                    elif step == "down":
                        if t is None:
                            t, j = Tile(0, -1), FC - 1
                            round_act(Tile(0, 0), 0)
                            round_w(Tile(0, 0), 0, DOWN)
                            continue
                        act.wait_ge(pe["down"], t.count(FC, j + 1))
                        if j == FC - 1:
                            act.wait_ge(rank_made, t.count(1, 1))
                            copy(x_hi[:], ranks[:, 0, :]).then_inc(hi["rank"], 1)
                        if t.has_chunk(j + 1):
                            round_act(t, j + 1)
                            round_w(t, j + 1, DOWN)
                    elif step == "final":
                        act.wait_ge(pe["final"], t.count(1, 1))
                        act.wait_ge(lo["bd"], t.count(1, 1))
                        for m in range(0, KD, 2):
                            last = copy(d_raw[:, m, :], p_d[m][:])
                        last.then_inc(d_act, 1)
                        act.wait_ge(d_dve, t.count(1, 1))
                        act.wait_ge(d_act, t.count(1, 1))
                        copy(da_hi[:], d_raw[:].rearrange("p k n -> p (k n)")).then_inc(hi["d"], 1)
                    elif step == "cluster":
                        act.wait_ge(pe["cluster"], t.count(1, 1))
                        copy(cl_t, spare[:]).then_inc(spare_free, 1)
                    elif step == "cl_turn":
                        act.wait_ge(spare_free, after_front(t) + 2)
                        nc.scalar.activation(cl[:], cl[:], ACT.Exp, scale=1.0 / TEMPERATURE).then_inc(cl_exp, 1)

            def prepare(t):
                act.wait_ge(in_d[t.par], 16 * (t.i + t.k // 2 + 1))
                if t.fixed and t.k < 2:
                    act.wait_ge(pe["up"], FC * (TILES - 1 + t.k))
                else:
                    act.wait_ge(dense_free, t.count(KD, -KD))
                copy(x1_hi[t.par][:].rearrange("p k n -> p (k n)"), d_in[t.par]).then_inc(hi["dense"], 1)

            def round_act(t, c):
                act.wait_ge(prod_done, t.count(FC, c + 1))
                copy(act_hi[:], s[:, t.chunk(c)[0], :]).then_inc(hi["act"], 1)

            t0 = Tile(0, 0)
            serve(front_steps(t0))
            serve(seam_steps(None, t0))
            with act.Fori(0, TILES // 2 - 1) as i:
                for k in range(2):
                    serve(body_steps(Tile(i, k), Tile(i, k + 1)))
            serve(body_steps(Tile(0, TILES - 2), Tile(0, TILES - 1)))
            serve(body_steps(Tile(0, TILES - 1), None))

            def copy_hits(t):
                act.wait_ge(pe["hits"], t.count(1, 1))
                copy(ranks[:, t.par, :], spare[:]).then_inc(hits_copied, 1)

            prepare(Tile(0, 1))
            copy_hits(Tile(0, 0))
            with act.Fori(0, TILES // 2 - 1) as i:
                for k in (1, 2):
                    copy_hits(Tile(i, k))
                    prepare(Tile(i, k + 1))
            copy_hits(Tile(0, TILES - 1))

        @block.vector
        def _(dve):
            def minus(out, a, b):
                return nc.vector.tensor_tensor(out, a, b.bitcast(F32), ALU.subtract)

            def rest_w(t, c, q):
                name = ("wg", "wu", "wd")[q]
                a, _ = t.chunk(c)
                dve.wait_ge(hi[name], t.count(FC, c + 1))
                minus(w_lo[q][:], w_raw[:, a, q, :], w_hi[q][:]).then_inc(lo[name], 1)
                other = ("bg", "bu", "ad")[q]
                dve.wait_ge(hi[other], t.count(FC, c + 1))
                if q == DOWN:
                    minus(ad_lo[:], ad_raw[:, :, c % FC, :], ad_hi[:]).then_inc(lo["ad"], 1)
                else:
                    minus(b_lo[q][:], b_raw[:, a, :, q * P:(q + 1) * P], b_hi[q][:]).then_inc(lo[other], 1)

            def rest(t):
                dve.wait_ge(hi["dense"], t.count(1, 1))
                minus(x1_lo[t.par][:].rearrange("p k n -> p (k n)"), d_in[t.par],
                      x1_hi[t.par][:].rearrange("p k n -> p (k n)")).then_inc(lo["dense"], 1)

            def rest_act(t, c):
                dve.wait_ge(hi["act"], t.count(FC, c + 1))
                minus(act_lo[:], s[:, t.chunk(c)[0], :], act_hi[:]).then_inc(lo["act"], 1)

            def masked(out, psum):
                return nc.vector.tensor_tensor(
                    out.rearrange("p (w n) -> p w n", w=NW), psum[:].rearrange("p (w n) -> p w n", w=NW),
                    rank_mask[:].rearrange("p s c -> p (s c)").unsqueeze(1).to_broadcast([P, NW, WIN]), ALU.mult)

            def route(t):
                def link(ins, n, before_max=False):
                    ins.then_inc(route_step, 1)
                    dve.wait_ge(route_step, t.count(6, n))
                    if before_max:
                        passed(dve)

                def wide(x):
                    return x.unsqueeze(2).to_broadcast([P, BLK, NR])

                dve.wait_ge(pe["turn"], t.count(1, 1))
                nc.vector.tensor_tensor(logit[:], spare[:, 0:BLK * NR].rearrange("p (b n) -> p b n", b=BLK),
                                        rbias[:].unsqueeze(1).to_broadcast([P, BLK, NR]), ALU.add)\
                    .then_inc(spare_free, 1)
                dve.wait_ge(spare_free, t.count(SPARE, USE["turn", 0] + 1))
                link(nc.vector.tensor_reduce(stat[:, 0, :], logit[:], AX.X, ALU.max), 1)
                nc.vector.tensor_tensor(logit[:], logit[:], wide(stat[:, 0, :]), ALU.subtract).then_inc(exp_ready, 1)
                dve.wait_ge(exp_done, t.count(1, 1))
                link(nc.vector.tensor_reduce(stat[:, 1, :], logit[:], AX.X, ALU.add), 2)
                link(nc.vector.reciprocal(stat[:, 2, :], stat[:, 1, :]), 3)
                link(nc.vector.tensor_tensor(logit[:], logit[:], wide(stat[:, 2, :]), ALU.mult), 4, True)
                for b in range(BLK):
                    last = nc.vector.max(top[:, b, :], logit[:, b, :])
                link(last, 5, True)
                for b in range(BLK):
                    last = nc.vector.match_replace(chosen[:, b, :], top[:, b, :], logit[:, b, :], 0.0)
                link(last, 6)
                nc.vector.tensor_tensor(chosen[:], logit[:], chosen[:], ALU.subtract).then_inc(chosen_done, 1)

            def clusters(t):
                def link(ins, n):
                    ins.then_inc(cl_step, 1)
                    dve.wait_ge(cl_step, t.count(6, n))

                def wide(x):
                    return x.unsqueeze(2).to_broadcast([P, BLK, CL])

                logits = spare[:, 0:BLK * CL].rearrange("p (b n) -> p b n", b=BLK)
                dve.wait_ge(pe["cl_turn"], t.count(1, 1))
                link(nc.vector.tensor_reduce(cl_stat[:, 0, :], logits, AX.X, ALU.max), 1)
                nc.vector.tensor_tensor(cl[:], logits, wide(cl_stat[:, 0, :]), ALU.subtract).then_inc(spare_free, 1)
                dve.wait_ge(cl_exp, t.count(1, 1))
                link(nc.vector.tensor_reduce(cl_stat[:, 1, :], cl[:], AX.X, ALU.add), 2)
                link(nc.vector.reciprocal(cl_stat[:, 2, :], cl_stat[:, 1, :]), 3)
                link(nc.vector.tensor_tensor(cl[:], cl[:], wide(cl_stat[:, 2, :]), ALU.mult), 4)
                link(nc.vector.tensor_reduce(cl_stat[:, 0, :], cl[:], AX.X, ALU.max), 5)
                nc.vector.tensor_tensor(cl_best[:], cl_best[:], cl[:], ALU.max)
                link(nc.vector.tensor_scalar(hit[:, bass.ds(t.count(BLK, 0), BLK)], cl_stat[:, 0, :], THRESHOLD, None,
                                             ALU.is_gt), 6)

            def serve(steps):
                for step, j, t in steps:
                    if step == "prep_x":
                        if t.first() and j == 0:
                            dve.wait_ge(in_mix_first, 16)
                        else:
                            dve.wait_ge(in_mix[t.par], 16 * BLK * (t.i + t.k // 2 + 1) - (16 if t.par == 0 else 0))
                        wait(dve, lo["mix"], t.count(BLK, j))
                        nc.vector.tensor_tensor(mix[:], mixw[:, t.par, j:j + 1, :].to_broadcast([P, SPB, SEQ]),
                                                mix_mask[:], ALU.mult).then_inc(mix_made, 1)
                        dve.wait_ge(hi["x"], t.count(BLK, j + 1))
                        x_h, x_l = x_part(t, j)
                        minus(x_l[:], x_raw[:, j % 2, :], x_h[:]).then_inc(lo["x"], 1)
                        dve.wait_ge(hi["mix"], t.count(BLK, j + 1))
                        mix_h, mix_l = mix_part(t, j)
                        minus(mix_l, mix[:].rearrange("p s c -> p (s c)"), mix_h).then_inc(lo["mix"], 1)
                    elif step == "prep_a":
                        dve.wait_ge(hi["ag"], t.count(1, 1))
                        for w in range(NW):
                            last = minus(by_window(da_lo)[:, w], ag_by_window[:, w], by_window(da_hi)[:, w])
                        last.then_inc(lo["ag"], 1)
                    elif step == "prep_b":
                        dve.wait_ge(hi["bd"], t.count(1, 1))
                        minus(bd_lo[:], bd_raw, bd_hi[:]).then_inc(lo["bd"], 1)
                    elif step == "small":
                        dve.wait_ge(in_small, 64)
                        dve.wait_ge(pool_const, 5)
                        for fold, n in ((fold_rt, NR), (fold_ct, CL)):
                            nc.vector.tensor_tensor(fold[:], ident[0:2 * n, 0:n], ident[0:2 * n, n:2 * n], ALU.add)
                        start(nc.vector.tensor_copy(map_f[:], map_i[:]), 3)
                        nc.vector.tensor_scalar(spread[:], e_index[:], map_f[:], SCALING, ALU.is_equal, ALU.mult)\
                            .then_inc(spread_made, 1)
                        at = 0
                        for w, (part_hi, part_lo) in enumerate((
                                (rt_hi, rt_lo), (a0_hi[:], a0_lo[:]), (b0_hi[:].unsqueeze(1), b0_lo[:].unsqueeze(1)),
                                (ct_hi, ct_lo))):
                            _, groups, n = part_hi.shape
                            dve.wait_ge(hi["const"], w + 1)
                            minus(part_lo, d_in[0][:, at:at + groups * n].rearrange("p (k n) -> p k n", k=groups),
                                  part_hi).then_inc(lo["const"], 1)
                            at += groups * n
                    elif step == "first_base":
                        dve.wait_ge(hi["d"], 1)
                        minus(base_lo[:].rearrange("p k n -> p (k n)"), d_in[1],
                              base_hi[:].rearrange("p k n -> p (k n)")).then_inc(lo["d"], 1)
                    elif step == "first_w":
                        rest_w(t, 0, j)
                    elif step == "prep_dense":
                        rest(Tile(0, 0))
                    elif step == "prep_ffn":
                        dve.wait_ge(hi["ffn"], 1)
                        minus(base_lo[:].rearrange("p k n -> p (k n)"), d_in[0],
                              base_hi[:].rearrange("p k n -> p (k n)")).then_inc(lo["ffn"], 1)
                    elif step == "cond":
                        dve.wait_ge(hi["xc"], t.count(BLK, j + 1))
                        cols = slice(j * P, (j + 1) * P)
                        minus(xc_lo[:, :, cols], front_bank(t, step, j)[:].rearrange("p (k n) -> p k n", k=KD),
                              xc_hi[:, :, cols])\
                            .then_inc(spare_free, 1)
                    elif step == "turn":
                        route(t)
                    elif step == "h":
                        dve.wait_ge(pe["h"], t.count(1, 1))
                        dve.wait_ge(spare_free, t.count(SPARE, USE["h", 0]))
                        nc.vector.tensor_tensor(hw[:], front_bank(t, step, j)[:], hw[:], ALU.mult)\
                            .then_inc(spare_free, 1)
                        dve.wait_ge(hi["hw"], t.count(1, 1))
                        minus(hw_lo[:], hw[:], hw_hi[:]).then_inc(lo["hw"], 1)
                    elif step == "base":
                        dve.wait_ge(pe["base"], t.count(KD, j + 1))
                        dve.wait_ge(in_res[j % 2], 16 * res_loads(t, j))
                        r = res_place(t, j)
                        nc.vector.scalar_tensor_tensor(r, front_bank(t, step, j)[:], bias0[:, j:j + 1], r,
                                                       ALU.add, ALU.add)\
                            .then_inc(spare_free, 1)
                        split = range(max(j - 1, 0), j + (j == KD - 1)) if t.first() else (j,)
                        for m in split:
                            dve.wait_ge(hi["x1"], t.count(KD, m + 1))
                            minus(x1_lo[t.par][:, m, :], res_place(t, m), x1_hi[t.par][:, m, :]).then_inc(lo["x1"], 1)
                    elif step == "lora":
                        dve.wait_ge(pe["lora"], t.count(2, j + 1))
                        masked(ranks[:, j, :], front_bank(t, step, j))\
                            .then_inc(spare_free, 3 if t.fixed and t.k == 0 and j == 1 else 1)
                        dve.wait_ge(hi["lora"], t.count(2, j + 1))
                        minus(gu_lo[j][:], ranks[:, j, :], gu_hi[j][:]).then_inc(lo["lora"], 1)
                    elif step == "gate":
                        if t.has_chunk(j + 1):
                            rest_w(t, j + 1, GATE)
                    elif step == "up":
                        dve.wait_ge(pe["up"], t.count(FC, j + 1))
                        dve.wait_ge(silu_done, t.count(FC, j + 1))
                        chunk = s[:, t.chunk(j)[0], :]
                        nc.vector.tensor_tensor(chunk, chunk, p_up[:], ALU.mult).then_inc(prod_done, 1)
                        if t.has_chunk(j + 1):
                            rest_w(t, j + 1, UP)
                    elif step == "down":
                        if t is None:
                            rest_act(Tile(0, 0), 0)
                            rest_w(Tile(0, 0), 0, DOWN)
                            continue
                        if j == FC - 1:
                            dve.wait_ge(pe["down"], t.count(FC, FC))
                            masked(ranks[:, 0, :], p_rank).then_inc(rank_made, 1)
                            dve.wait_ge(hi["rank"], t.count(1, 1))
                            minus(x_lo[:], ranks[:, 0, :], x_hi[:]).then_inc(lo["rank"], 1)
                        if t.has_chunk(j + 1):
                            rest_act(t, j + 1)
                            rest_w(t, j + 1, DOWN)
                    elif step == "final":
                        dve.wait_ge(pe["final"], t.count(1, 1))
                        for m in range(1, KD, 2):
                            last = nc.vector.tensor_copy(d_raw[:, m, :], p_d[m][:])
                        last.then_inc(d_dve, 1)
                        dve.wait_ge(hi["d"], t.count(1, 2))
                        minus(da_lo[:], d_raw[:].rearrange("p k n -> p (k n)"), da_hi[:]).then_inc(lo["d"], 1)
                    elif step == "cl_turn":
                        clusters(t)

            t0 = Tile(0, 0)

            def start(ins, n):
                ins.then_inc(start_step, 1)
                dve.wait_ge(start_step, n)

            dve.wait_ge(pool_const, 1)
            nc.vector.tensor_scalar(low5[:], part[:], SEQ - 1, None, ALU.bitwise_and)
            start(nc.vector.tensor_scalar(low4[:], part[:], RANK - 1, None, ALU.bitwise_and), 1)
            nc.vector.tensor_copy(low5f[:], low5[:])
            nc.vector.tensor_copy(part_f[:], part[:])
            start(nc.vector.tensor_copy(low4f[:], low4[:]), 2)
            dve.wait_ge(in_index, 32)
            nc.vector.tensor_scalar(subj_row[:], subj_i[:], float(SEQ), low5f[:], ALU.mult, ALU.add)\
                .then_inc(index_made, 1)
            nc.vector.tensor_scalar(lora_row[:], lora_i[:], float(RANK), low4f[:], ALU.mult, ALU.add)\
                .then_inc(index_made, 1)
            nc.vector.memset(cl_best[:], 0.0)
            dve.wait_ge(pool_const, 7)
            serve(front_steps(t0))
            serve(seam_steps(None, t0))
            with dve.Fori(0, TILES // 2 - 1) as i:
                for k in range(2):
                    serve(body_steps(Tile(i, k), Tile(i, k + 1)))
            serve(body_steps(Tile(0, TILES - 2), Tile(0, TILES - 1)))
            serve(body_steps(Tile(0, TILES - 1), None))

            dve.wait_ge(cl_step, 6 * TILES)
            nc.vector.tensor_reduce(best_1, cl_best[:].rearrange("p b c -> p c b"), AX.X, ALU.max).then_inc(sel_step, 1)
            nc.vector.tensor_copy(ident_r, ident[:]).then_inc(identr_made, 1)
            dve.wait_ge(in_assign, 16)
            nc.vector.tensor_copy(assign_f, assign_i).then_inc(sel_step, 1)
            dve.wait_ge(sel_step, 2)
            nc.vector.tensor_scalar(onehot, assign_f, part_f[0:CL], None, ALU.is_equal).then_inc(sel_step, 1)
            dve.wait_ge(pe["best"], 1)
            nc.vector.tensor_reduce(best_2, spare[0:CL, 0:P], AX.X, ALU.max).then_inc(sel_step, 1)
            dve.wait_ge(sel_step, 4)
            nc.vector.tensor_scalar(sel, best_2, THRESHOLD, None, ALU.is_gt).then_inc(sel_step, 1)

            def spread_hits(t):
                nc.vector.tensor_copy(
                    hit_spread, hit[:, bass.ds(t.count(BLK, 0), BLK)].unsqueeze(2).to_broadcast([P, BLK, P]))\
                    .then_inc(hits_spread, 1)

            def output(t):
                dve.wait_ge(hits_copied, t.count(1, 1))
                for m in range(KD):
                    b = KD * t.par + m
                    dve.wait_ge(pe["dense"], t.count(KD, m + 1))
                    nc.vector.scalar_tensor_tensor(s[:, m % 2, :], dense_bank[t.par][m][:], bias1[:, m:m + 1],
                                                   ranks[:, t.par, :], ALU.add, ALU.mult).then_inc(dense_free, 1)
                    dve.wait_ge(dense_free, t.count(KD, m + 1))
                    dve.wait_ge(in_x1[b], 16 * (t.i + t.k // 2 + 1))
                    nc.vector.scalar_tensor_tensor(y_buf[b], s[:, m % 2, :], row_sel[:, m:m + 1], y_buf[b],
                                                   ALU.mult, ALU.add).then_inc(y_made, 1)
                    if m == 0 and t.next().exists():
                        spread_hits(t.next())
                    if m == 1 and t.next().exists() and not (t.fixed and t.k == 0):
                        rest(t.next())

            spread_hits(Tile(0, 0))
            rest(Tile(0, 1))
            dve.wait_ge(pe["rows"], 1)
            nc.vector.tensor_copy(row_sel, spare[:, 0:KD]).then_inc(rows_ready, 1)
            dve.wait_ge(rows_ready, 1)
            output(Tile(0, 0))
            with dve.Fori(0, TILES // 2 - 1) as i:
                for k in (1, 2):
                    output(Tile(i, k))
            output(Tile(0, TILES - 1))

        @block.tensor
        def _(ten):
            def product(out, w, x, first=True, last=True):
                nc.tensor.matmul(out, w[0], x[0], start=first, stop=False, skip_group_check=True)
                nc.tensor.matmul(out, w[0], x[1], start=False, stop=False, skip_group_check=True)
                return nc.tensor.matmul(out, w[1], x[0], start=False, stop=last, skip_group_check=True)

            def cols(pr, a, b):
                return pr[0][:, a:b], pr[1][:, a:b]

            def chunk3(pr, k, a, b):
                return pr[0][:, k, a:b], pr[1][:, k, a:b]

            da, bd, act_p, x_p = (da_hi, da_lo), (bd_hi, bd_lo), (act_hi, act_lo), (x_hi, x_lo)
            xc, hw_p, base_p, a0_p, b0_p = (xc_hi, xc_lo), (hw_hi, hw_lo), (base_hi, base_lo), (a0_hi, a0_lo), (b0_hi, b0_lo)
            ad = (ad_hi, ad_lo)

            def product_packed(out, w, x, first, last):
                nc.tensor.matmul(out, w, x[0], start=first, stop=False, skip_group_check=True)
                return nc.tensor.matmul(out, w, x[1], start=False, stop=last, skip_group_check=True)

            def gate_up(t, c, q):
                ten.wait_ge(lo[("wg", "wu")[q]], t.count(FC, c + 1))
                wait(ten, (silu_done, prod_done)[q], t.count(FC, c))
                if c == 0 and q == 0:
                    ten.wait_ge(lo["x1"], t.count(KD, KD))
                bank_ = (p_gate, p_up)[q]
                w, x1 = (w_hi[q], w_lo[q]), (x1_hi[t.par], x1_lo[t.par])
                for k in range(KD):
                    product(bank_[:], cols(w, k * P, (k + 1) * P), chunk3(x1, k, 0, N), first=k == 0, last=False)
                ten.wait_ge(lo[("bg", "bu")[q]], t.count(FC, c + 1))
                if c == 0:
                    ten.wait_ge(lo["lora"], t.count(2, q + 1))
                for v in range(NW):
                    at = slice(v * WIN, (v + 1) * WIN)
                    mm = product(bank_[:, at], (b_hi[q][:, v, :], b_lo[q][:, v, :]),
                                 cols((gu_hi[q], gu_lo[q]), v * WIN, (v + 1) * WIN), first=False)
                mm.then_inc(pe[("gate", "up")[q]], 1)

            def down(t, c):
                ten.wait_ge(lo["act"], t.count(FC, c + 1))
                ten.wait_ge(lo["wd"], t.count(FC, c + 1))
                if c == 0:
                    wait(ten, d_act, t.count(1, 0))
                    wait(ten, d_dve, t.count(1, 0))
                    wait(ten, rank_made, t.count(1, 0))
                for m in range(KD):
                    product(p_d[m][:], cols((w_hi[DOWN], w_lo[DOWN]), m * P, (m + 1) * P), cols(act_p, 0, N),
                            first=c == 0, last=False)
                ten.wait_ge(lo["ad"], t.count(FC, c + 1))
                for v in range(NW):
                    w = [x[:, v * SPW:(v + 1) * SPW, :].rearrange("p s r -> p (s r)") for x in ad]
                    mm = product(p_rank[:, v * WIN:(v + 1) * WIN], w, cols(act_p, v * WIN, (v + 1) * WIN),
                                 first=c == 0 and v == 0, last=c == FC - 1)
                mm.then_inc(pe["down"], 1)

            def base_main(t, j):
                ten.wait_ge(lo["d"], 1)
                for k in range(KD):
                    product(front_bank(t, "base", j)[:], chunk3(base_p, k, j * P, (j + 1) * P),
                            chunk3(xc, k, 0, N), k == 0, False)

            def front(step, j, t):
                to = front_bank(t, step, j)
                if to is spare:
                    wait(ten, spare_free, t.count(SPARE, USE[step, j]))
                if step == "cond":
                    ten.wait_ge(lo["x"], t.count(BLK, j + 1))
                    ten.wait_ge(lo["mix"], t.count(BLK, j + 1))
                    for k in range(KD):
                        mm = product(to[:, k * P:(k + 1) * P], cols(x_part(t, j), k * P, (k + 1) * P),
                                     mix_part(t, j))
                elif step == "router":
                    ten.wait_ge(lo["const"], 4)
                    for k in range(KD):
                        mm = product_packed(spare[0:2 * NR, :], rt[:, k, :], chunk3(xc, k, 0, N), k == 0, k == KD - 1)
                elif step == "turn":
                    passed(ten)
                    for b in range(BLK):
                        mm = nc.tensor.matmul(spare[:, b * NR:(b + 1) * NR], logit_t[:, b * P:(b + 1) * P], fold_rt[:],
                                              start=True, stop=True)
                elif step == "probs":
                    ten.wait_ge(chosen_done, t.count(1, 1))
                    for b in range(BLK):
                        mm = nc.tensor.transpose(spare[0:NR, b * P:(b + 1) * P], chosen[:, b, :], ident[:])
                elif step == "expand":
                    ten.wait_ge(spread_made, 1)
                    mm = nc.tensor.matmul(spare[:], spread[:].rearrange("n e r -> n (e r)"), probs_t,
                                          start=True, stop=True)
                elif step == "h":
                    for k in range(KD):
                        mm = product(to[:], chunk3(a0_p, k, 0, P), chunk3(xc, k, 0, N), k == 0, k == KD - 1)
                elif step == "base":
                    if not t.first():
                        base_main(t, j)
                    ten.wait_ge(lo["hw"], t.count(1, 1))
                    mm = product(to[:], cols(b0_p, j * P, (j + 1) * P), cols(hw_p, 0, N), False, True)
                elif step == "lora":
                    ten.wait_ge(lo["ag"], t.count(1, 1))
                    for v in range(NW):
                        for k in range(KD):
                            if j == 0 and v == 0:
                                ten.wait_ge(lo["x1"], t.count(KD, k + 1))
                            at = (v * 2 * KD + 2 * k + j) * P
                            mm = product(to[:, v * WIN:(v + 1) * WIN], cols(da, at, at + P),
                                         chunk3((x1_hi[t.par], x1_lo[t.par]), k, v * WIN, (v + 1) * WIN),
                                         k == 0, k == KD - 1)
                mm.then_inc(pe[step], 1)

            def serve(steps):
                for step, j, t in steps:
                    if step in ("gate", "up"):
                        gate_up(t, j, GATE if step == "gate" else UP)
                    elif step == "down" and t is not None:
                        down(t, j)
                    elif step == "early_h":
                        front("h", 0, t)
                    elif step == "early_base":
                        base_main(t, j)
                    elif (step, j) in USE and not (step == "h" and t.first()):
                        front(step, j, t)
                    elif step == "final":
                        ten.wait_ge(lo["rank"], t.count(1, 1))
                        ten.wait_ge(lo["bd"], t.count(1, 1))
                        for m in range(KD):
                            for v in range(NW):
                                w = [x[:, v, m * P:(m + 1) * P] for x in bd]
                                mm = product(p_d[m][:, v * WIN:(v + 1) * WIN], w,
                                             cols(x_p, v * WIN, (v + 1) * WIN), False, True)
                        mm.then_inc(pe["final"], 1)
                    elif step == "cluster":
                        ten.wait_ge(lo["d"], t.count(1, 2))
                        ten.wait_ge(spare_free, after_front(t))
                        for k in range(KD):
                            mm = product_packed(spare[:], ct[:, k, :], cols(da, k * N, (k + 1) * N),
                                                k == 0, k == KD - 1)
                        mm.then_inc(pe["cluster"], 1)
                    elif step == "cl_turn":
                        ten.wait_ge(spare_free, after_front(t) + 1)
                        passed(ten)
                        for b in range(BLK):
                            mm = nc.tensor.matmul(spare[:, b * CL:(b + 1) * CL], cl_t[:, b * P:(b + 1) * P],
                                                  fold_ct[:], start=True, stop=True)
                        mm.then_inc(pe["cl_turn"], 1)
                    elif step == "dense":
                        if j == 0:
                            ten.wait_ge(lo["dense"], 1)
                            ten.wait_ge(lo["ffn"], 1)
                        ten.wait_ge((silu_done, prod_done, rank_made, d_act)[j], (FC, FC, 1, 1)[j] * TILES)
                        dense(Tile(0, 0), j)

            def dense(t, m):
                for k in range(KD):
                    mm = product(dense_bank[t.par][m][:], chunk3(base_p, k, m * P, (m + 1) * P),
                                 chunk3((x1_hi[t.par], x1_lo[t.par]), k, 0, N), k == 0, k == KD - 1)
                mm.then_inc(pe["dense"], 1)

            def hits(t):
                ten.wait_ge(hits_spread, t.count(1, 1))
                for b in range(BLK):
                    mm = nc.tensor.matmul(spare[:, b * P:(b + 1) * P], hit_spread[:, b, :], ident_r,
                                          start=True, stop=True)
                mm.then_inc(pe["hits"], 1)

            t0 = Tile(0, 0)
            ten.wait_ge(pool_const, 5)
            serve(front_steps(t0))
            serve(seam_steps(None, t0))
            with ten.Fori(0, TILES // 2 - 1) as i:
                for k in range(2):
                    serve(body_steps(Tile(i, k), Tile(i, k + 1)))
            serve(body_steps(Tile(0, TILES - 2), Tile(0, TILES - 1)))
            serve(body_steps(Tile(0, TILES - 1), None))

            ten.wait_ge(sel_step, 1)
            ten.wait_ge(spare_free, SPARE * TILES + 2)
            nc.tensor.transpose(spare[0:CL, 0:P], best_1, ident[:]).then_inc(pe["best"], 1)
            ten.wait_ge(sel_step, 5)
            for m in range(KD):
                mm = nc.tensor.matmul(spare[:, m:m + 1], onehot[:, m * P:(m + 1) * P], sel, start=True, stop=True)
            mm.then_inc(pe["rows"], 1)
            ten.wait_ge(lo["dense"], 2)
            ten.wait_ge(d_dve, TILES)
            dense(t0.next(), 0)
            ten.wait_ge(rows_ready, 1)
            ten.wait_ge(identr_made, 1)
            hits(t0)

            def dense_tile(t):
                ten.wait_ge(lo["dense"], t.count(1, 1))
                for m in range(KD):
                    if m < KD - 1:
                        if not (t.fixed and t.k == 1):
                            ten.wait_ge(dense_free, t.count(KD, m + 1 - 2 * KD))
                    else:
                        ten.wait_ge(dense_free, t.count(KD, 0))
                    if m or not (t.fixed and t.k == 1):
                        dense(t, m)
                    if m == 0:
                        ten.wait_ge(hits_copied, t.count(1, 0))
                        hits(t)

            dense_tile(t0.next())
            with ten.Fori(0, TILES // 2 - 1) as i:
                for k in (2, 3):
                    dense_tile(Tile(i, k))


def kernel(**inputs):
    import concourse.bacc as bacc
    from concourse.bass_utils import run_bass_kernel_spmd as run

    a = {k: np.asarray(v) for k, v in inputs.items()}

    def kmajor(w):
        return w.T.reshape(KD, P, -1).transpose(1, 0, 2).reshape(P, -1)

    def pad_f(w, axis):
        shape = list(w.shape)
        shape[axis] = FC * P
        full = np.zeros(shape, w.dtype)
        full[tuple(slice(0, n) for n in w.shape)] = w
        return full

    x = a["x"].reshape(TOKENS, D)
    router = np.zeros((NR, D), x.dtype)
    router[:NR - 1] = a["L0_ffn_router_W"]
    gate, up = (pad_f(a[n], 0).reshape(FC, P, KD, P).transpose(0, 3, 2, 1).reshape(FC, P, D)
                for n in ("L1_cond_W_gate", "L1_cond_W_up"))
    down = pad_f(a["L1_cond_W_down"], 1).reshape(D, FC, P).transpose(1, 2, 0)
    a_gu = np.stack([a["L1_cond_A_gate"][0], a["L1_cond_A_up"][0]])
    a_gu = a_gu.reshape(2, ADAPTERS, RANK, KD, P).transpose(1, 4, 3, 0, 2).reshape(ADAPTERS, P, -1)
    b_gu = pad_f(np.stack([a["L1_cond_B_gate"][0], a["L1_cond_B_up"][0]]), 2)
    b_gu = b_gu.reshape(2, ADAPTERS, FC, P, RANK).transpose(2, 1, 4, 0, 3).reshape(FC * ADAPTERS * RANK, 2 * P)
    a_dn = pad_f(a["L1_cond_A_down"][0], 2).reshape(ADAPTERS, RANK, FC, P).transpose(0, 3, 2, 1)
    subjects, loras = a["itok_B_0_30"], a["itok_B_2_6"]
    arrays = {
        "x_rows": x, "x_cols": x.T,
        "subj_rows": np.repeat(subjects.reshape(-1, SPB), SEQ, axis=1).T,
        "lora_rows": np.repeat(loras.reshape(-1, SPW), RANK, axis=1).T,
        "lora_index": loras.reshape(1, -1),
        "cond_w": a["L0_cond_weights"].reshape(-1, SEQ),
        "base_w": kmajor(a["L0_ffn_base_W"]), "base_b": a["L0_ffn_base_b"].reshape(KD, P).T,
        "router_w": kmajor(router), "router_b": a["L0_ffn_router_b"].reshape(1, -1),
        "a0": kmajor(a["L0_ffn_A"].reshape(-1, D)), "b0": a["L0_ffn_B"].transpose(0, 2, 1).reshape(-1, D),
        "expert_map": a["L0_ffn_expert_map"].reshape(-1, 1),
        "w1": np.stack([gate, up, down], axis=1),
        "a_gu": a_gu, "b_gu": b_gu, "a_dn": a_dn.reshape(ADAPTERS, P, -1),
        "b_dn": a["L1_cond_B_down"][0].transpose(0, 2, 1).reshape(-1, D),
        "ffn_w": kmajor(a["L1_ffn_weight"]), "ffn_b": a["L1_ffn_bias"].reshape(KD, P).T,
        "centroids": kmajor(a["L1_ffn_centroids"]), "assignments": a["L1_ffn_assignments"].reshape(1, -1),
    }
    arrays = {n: np.ascontiguousarray(v) for n, v in arrays.items()}
    nc = bacc.Bacc("TRN2", target_bir_lowering=False, num_devices=1)
    args = [nc.dram_tensor(n, v.shape, mybir.dt.from_np(v.dtype), kind="ExternalInput").ap() for n, v in arrays.items()]
    out = nc.dram_tensor("out_cols", (D, TOKENS), F32, kind="ExternalOutput").ap()
    adaln_ffn_kernel(nc, *args, out)
    got = run(nc, [arrays], core_ids=[0]).results[0]["out_cols"]
    return np.ascontiguousarray(got.T).reshape(BATCH, SEQ, D)
```

```python
from contextlib import ExitStack

import numpy as np

import concourse.bass as bass
from concourse import mybir
from concourse.alu_op_type import AluOpType as ALU

F32 = mybir.dt.float32
F32R = mybir.dt.float32r
I32 = mybir.dt.int32
U32 = mybir.dt.uint32
ACT = mybir.ActivationFunctionType
AX = mybir.AxisListType

P = 128
BATCH, SEQ, D = 128, 32, 512
TOKENS = BATCH * SEQ
N = 512
TILES = TOKENS // N
KD = D // P
BLK = N // P
SPB = P // SEQ
E, R0 = 8, 16
NR = 2 * E
F = 1376
FC = -(-F // P)
RANK = 16
ADAPTERS = 16
WIN = P // RANK * SEQ
NW = N // WIN
SPW = P // RANK
SPT = N // SEQ
CL = 64
QUAD = 32
THRESHOLD = 0.01
TEMPERATURE = 0.1
SCALING = 32.0 / 16.0
SCALE = 0.5

GATE, UP, DOWN = range(3)
CONDS = 2 * BLK
KH = KD // 2

FRONT_STEPS = [("cond", h) for h in range(CONDS)] + [("router", 0), ("turn", 0), ("probs", 0), ("expand", 0), ("h", 0)] \
    + [("base", m) for m in range(KD)] + [("lora", u) for u in range(2)]
USE = {step: n for n, step in enumerate(FRONT_STEPS)}
FRONT = len(FRONT_STEPS)
SPARE = FRONT + 2
HALF = 6
PART = 4


class Tile:

    def __init__(self, i, k):
        self.i, self.k, self.par = i, k, k % 2
        self.fixed = isinstance(i, int)

    def next(self):
        return Tile(self.i, self.k + 1)

    def count(self, per_tile, n):
        if self.fixed:
            return per_tile * (2 * self.i + self.k) + n
        return 2 * per_tile * self.i + (per_tile * self.k + n)

    def index(self):
        return self.count(1, 0)

    def chunk(self, c):
        g = FC * self.k + c
        half = g // 2 + 1
        if self.fixed:
            return g % 2, FC * self.i + half
        return g % 2, FC * self.i + half

    def has_chunk(self, c):
        return not self.fixed or FC * (2 * self.i + self.k) + c < FC * TILES

    def fill(self):
        return self.i + self.k // 2 + 1

    def first(self):
        return self.fixed and 2 * self.i + self.k == 0

    def exists(self):
        return not self.fixed or 2 * self.i + self.k < TILES


def wait(engine, semaphore, value):
    if not isinstance(value, int) or value > 0:
        engine.wait_ge(semaphore, value)


def after_front(t):
    return t.next().count(SPARE, FRONT if t.next().exists() else 0)


def body_steps(t, n):
    front = {
        3: ([("prep_x", 0)], [], [("cond", 0)]),
        4: ([("cond", 1), ("prep_x", 1)], [], [("cond", 2)]),
        5: ([("cond", 3), ("prep_x", 2)], [], [("cond", 4)]),
        6: ([("cond", 5), ("prep_x", 3)], [], [("cond", 6)]),
        7: ([("cond", 7)], [("router", 0)], [("turn", 0)]),
        8: ([("prep_a", 0)], [("probs", 0)], [("expand", 0)]),
        9: ([("h", 0)], [("base", 0)], [("base", 1)]),
        10: ([("base", 2)], [("base", 3)], [("lora", 0)]),
    }
    for c in range(3, FC):
        before, mid, late = front[c] if n else ([], [], [])
        if c == 5 and not n:
            yield "prep_ffn", 0, t
        if c == 8 and not n:
            yield "prep_dense", 0, t
        yield from ((s, j, n) for s, j in before)
        yield "gate", c, t
        if c == 6:
            yield "prep_b", 0, t
        yield from ((s, j, n) for s, j in mid)
        yield "up", c, t
        yield from ((s, j, n) for s, j in late)
        yield "down", c - 1, t
        if c == FC - 1 and n:
            yield "lora", 1, n
    yield from seam_steps(t, n)


def seam_steps(t, n):
    if n:
        yield "gate", 0, n
        yield "up", 0, n
    else:
        yield "dense", 0, t
    yield "down", FC - 1, t
    if n:
        yield "gate", 1, n
        yield "up", 1, n
    else:
        yield "dense", 1, t
    if t:
        yield "final", 0, t
    if n:
        yield "gate", 2, n
        yield "down", 0, n
    else:
        yield "dense", 2, t
        yield "dense", 3, t
    if t:
        yield "cluster", 0, t
    if n:
        yield "up", 2, n
    if t:
        yield "cl_turn", 0, t
    if n:
        yield "down", 1, n


def front_steps(n):
    yield from ((s, j, n) for s, j in (
        ("prep_x", 0), ("prep_x", 1), ("cond", 0), ("cond", 1), ("prep_x", 2), ("small", 0), ("cond", 2),
        ("cond", 3), ("prep_x", 3), ("cond", 4), ("cond", 5), ("cond", 6), ("cond", 7), ("first_base", 0),
        ("router", 0), ("early_h", 0), ("turn", 0), ("early_base", 0), ("early_base", 1), ("probs", 0),
        ("prep_a", 0), ("early_base", 2), ("expand", 0), ("early_base", 3), ("h", 0),
        ("base", 0), ("base", 1), ("base", 2), ("base", 3), ("first_w", GATE), ("lora", 0), ("first_w", UP),
        ("lora", 1)))


def adaln_ffn_kernel(nc, x_rows, x_cols, subj_rows, lora_rows, lora_index, cond_w, base_w, base_b, router_w,
                     router_b, a0, b0, expert_map, w1, a_gu, b_gu, a_dn, b_dn, ffn_w, ffn_b, centroids,
                     assignments, out):
    ctx = ExitStack()
    with ctx:
        def sb(name, shape, dt=F32):
            return ctx.enter_context(nc.sbuf_tensor(name, shape, dt))

        def pair(name, shape):
            return sb(name + "_hi", shape, F32R), sb(name + "_lo", shape, F32R)

        def sem(name):
            return ctx.enter_context(nc.semaphore(name))

        x1_dram = nc.dram_tensor("x1_scratch", [TILES, KD, P, N], F32, kind="Internal").ap()
        d_dram = nc.dram_tensor("d_scratch", [TILES, P, KD * N], F32, kind="Internal").ap()

        w_raw = sb("w_raw", [P, 2, 3, N])
        w_hi, w_lo = zip(*[pair(f"w{q}", [P, N]) for q in ("gate", "up", "down")])
        b_raw = sb("b_raw", [P, 2, NW, 2 * P])
        b_hi, b_lo = zip(*[pair(f"b{q}", [P, NW, P]) for q in ("gate", "up")])
        ad_raw = sb("ad_raw", [P, SPT, FC, RANK])
        ad_hi, ad_lo = pair("ad", [P, SPT, RANK])
        ag_raw = sb("ag_raw", [P, SPT, KD * 2, RANK])
        da_hi, da_lo = pair("da", [P, KD * N])
        bd_hi, bd_lo = pair("bd", [P, NW, D])
        x_raw = sb("x_raw", [P, 2, D])
        x_hi, x_lo = pair("x", [P, D])
        mixw = sb("mixw", [P, 2, SPB, SEQ])
        mix = sb("mix", [P, SPB, SEQ])
        mix_parts = sb("mix_parts", [P, 2 * P], F32R)
        xc_hi, xc_lo = pair("xc", [P, KD, N])
        res = sb("res", [P, 2, N])
        x1_hi, x1_lo = zip(*[pair(f"x1_{q}", [P, KD, N]) for q in range(2)])
        s = sb("s", [P, 2, N])
        act_hi, act_lo = pair("act", [P, N])
        hw = sb("hw", [P, N])
        hw_hi, hw_lo = pair("hw", [P, N])
        probs_t = hw_hi[0:2 * QUAD, :]
        ranks = sb("ranks", [P, 2, N])
        logit_t = ranks[0:2 * NR, 1, :]
        xc = ranks[:, 0, :].rearrange("p (h k n) -> p h k n", h=2, k=KH)
        cl_t = ranks[:, 0, :]
        gu_hi, gu_lo = zip(*[pair(f"rank{q}", [P, N]) for q in ("gate", "up")])
        d_raw = sb("d_raw", [P, KD, N])
        bd_raw = d_raw[:, 0:NW, :]

        base_hi, base_lo = pair("base", [P, KD, D])
        a0_hi, a0_lo = pair("a0", [P, KD, P])
        b0_hi, b0_lo = pair("b0", [P, D])
        rt = sb("rt", [P, KD, 2 * NR], F32R)
        ct = sb("ct", [P, KD, 2 * CL], F32R)
        rt_hi, rt_lo, ct_hi, ct_lo = rt[:, :, 0:NR], rt[:, :, NR:], ct[:, :, 0:CL], ct[:, :, CL:]
        bias0 = sb("bias0", [P, KD])
        bias1 = sb("bias1", [P, KD])
        rbias = sb("rbias", [P, NR])
        rank_mask = sb("rank_mask", [P, SPW, SEQ])
        mix_mask = sb("mix_mask", [P, SPB, SEQ])
        ident = sb("ident", [P, P])
        fold_rt = sb("fold_rt", [2 * NR, NR])
        fold_ct = sb("fold_ct", [2 * CL, CL])
        e_index = hw[0:2 * QUAD, 0:P].rearrange("p (e r) -> p e r", e=E)
        map_i = sb("map_i", [2 * QUAD, 1], I32)
        map_f = sb("map_f", [2 * QUAD, 1])
        spread = sb("spread", [2 * QUAD, E, R0], F32R)
        part = sb("part", [P, 1], I32)
        low5 = sb("low5", [P, 1], I32)
        low4 = sb("low4", [P, 1], I32)
        low5f = sb("low5f", [P, 1])
        low4f = sb("low4f", [P, 1])
        part_f = sb("part_f", [P, 1])
        subj_i = sb("subj_i", [P, TILES * BLK], I32)
        subj_row = sb("subj_row", [P, TILES * BLK], U32)
        lora_i = sb("lora_i", [P, TILES * NW], I32)
        lora_row = sb("lora_row", [P, TILES * NW], U32)
        subj_now = sb("subj_now", [P, 2, BLK], U32)
        lora_now = sb("lora_now", [P, 2, NW], U32)
        index_i = sb("index_i", [1, BATCH], I32)
        logit_pad = sb("logit_pad", [P, BLK, QUAD])
        logit = logit_pad[:, :, 0:NR]
        left_pad = sb("left_pad", [P, BLK, QUAD])
        left = left_pad[:, :, 0:NR]
        top = sb("top", [P, BLK, 8])
        stat = sb("stat", [P, 4, BLK])
        cl = sb("cl", [P, BLK, CL])
        chosen = cl[:].rearrange("p b (h n) -> p b h n", h=2)
        cl_stat = sb("cl_stat", [P, 3, BLK])
        cl_best = sb("cl_best", [P, BLK, CL])
        hit = sb("hit", [P, TILES * BLK])

        bank = [ctx.enter_context(nc.psum_tensor(f"bank{b}", [P, N], F32)) for b in range(8)]
        p_gate, p_up, p_rank, spare = bank[0], bank[1], bank[2], bank[3]
        p_d = bank[4:8]

        in_w = [[sem(f"in_w{a}{q}") for q in range(3)] for a in range(2)]
        in_b = [sem(f"in_b{a}") for a in range(2)]
        in_ad = [sem(f"in_ad{a}") for a in range(2)]
        in_ag, in_bd = sem("in_ag"), sem("in_bd")
        in_x = [sem(f"in_x{a}") for a in range(2)]
        in_mix = [sem(f"in_mix{a}") for a in range(2)]
        in_res = [sem(f"in_res{a}") for a in range(2)]
        out_x1 = [sem(f"out_x1{a}") for a in range(2)]
        out_d = sem("out_d")
        in_mix_first = sem("in_mix_first")
        in_index, in_ids, in_small, in_first = sem("in_index"), sem("in_ids"), sem("in_small"), sem("in_first")
        in_ffn, in_assign = sem("in_ffn"), sem("in_assign")
        in_d = [sem(f"in_d{a}") for a in range(2)]
        in_x1 = [sem(f"in_x1{a}") for a in range(2 * KD)]
        out_y = [sem(f"out_y{a}") for a in range(2 * KD)]

        pe = {q: sem("pe_" + q) for q in ("gate", "up", "down", "cond", "router", "turn", "probs", "expand", "h",
                                          "base", "lora", "final", "cluster", "cl_turn", "dense", "hits", "best",
                                          "rows")}
        spare_free = sem("spare_free")
        parts = ("wg", "wu", "wd", "bg", "bu", "ad", "act", "x", "mix", "ag", "bd", "hw", "x1", "lora", "rank", "d", "probs",
                 "xc", "const", "ffn", "dense")
        hi = {q: sem("hi_" + q) for q in parts}
        lo = {q: sem("lo_" + q) for q in parts}
        silu_done, prod_done = sem("silu_done"), sem("prod_done")
        mix_made, rank_made = sem("mix_made"), sem("rank_made")
        d_act, d_dve = sem("d_act"), sem("d_dve")
        exp_ready, exp_done, chosen_done = sem("exp_ready"), sem("exp_done"), sem("chosen_done")
        cl_exp = sem("cl_exp")
        route_step, cl_step, start_step = sem("route_step"), sem("cl_step"), sem("start_step")
        pool_zero, pool_const, pool_lora, pool_mix = (
            sem(q) for q in ("pool_zero", "pool_const", "pool_lora", "pool_mix"))
        index_made, spread_made, best_cleared = sem("index_made"), sem("spread_made"), sem("best_cleared")
        waits_passed = sem("waits_passed")
        identr_made, hits_spread, hits_copied, dense_free, y_made, sel_step, rows_ready = (
            sem(q) for q in ("identr_made", "hits_spread", "hits_copied", "dense_free", "y_made", "sel_step",
                             "rows_ready"))

        d_in = [ag_raw[:].rearrange("p s g r -> p (s g r)"), d_raw[:].rearrange("p k n -> p (k n)")]
        ad_flat = ad_raw[:].rearrange("p s c r -> p (s c r)")
        y_buf = [w_raw[:, a, q, :] for a in range(2) for q in range(3)] + [ad_flat[:, 0:N], ad_flat[:, N:2 * N]]
        hit_spread = gu_hi[0][:].rearrange("p (b c) -> p b c", b=BLK)
        ident_r = gu_hi[1][:, 0:P]

        def dense_bank(q, m):
            if q.first():
                return (p_gate, p_up, p_rank, p_d[0])[m]
            return ((p_up, p_rank, p_d[0], p_gate), (p_d[1], p_d[2], p_d[3], p_gate))[q.par][m]

        b_flat = b_raw[0:CL].rearrange("p a w n -> p (a w n)")
        assign_i, onehot = b_flat[:, 0:D].bitcast(I32), b_flat[:, D:2 * D]
        best_1 = ad_flat[:, 2 * N:2 * N + CL]
        best_2 = ad_flat[0:CL, 2 * N + CL:2 * N + CL + 1]
        sel = ad_flat[0:CL, 2 * N + CL + 1:2 * N + CL + 2]
        row_sel = ad_flat[:, 2 * N + CL + 2:2 * N + CL + 2 + KD]
        assign_f = s[0:CL, 0, :]

        def by_window(x):
            return x[:].rearrange("p (w g s r) -> p w g s r", w=NW, g=2 * KD, s=SPW)

        ag_by_window = ag_raw[:].rearrange("p (w s) g r -> p w g s r", w=NW)

        x_blocks = x_rows.rearrange("(b p) d -> b p d", p=P)
        x_cols_t = x_cols.rearrange("(m p) n -> m p n", p=P)

        def tokens(t):
            return bass.ds(N * t.index(), N)

        def passed(engine):
            engine.sem_inc(waits_passed, 1)

        def x_part(t, j):
            return (act_hi, act_lo) if t.first() and j % 2 else (x_hi, x_lo)

        def mix_part(t, j):
            return hw_hi[:, 0:2 * P] if t.first() and j % 2 else mix_parts[:]

        def res_place(t, m):
            return d_raw[:, m, :] if t.first() and m >= 2 else res[:, m % 2, :]

        def res_loads(t, m):
            return 2 if t.first() else t.count(2, m // 2 + 1)

        def xc_place(x, h):
            b, k = h // 2, h % 2 * KH
            return x[:, k:k + KH, b * P:(b + 1) * P]

        def front_bank(t, step, j):
            if t.first() and step == "cond":
                return bank[j]
            if t.first() and step in ("base", "lora"):
                return p_d[j]
            return p_gate if t.first() and step == "h" else spare

        block = ctx.enter_context(nc.Block())

        @block.sync
        def _(sp):
            def load_w(t, c, q, after):
                a, n = t.chunk(c)
                if after is not None:
                    sp.wait_ge(lo[("wg", "wu", "wd")[q]], after)
                sp.dma_start(w_raw[:, a, q, :], w1[c % FC, q]).then_inc(in_w[a][q], 16)

            def load_x(t, j):
                sp.dma_start(x_raw[:, j % 2, :],
                             x_blocks[bass.ds(t.count(BLK, j), 1)].rearrange("b p d -> p (b d)")).then_inc(in_x[j % 2], 16)

            def load_res(t, m):
                sp.dma_start(res_place(t, m), x_cols_t[m, :, tokens(t)]).then_inc(in_res[m % 2], 16)

            def load_adapters(t, table, dst, first, last, done, samples=range(SPT)):
                passed(sp)
                for j in samples:
                    which = sp.value_load(index_i[0:1, bass.ds(t.count(SPT, j), 1)], min_val=0, max_val=ADAPTERS - 1)
                    sp.dma_start(dst[:, j, first:last].rearrange("p c r -> p (c r)"),
                                 table[bass.ds(which, 1), :, first * RANK:last * RANK]
                                 .rearrange("o p n -> p (o n)")).then_inc(done, 16)

            def serve(steps):
                for step, j, t in steps:
                    if step in ("gate", "up") and t.has_chunk(j + 3):
                        load_w(t, j + 3, GATE if step == "gate" else UP, t.count(FC, j + 2))
                    if step == "down":
                        if t is None:
                            load_w(Tile(0, 0), 2, DOWN, 1)
                        elif t.has_chunk(j + 3):
                            load_w(t, j + 3, DOWN, t.count(FC, j + 2))
                        if t is not None and j in range(SPT // PART):
                            if j == 0:
                                wait(sp, lo["ad"], t.count(FC, 0))
                            load_adapters(t, a_dn, ad_raw, HALF, FC, in_ad[1], range(PART * j, PART * (j + 1)))
                        if t is not None and j in range(HALF, HALF + SPT // PART) and t.next().exists():
                            if j == HALF:
                                sp.wait_ge(lo["ad"], t.count(FC, HALF))
                            q = j - HALF
                            load_adapters(t.next(), a_dn, ad_raw, 0, HALF, in_ad[0], range(PART * q, PART * (q + 1)))
                    if step == "prep_x" and (j < 2 or t.next().exists()):
                        sp.wait_ge(lo["x"], t.count(BLK, j + 1))
                        if j < 2:
                            load_x(t, j + 2)
                        else:
                            load_x(t.next(), j - 2)
                    if step == "gate" and j in range(SPT // PART) and t.next().exists():
                        if j == 0:
                            sp.wait_ge(lo["ag"], t.count(1, 1))
                        load_adapters(t.next(), a_gu, ag_raw, 0, 2 * KD, in_ag, range(PART * j, PART * (j + 1)))
                    if step == "base":
                        sp.wait_ge(spare_free, t.count(SPARE, USE[step, j] + 1))
                        sp.dma_start(x1_dram[bass.ds(t.index(), 1), j].rearrange("o p n -> p (o n)"),
                                     res_place(t, j)).then_inc(out_x1[j % 2], 16)
                    if step == "base" and j > 0 and not (j < 3 and t.first()) and (j < 3 or t.next().exists()):
                        sp.wait_ge(out_x1[(j - 1) % 2], 16 * t.count(2, (j - 1) // 2 + 1))
                        sp.wait_ge(lo["x1"], t.count(KD, j))
                        if j < 3:
                            load_res(t, j + 1)
                        else:
                            load_res(t.next(), 0)
                    if step == "lora" and j == 0 and t.next().exists():
                        sp.wait_ge(out_x1[1], 16 * t.count(2, 2))
                        sp.wait_ge(lo["x1"], t.count(KD, KD))
                        load_res(t.next(), 1)
                    if step == "prep_ffn":
                        sp.wait_ge(lo["ffn"], 1)
                        sp.dma_start(d_in[0], d_dram[0]).then_inc(in_d[0], 16)
                    if step == "final":
                        sp.wait_ge(d_act, t.count(1, 1))
                        sp.wait_ge(d_dve, t.count(1, 1))
                        sp.dma_start(d_dram[bass.ds(t.index(), 1)].rearrange("o p n -> p (o n)"),
                                     d_raw[:].rearrange("p k n -> p (k n)")).then_inc(out_d, 16)

            t0 = Tile(0, 0)
            sp.dma_start(subj_i[:], subj_rows).then_inc(in_index, 16)
            sp.dma_start(lora_i[:], lora_rows).then_inc(in_index, 16)
            load_x(t0, 0)
            load_x(t0, 1)
            small = d_in[0]
            at = 0
            for w in (router_w, a0, b0, centroids):
                sp.dma_start(small[:, at:at + w.shape[1]], w).then_inc(in_first, 16)
                at += w.shape[1]
            sp.wait_ge(pool_zero, 2)
            sp.dma_start(rbias[:, 0:NR - 1], router_b.to_broadcast([P, NR - 1])).then_inc(in_small, 16)
            for at in (0, QUAD):
                sp.dma_start(map_i[at:at + NR - 1], expert_map).then_inc(in_small, 16)
            sp.dma_start(bias0[:], base_b).then_inc(in_small, 16)
            sp.dma_start(bias1[:], ffn_b).then_inc(in_small, 16)
            sp.dma_start(index_i[:], lora_index).then_inc(in_ids, 16)
            serve([("prep_x", 0, t0)])
            sp.dma_start(d_in[1], base_w).then_inc(out_d, 16)
            serve([("prep_x", 1, t0)])
            sp.wait_ge(in_ids, 16)
            sp.wait_ge(lo["const"], 4)
            load_adapters(t0, a_gu, ag_raw, 0, 2 * KD, in_ag, range(0, SPT // 2))
            serve([("prep_x", 2, t0), ("prep_x", 3, t0)])
            load_adapters(t0, a_gu, ag_raw, 0, 2 * KD, in_ag, range(SPT // 2, SPT))
            load_res(t0, 0)
            load_res(t0, 1)
            sp.wait_ge(lo["d"], 1)
            load_res(t0, 2)
            load_res(t0, 3)
            for c in range(2):
                for q in range(3):
                    load_w(t0, c, q, None)
            load_adapters(t0, a_dn, ad_raw, 0, HALF, in_ad[0])
            serve(s for s in front_steps(t0) if s[0] == "base")
            serve(s for s in front_steps(t0) if s[0] == "lora")
            load_w(t0, 2, GATE, 1)
            load_w(t0, 2, UP, 1)
            serve(seam_steps(None, t0))
            with sp.Fori(0, TILES // 2 - 1) as i:
                for k in range(2):
                    serve(body_steps(Tile(i, k), Tile(i, k + 1)))
            serve(body_steps(Tile(0, TILES - 2), Tile(0, TILES - 1)))

            sp.wait_ge(lo["ag"], TILES)
            sp.dma_start(d_in[0], ffn_w).then_inc(in_ffn, 16)
            serve(body_steps(Tile(0, TILES - 1), None))

            def load_d(t):
                sp.dma_start(d_in[t.par], d_dram[bass.ds(t.index(), 1)].rearrange("o p n -> p (o n)"))\
                    .then_inc(in_d[t.par], 16)

            def load_x1(t, q, m):
                b = KD * q.par + m
                sp.dma_start(y_buf[b], x1_dram[bass.ds(t.index(), 1), m].rearrange("o p n -> p (o n)"))\
                    .then_inc(in_x1[b], 16)

            def store_y(t, q):
                for m in range(KD):
                    b = KD * q.par + m
                    sp.wait_ge(y_made, q.count(KD, m + 1))
                    sp.dma_start(out[m * P:(m + 1) * P, tokens(t)], y_buf[b]).then_inc(out_y[b], 16)

            def reload_x1(t, q):
                for m in range(KD):
                    sp.wait_ge(out_y[KD * q.par + m], 16 * (q.fill() - 1))
                    load_x1(t, q, m)

            sp.wait_ge(out_d, 16 * (TILES + 1))
            sp.wait_ge(lo["d"], TILES + 1)
            load_d(Tile(0, 1))
            for q in range(2):
                sp.wait_ge(out_x1[q], 16 * 2 * TILES)
            for q in ("wg", "wu", "wd", "ad", "bg", "bu"):
                sp.wait_ge(lo[q], FC * TILES)
            sp.dma_start(assign_i, assignments.to_broadcast([CL, D])).then_inc(in_assign, 16)
            turns = (t0, Tile(0, TILES - 1))
            for q in range(2):
                for m in range(KD):
                    load_x1(turns[q], Tile(0, q), m)
            sp.wait_ge(lo["dense"], 1)
            load_d(Tile(0, 2))
            for q in range(2):
                store_y(turns[q], Tile(0, q))
                reload_x1(Tile(0, q + 1), Tile(0, q + 2))

            with sp.Fori(0, TILES // 2 - 2) as i:
                for k in (1, 2):
                    sp.wait_ge(lo["dense"], Tile(i, k).count(1, 1))
                    load_d(Tile(i, k + 2))
                    store_y(Tile(i, k), Tile(i, k + 1))
                    reload_x1(Tile(i, k + 2), Tile(i, k + 3))
            for k in range(TILES - 3, TILES - 1):
                store_y(Tile(0, k), Tile(0, k + 1))
            for b in range(8):
                sp.wait_ge(out_y[b], 16 * (TILES // 2))

        @block.gpsimd
        def _(pool):
            def set_lora_rows(t):
                nc.gpsimd.tensor_copy(lora_now[:, t.par, :], lora_row[:, bass.ds(t.count(NW, 0), NW)])\
                    .then_inc(pool_lora, 1)
                pool.wait_ge(pool_lora, t.count(1, 1))

            def gather_mix(t):
                nc.gpsimd.tensor_copy(subj_now[:, t.par, :], subj_row[:, bass.ds(t.count(BLK, 0), BLK)])\
                    .then_inc(pool_mix, 1)
                pool.wait_ge(pool_mix, t.count(1, 1))
                passed(pool)
                for j in range(BLK):
                    nc.gpsimd.indirect_dma_start(
                        mixw[:, t.par, j, :], None, cond_w,
                        bass.IndirectOffsetOnAxis(subj_now[:, t.par, j:j + 1], 0))\
                        .then_inc(in_mix_first if t.first() and j == 0 else in_mix[t.par], 16)

            def gather_b(t, c):
                a, _ = t.chunk(c)
                rows = t if c < FC else t.next()
                passed(pool)
                for w in range(NW):
                    nc.gpsimd.indirect_dma_start(
                        b_raw[:, a, w, :], None, b_gu,
                        bass.IndirectOffsetOnAxis(lora_now[:, rows.par, w:w + 1], 0),
                        element_offset=(c % FC) * ADAPTERS * RANK * 2 * P).then_inc(in_b[a], 16)

            def serve(steps):
                for step, j, t in steps:
                    if step == "gate" and j == 3:
                        pool.wait_ge(out_d, 16 * t.count(1, 1))
                        pool.wait_ge(lo["d"], t.count(1, 1))
                        for q in range(2):
                            pool.wait_ge(out_x1[q], 16 * t.count(2, 2))
                        passed(pool)
                        for w in range(NW):
                            nc.gpsimd.indirect_dma_start(
                                bd_raw[:, w, :], None, b_dn,
                                bass.IndirectOffsetOnAxis(lora_now[:, t.par, w:w + 1], 0)).then_inc(in_bd, 16)
                    if step == "gate" and j == 7 and t.next().exists():
                        set_lora_rows(t.next())
                    if step == "gate" and j == 7 and t.next().next().exists():
                        pool.wait_ge(lo["mix"], t.count(BLK, BLK))
                        gather_mix(t.next().next())
                    if step == "up" and t.has_chunk(j + 3):
                        pool.wait_ge(lo["bg"], t.count(FC, j + 2))
                        pool.wait_ge(lo["bu"], t.count(FC, j + 2))
                        gather_b(t, j + 3)

            t0 = Tile(0, 0)
            nc.gpsimd.iota(part[:], [[0, 1]], base=0, channel_multiplier=1).then_inc(pool_const, 1)
            nc.gpsimd.memset(map_i[:], -1).then_inc(pool_zero, 1)
            nc.gpsimd.memset(rbias[:], -1e30).then_inc(pool_zero, 1)
            nc.gpsimd.iota(e_index, [[1, E], [0, R0]], base=0, channel_multiplier=0,
                           allow_small_or_imprecise_dtypes=True).then_inc(pool_const, 1)
            nc.gpsimd.memset(mix_mask[:], 1.0).then_inc(pool_zero, 1)
            nc.gpsimd.memset(rank_mask[:], SCALE).then_inc(pool_zero, 1)
            nc.gpsimd.memset(ident[:], 0.0).then_inc(pool_zero, 1)
            pool.wait_ge(pool_zero, 5)
            nc.gpsimd.affine_select(mix_mask[:], mix_mask[:], [[-SEQ, SPB], [0, SEQ]], ALU.is_ge, 0.0,
                                    base=0, channel_multiplier=1).then_inc(pool_const, 1)
            nc.gpsimd.affine_select(rank_mask[:], rank_mask[:], [[-RANK, SPW], [0, SEQ]], ALU.is_ge, 0.0,
                                    base=0, channel_multiplier=1).then_inc(pool_const, 1)
            nc.gpsimd.affine_select(ident[:], ident[:], [[-1, P]], ALU.not_equal, 1.0,
                                    base=0, channel_multiplier=1).then_inc(pool_const, 1)
            pool.wait_ge(pool_const, 5)
            nc.gpsimd.affine_select(mix_mask[:], mix_mask[:], [[SEQ, SPB], [0, SEQ]], ALU.is_ge, 0.0,
                                    base=SEQ - 1, channel_multiplier=-1).then_inc(pool_const, 1)
            nc.gpsimd.affine_select(rank_mask[:], rank_mask[:], [[RANK, SPW], [0, SEQ]], ALU.is_ge, 0.0,
                                    base=RANK - 1, channel_multiplier=-1).then_inc(pool_const, 1)
            pool.wait_ge(index_made, 2)
            gather_mix(t0)
            set_lora_rows(t0)
            for c in range(2):
                gather_b(t0, c)
            gather_mix(t0.next())
            pool.wait_ge(lo["bg"], 1)
            pool.wait_ge(lo["bu"], 1)
            gather_b(t0, 2)
            serve(seam_steps(None, t0))
            with pool.Fori(0, TILES // 2 - 1) as i:
                for k in range(2):
                    serve(body_steps(Tile(i, k), Tile(i, k + 1)))
            serve(body_steps(Tile(0, TILES - 2), Tile(0, TILES - 1)))
            serve(body_steps(Tile(0, TILES - 1), None))

        @block.scalar
        def _(act):
            def copy(out, in_):
                return nc.scalar.activation(out, in_, ACT.Copy)

            def round_w(t, c, q):
                name = ("wg", "wu", "wd")[q]
                a, fill = t.chunk(c)
                act.wait_ge(in_w[a][q], 16 * fill)
                copy(w_hi[q][:], w_raw[:, a, q, :]).then_inc(hi[name], 1)
                if q == DOWN:
                    rows = t if c < FC else t.next()
                    act.wait_ge(in_ad[c % FC >= HALF], 16 * SPT * rows.count(1, 1))
                    copy(ad_hi[:], ad_raw[:, :, c % FC, :]).then_inc(hi["ad"], 1)
                else:
                    act.wait_ge(in_b[a], 16 * NW * fill)
                    copy(b_hi[q][:], b_raw[:, a, :, q * P:(q + 1) * P]).then_inc(hi[("bg", "bu")[q]], 1)

            def serve(steps):
                for step, j, t in steps:
                    if step == "prep_x":
                        act.wait_ge(in_x[j % 2], 16 * t.count(2, j // 2 + 1))
                        wait(act, pe["cond"], t.count(CONDS, 2 * (j - 1 if t.first() else j)))
                        wait(act, pe["gate"], t.count(FC, 3 - FC))
                        copy(x_part(t, j)[0][:], x_raw[:, j % 2, :]).then_inc(hi["x"], 1)
                        act.wait_ge(mix_made, t.count(BLK, j + 1))
                        copy(mix_part(t, j)[:, 0:P], mix[:].rearrange("p s c -> p (s c)")).then_inc(hi["mix"], 1)
                    elif step == "prep_a":
                        act.wait_ge(in_ag, 16 * SPT * t.count(1, 1))
                        act.wait_ge(pe["cond"], t.count(CONDS, CONDS))
                        for w in range(NW):
                            last = copy(by_window(da_hi)[:, w], ag_by_window[:, w])
                        last.then_inc(hi["ag"], 1)
                    elif step == "prep_b":
                        act.wait_ge(in_bd, 16 * NW * t.count(1, 1))
                        act.wait_ge(pe["gate"], t.count(FC, 3))
                        copy(bd_hi[:], bd_raw).then_inc(hi["bd"], 1)
                    elif step == "small":
                        act.wait_ge(in_first, 64)
                        at = 0
                        for part_hi in (rt_hi, a0_hi[:], b0_hi[:].unsqueeze(1), ct_hi):
                            _, groups, n = part_hi.shape
                            copy(part_hi, d_in[0][:, at:at + groups * n].rearrange("p (k n) -> p k n", k=groups))\
                                .then_inc(hi["const"], 1)
                            at += groups * n
                    elif step == "first_base":
                        act.wait_ge(out_d, 16)
                        copy(base_hi[:].rearrange("p k n -> p (k n)"), d_in[1]).then_inc(hi["d"], 1)
                    elif step == "first_w":
                        round_w(t, 0, j)
                    elif step == "prep_dense":
                        prepare(Tile(0, 0))
                    elif step == "prep_ffn":
                        act.wait_ge(in_ffn, 16)
                        act.wait_ge(pe["base"], KD * TILES)
                        copy(base_hi[:].rearrange("p k n -> p (k n)"), d_in[0]).then_inc(hi["ffn"], 1)
                    elif step == "cond":
                        act.wait_ge(spare_free, t.count(SPARE, USE[step, j] + 1))
                        copy(xc_place(xc_hi, j), xc[:, j % 2]).then_inc(hi["xc"], 1)
                    elif step == "router":
                        act.wait_ge(pe["router"], t.count(1, 1))
                        copy(logit_t, spare[0:2 * NR, :]).then_inc(spare_free, 1)
                    elif step == "turn":
                        act.wait_ge(exp_ready, t.count(1, 1))
                        nc.scalar.activation(logit, logit, ACT.Exp).then_inc(exp_done, 1)
                    elif step == "probs":
                        act.wait_ge(pe["probs"], t.count(1, 1))
                        copy(probs_t, spare[0:2 * QUAD, :]).then_inc(hi["probs"], 1)
                    elif step == "expand":
                        act.wait_ge(pe["expand"], t.count(1, 1))
                        copy(hw[:], spare[:]).then_inc(spare_free, 1)
                    elif step == "h":
                        act.wait_ge(spare_free, t.count(SPARE, USE[step, j] + 1))
                        copy(hw_hi[:], hw[:]).then_inc(hi["hw"], 1)
                    elif step == "base":
                        act.wait_ge(spare_free, t.count(SPARE, USE[step, j] + 1))
                        copy(x1_hi[t.par][:, j, :], res_place(t, j)).then_inc(hi["x1"], 1)
                    elif step == "lora":
                        act.wait_ge(spare_free, t.count(SPARE, USE[step, j] + 1))
                        wait(act, pe[("gate", "up")[j]], t.count(FC, 0))
                        copy(gu_hi[j][:], ranks[:, j, :]).then_inc(hi["lora"], 1)
                    elif step in ("gate", "up"):
                        act.wait_ge(pe[step], t.count(FC, j + 1))
                        if step == "gate":
                            wait(act, lo["act"], t.count(FC, j - 1))
                            nc.scalar.activation(s[:, t.chunk(j)[0], :], p_gate[:], ACT.Silu).then_inc(silu_done, 1)
                        if t.has_chunk(j + 1):
                            round_w(t, j + 1, GATE if step == "gate" else UP)
                    elif step == "down":
                        if t is None:
                            t, j = Tile(0, -1), FC - 1
                            round_act(Tile(0, 0), 0)
                            round_w(Tile(0, 0), 0, DOWN)
                            continue
                        act.wait_ge(pe["down"], t.count(FC, j + 1))
                        if j == FC - 1:
                            act.wait_ge(rank_made, t.count(1, 1))
                            copy(x_hi[:], ranks[:, 0, :]).then_inc(hi["rank"], 1)
                        if t.has_chunk(j + 1):
                            round_act(t, j + 1)
                            round_w(t, j + 1, DOWN)
                    elif step == "final":
                        act.wait_ge(pe["final"], t.count(1, 1))
                        act.wait_ge(lo["bd"], t.count(1, 1))
                        for m in range(0, KD, 2):
                            last = copy(d_raw[:, m, :], p_d[m][:])
                        last.then_inc(d_act, 1)
                        act.wait_ge(d_dve, t.count(1, 1))
                        act.wait_ge(d_act, t.count(1, 1))
                        copy(da_hi[:], d_raw[:].rearrange("p k n -> p (k n)")).then_inc(hi["d"], 1)
                    elif step == "cluster":
                        act.wait_ge(pe["cluster"], t.count(1, 1))
                        copy(cl_t, spare[:]).then_inc(spare_free, 1)
                    elif step == "cl_turn":
                        act.wait_ge(spare_free, after_front(t) + 2)
                        nc.scalar.activation(cl[:], cl[:], ACT.Exp, scale=1.0 / TEMPERATURE).then_inc(cl_exp, 1)

            def prepare(t):
                act.wait_ge(in_d[t.par], 16 * t.fill())
                if t.fixed and t.k < 2:
                    act.wait_ge(pe["up"], FC * (TILES - 1 + t.k))
                else:
                    act.wait_ge(dense_free, t.count(KD, 0))
                copy(x1_hi[t.par][:].rearrange("p k n -> p (k n)"), d_in[t.par]).then_inc(hi["dense"], 1)

            def round_act(t, c):
                act.wait_ge(prod_done, t.count(FC, c + 1))
                copy(act_hi[:], s[:, t.chunk(c)[0], :]).then_inc(hi["act"], 1)

            t0 = Tile(0, 0)
            serve(front_steps(t0))
            serve(seam_steps(None, t0))
            with act.Fori(0, TILES // 2 - 1) as i:
                for k in range(2):
                    serve(body_steps(Tile(i, k), Tile(i, k + 1)))
            serve(body_steps(Tile(0, TILES - 2), Tile(0, TILES - 1)))
            serve(body_steps(Tile(0, TILES - 1), None))

            def copy_hits(q):
                act.wait_ge(pe["hits"], q.count(1, 1))
                copy(ranks[:, q.par, :], spare[:]).then_inc(hits_copied, 1)

            prepare(Tile(0, 1))
            copy_hits(Tile(0, 0))
            copy_hits(Tile(0, 1))
            with act.Fori(0, TILES // 2 - 2) as i:
                for k in (1, 2):
                    copy_hits(Tile(i, k + 1))
                    prepare(Tile(i, k + 1))
            copy_hits(Tile(0, TILES - 2))
            prepare(Tile(0, TILES - 2))
            copy_hits(Tile(0, TILES - 1))

        @block.vector
        def _(dve):
            def minus(out, a, b):
                return nc.vector.tensor_tensor(out, a, b.bitcast(F32), ALU.subtract)

            def rest_w(t, c, q):
                name = ("wg", "wu", "wd")[q]
                a, _ = t.chunk(c)
                dve.wait_ge(hi[name], t.count(FC, c + 1))
                minus(w_lo[q][:], w_raw[:, a, q, :], w_hi[q][:]).then_inc(lo[name], 1)
                other = ("bg", "bu", "ad")[q]
                dve.wait_ge(hi[other], t.count(FC, c + 1))
                if q == DOWN:
                    minus(ad_lo[:], ad_raw[:, :, c % FC, :], ad_hi[:]).then_inc(lo["ad"], 1)
                else:
                    minus(b_lo[q][:], b_raw[:, a, :, q * P:(q + 1) * P], b_hi[q][:]).then_inc(lo[other], 1)

            def rest(t):
                dve.wait_ge(hi["dense"], t.count(1, 1))
                minus(x1_lo[t.par][:].rearrange("p k n -> p (k n)"), d_in[t.par],
                      x1_hi[t.par][:].rearrange("p k n -> p (k n)")).then_inc(lo["dense"], 1)

            def rest_act(t, c):
                dve.wait_ge(hi["act"], t.count(FC, c + 1))
                minus(act_lo[:], s[:, t.chunk(c)[0], :], act_hi[:]).then_inc(lo["act"], 1)

            def masked(out, psum):
                return nc.vector.tensor_tensor(
                    out.rearrange("p (w n) -> p w n", w=NW), psum[:].rearrange("p (w n) -> p w n", w=NW),
                    rank_mask[:].rearrange("p s c -> p (s c)").unsqueeze(1).to_broadcast([P, NW, WIN]), ALU.mult)

            def route(t):
                def link(ins, n, before_max=False):
                    ins.then_inc(route_step, 1)
                    dve.wait_ge(route_step, t.count(6, n))
                    if before_max:
                        passed(dve)

                def wide(x):
                    return x.unsqueeze(2).to_broadcast([P, BLK, NR])

                dve.wait_ge(pe["turn"], t.count(1, 1))
                nc.vector.tensor_tensor(logit, spare[:, 0:BLK * NR].rearrange("p (b n) -> p b n", b=BLK),
                                        rbias[:].unsqueeze(1).to_broadcast([P, BLK, NR]), ALU.add)\
                    .then_inc(spare_free, 1)
                dve.wait_ge(spare_free, t.count(SPARE, USE["turn", 0] + 1))
                link(nc.vector.tensor_reduce(stat[:, 0, :], logit, AX.X, ALU.max), 1)
                nc.vector.tensor_tensor(logit, logit, wide(stat[:, 0, :]), ALU.subtract).then_inc(exp_ready, 1)
                dve.wait_ge(exp_done, t.count(1, 1))
                link(nc.vector.tensor_reduce(stat[:, 1, :], logit, AX.X, ALU.add), 2)
                link(nc.vector.reciprocal(stat[:, 2, :], stat[:, 1, :]), 3)
                link(nc.vector.tensor_tensor(logit, logit, wide(stat[:, 2, :]), ALU.mult), 4, True)
                for b in range(BLK):
                    last = nc.vector.max(top[:, b, :], logit[:, b, :])
                link(last, 5, True)
                for b in range(BLK):
                    last = nc.vector.match_replace(left[:, b, :], top[:, b, :], logit[:, b, :], 0.0)
                link(last, 6)
                twice = [x[:].unsqueeze(2).to_broadcast([P, BLK, 2, QUAD]) for x in (logit_pad, left_pad)]
                nc.vector.tensor_tensor(chosen, *twice, ALU.subtract).then_inc(chosen_done, 1)

            def clusters(t):
                def link(ins, n):
                    ins.then_inc(cl_step, 1)
                    dve.wait_ge(cl_step, t.count(6, n))

                def wide(x):
                    return x.unsqueeze(2).to_broadcast([P, BLK, CL])

                logits = spare[:, 0:BLK * CL].rearrange("p (b n) -> p b n", b=BLK)
                dve.wait_ge(pe["cl_turn"], t.count(1, 1))
                link(nc.vector.tensor_reduce(cl_stat[:, 0, :], logits, AX.X, ALU.max), 1)
                nc.vector.tensor_tensor(cl[:], logits, wide(cl_stat[:, 0, :]), ALU.subtract).then_inc(spare_free, 1)
                dve.wait_ge(cl_exp, t.count(1, 1))
                link(nc.vector.tensor_reduce(cl_stat[:, 1, :], cl[:], AX.X, ALU.add), 2)
                link(nc.vector.reciprocal(cl_stat[:, 2, :], cl_stat[:, 1, :]), 3)
                link(nc.vector.tensor_tensor(cl[:], cl[:], wide(cl_stat[:, 2, :]), ALU.mult), 4)
                link(nc.vector.tensor_reduce(cl_stat[:, 0, :], cl[:], AX.X, ALU.max), 5)
                nc.vector.tensor_tensor(cl_best[:], cl_best[:], cl[:], ALU.max)
                link(nc.vector.tensor_scalar(hit[:, bass.ds(t.count(BLK, 0), BLK)], cl_stat[:, 0, :], THRESHOLD, None,
                                             ALU.is_gt), 6)

            def serve(steps):
                for step, j, t in steps:
                    if step == "prep_x":
                        if t.first() and j == 0:
                            dve.wait_ge(in_mix_first, 16)
                        else:
                            dve.wait_ge(in_mix[t.par], 16 * BLK * t.fill() - (16 if t.par == 0 else 0))
                        wait(dve, lo["mix"], t.count(BLK, j))
                        nc.vector.tensor_tensor(mix[:], mixw[:, t.par, j:j + 1, :].to_broadcast([P, SPB, SEQ]),
                                                mix_mask[:], ALU.mult).then_inc(mix_made, 1)
                        dve.wait_ge(hi["x"], t.count(BLK, j + 1))
                        x_h, x_l = x_part(t, j)
                        minus(x_l[:], x_raw[:, j % 2, :], x_h[:]).then_inc(lo["x"], 1)
                        dve.wait_ge(hi["mix"], t.count(BLK, j + 1))
                        both = mix_part(t, j)
                        minus(both[:, P:], mix[:].rearrange("p s c -> p (s c)"), both[:, 0:P]).then_inc(lo["mix"], 1)
                    elif step == "prep_a":
                        dve.wait_ge(hi["ag"], t.count(1, 1))
                        for w in range(NW):
                            last = minus(by_window(da_lo)[:, w], ag_by_window[:, w], by_window(da_hi)[:, w])
                        last.then_inc(lo["ag"], 1)
                    elif step == "prep_b":
                        dve.wait_ge(hi["bd"], t.count(1, 1))
                        minus(bd_lo[:], bd_raw, bd_hi[:]).then_inc(lo["bd"], 1)
                    elif step == "small":
                        dve.wait_ge(in_small, 80)
                        dve.wait_ge(pool_const, 5)
                        for fold, n in ((fold_rt, NR), (fold_ct, CL)):
                            nc.vector.tensor_tensor(fold[:], ident[0:2 * n, 0:n], ident[0:2 * n, n:2 * n], ALU.add)
                        start(nc.vector.tensor_copy(map_f[:], map_i[:]), 3)
                        nc.vector.tensor_scalar(spread[:], e_index, map_f[:], SCALING, ALU.is_equal, ALU.mult)\
                            .then_inc(spread_made, 1)
                        at = 0
                        for w, (part_hi, part_lo) in enumerate((
                                (rt_hi, rt_lo), (a0_hi[:], a0_lo[:]), (b0_hi[:].unsqueeze(1), b0_lo[:].unsqueeze(1)),
                                (ct_hi, ct_lo))):
                            _, groups, n = part_hi.shape
                            dve.wait_ge(hi["const"], w + 1)
                            minus(part_lo, d_in[0][:, at:at + groups * n].rearrange("p (k n) -> p k n", k=groups),
                                  part_hi).then_inc(lo["const"], 1)
                            at += groups * n
                    elif step == "first_base":
                        dve.wait_ge(hi["d"], 1)
                        minus(base_lo[:].rearrange("p k n -> p (k n)"), d_in[1],
                              base_hi[:].rearrange("p k n -> p (k n)")).then_inc(lo["d"], 1)
                    elif step == "first_w":
                        rest_w(t, 0, j)
                    elif step == "prep_dense":
                        rest(Tile(0, 0))
                    elif step == "prep_ffn":
                        dve.wait_ge(hi["ffn"], 1)
                        minus(base_lo[:].rearrange("p k n -> p (k n)"), d_in[0],
                              base_hi[:].rearrange("p k n -> p (k n)")).then_inc(lo["ffn"], 1)
                    elif step == "cond":
                        dve.wait_ge(pe["cond"], t.count(CONDS, j + 1))
                        wait(dve, lo["xc"], t.count(CONDS, j - 1))
                        both = front_bank(t, step, j)[:].rearrange("p (k m n) -> p k n m", k=KH, m=2)
                        nc.vector.tensor_reduce(xc[:, j % 2], both, AX.X, ALU.add).then_inc(spare_free, 1)
                        for h in (range(max(j - 1, 0), j + (j == CONDS - 1)) if t.first() else (j,)):
                            dve.wait_ge(hi["xc"], t.count(CONDS, h + 1))
                            minus(xc_place(xc_lo, h), xc[:, h % 2], xc_place(xc_hi, h)).then_inc(lo["xc"], 1)
                    elif step == "turn":
                        route(t)
                    elif step == "probs":
                        dve.wait_ge(hi["probs"], t.count(1, 1))
                        minus(probs_t[QUAD:], spare[QUAD:2 * QUAD, :], probs_t[QUAD:]).then_inc(spare_free, 1)
                    elif step == "h":
                        dve.wait_ge(pe["h"], t.count(1, 1))
                        dve.wait_ge(spare_free, t.count(SPARE, USE["h", 0]))
                        nc.vector.tensor_tensor(hw[:], front_bank(t, step, j)[:], hw[:], ALU.mult)\
                            .then_inc(spare_free, 1)
                        dve.wait_ge(hi["hw"], t.count(1, 1))
                        minus(hw_lo[:], hw[:], hw_hi[:]).then_inc(lo["hw"], 1)
                    elif step == "base":
                        dve.wait_ge(pe["base"], t.count(KD, j + 1))
                        dve.wait_ge(in_res[j % 2], 16 * res_loads(t, j))
                        r = res_place(t, j)
                        nc.vector.scalar_tensor_tensor(r, front_bank(t, step, j)[:], bias0[:, j:j + 1], r,
                                                       ALU.add, ALU.add)\
                            .then_inc(spare_free, 1)
                        split = range(max(j - 1, 0), j + (j == KD - 1)) if t.first() else (j,)
                        for m in split:
                            dve.wait_ge(hi["x1"], t.count(KD, m + 1))
                            minus(x1_lo[t.par][:, m, :], res_place(t, m), x1_hi[t.par][:, m, :]).then_inc(lo["x1"], 1)
                    elif step == "lora":
                        dve.wait_ge(pe["lora"], t.count(2, j + 1))
                        masked(ranks[:, j, :], front_bank(t, step, j))\
                            .then_inc(spare_free, 3 if t.fixed and t.k == 0 and j == 1 else 1)
                        dve.wait_ge(hi["lora"], t.count(2, j + 1))
                        minus(gu_lo[j][:], ranks[:, j, :], gu_hi[j][:]).then_inc(lo["lora"], 1)
                    elif step == "gate":
                        if t.has_chunk(j + 1):
                            rest_w(t, j + 1, GATE)
                    elif step == "up":
                        dve.wait_ge(pe["up"], t.count(FC, j + 1))
                        dve.wait_ge(silu_done, t.count(FC, j + 1))
                        chunk = s[:, t.chunk(j)[0], :]
                        nc.vector.tensor_tensor(chunk, chunk, p_up[:], ALU.mult).then_inc(prod_done, 1)
                        if t.has_chunk(j + 1):
                            rest_w(t, j + 1, UP)
                    elif step == "down":
                        if t is None:
                            rest_act(Tile(0, 0), 0)
                            rest_w(Tile(0, 0), 0, DOWN)
                            continue
                        if j == FC - 1:
                            dve.wait_ge(pe["down"], t.count(FC, FC))
                            masked(ranks[:, 0, :], p_rank).then_inc(rank_made, 1)
                            dve.wait_ge(hi["rank"], t.count(1, 1))
                            minus(x_lo[:], ranks[:, 0, :], x_hi[:]).then_inc(lo["rank"], 1)
                        if t.has_chunk(j + 1):
                            rest_act(t, j + 1)
                            rest_w(t, j + 1, DOWN)
                    elif step == "final":
                        dve.wait_ge(pe["final"], t.count(1, 1))
                        for m in range(1, KD, 2):
                            last = nc.vector.tensor_copy(d_raw[:, m, :], p_d[m][:])
                        last.then_inc(d_dve, 1)
                        dve.wait_ge(hi["d"], t.count(1, 2))
                        minus(da_lo[:], d_raw[:].rearrange("p k n -> p (k n)"), da_hi[:]).then_inc(lo["d"], 1)
                    elif step == "cl_turn":
                        clusters(t)

            t0 = Tile(0, 0)

            def start(ins, n):
                ins.then_inc(start_step, 1)
                dve.wait_ge(start_step, n)

            dve.wait_ge(pool_const, 1)
            nc.vector.tensor_scalar(low5[:], part[:], SEQ - 1, None, ALU.bitwise_and)
            start(nc.vector.tensor_scalar(low4[:], part[:], RANK - 1, None, ALU.bitwise_and), 1)
            nc.vector.tensor_copy(low5f[:], low5[:])
            nc.vector.tensor_copy(part_f[:], part[:])
            start(nc.vector.tensor_copy(low4f[:], low4[:]), 2)
            dve.wait_ge(in_index, 32)
            nc.vector.tensor_scalar(subj_row[:], subj_i[:], float(SEQ), low5f[:], ALU.mult, ALU.add)\
                .then_inc(index_made, 1)
            nc.vector.tensor_scalar(lora_row[:], lora_i[:], float(RANK), low4f[:], ALU.mult, ALU.add)\
                .then_inc(index_made, 1)
            nc.vector.memset(cl_best[:], 0.0)
            nc.vector.memset(logit_pad[:], 0.0)
            nc.vector.memset(left_pad[:], 0.0)
            dve.wait_ge(pool_const, 7)
            serve(front_steps(t0))
            serve(seam_steps(None, t0))
            with dve.Fori(0, TILES // 2 - 1) as i:
                for k in range(2):
                    serve(body_steps(Tile(i, k), Tile(i, k + 1)))
            serve(body_steps(Tile(0, TILES - 2), Tile(0, TILES - 1)))
            serve(body_steps(Tile(0, TILES - 1), None))

            dve.wait_ge(cl_step, 6 * TILES)
            nc.vector.tensor_reduce(best_1, cl_best[:].rearrange("p b c -> p c b"), AX.X, ALU.max).then_inc(sel_step, 1)
            nc.vector.tensor_copy(ident_r, ident[:]).then_inc(identr_made, 1)
            dve.wait_ge(in_assign, 16)
            nc.vector.tensor_copy(assign_f, assign_i).then_inc(sel_step, 1)
            dve.wait_ge(sel_step, 2)
            nc.vector.tensor_scalar(onehot, assign_f, part_f[0:CL], None, ALU.is_equal).then_inc(sel_step, 1)
            dve.wait_ge(pe["best"], 1)
            nc.vector.tensor_reduce(best_2, spare[0:CL, 0:P], AX.X, ALU.max).then_inc(sel_step, 1)
            dve.wait_ge(sel_step, 4)
            nc.vector.tensor_scalar(sel, best_2, THRESHOLD, None, ALU.is_gt).then_inc(sel_step, 1)

            def spread_hits(t):
                nc.vector.tensor_copy(
                    hit_spread, hit[:, bass.ds(t.count(BLK, 0), BLK)].unsqueeze(2).to_broadcast([P, BLK, P]))\
                    .then_inc(hits_spread, 1)

            def output(t, q, after=None, split=False):
                dve.wait_ge(hits_copied, q.count(1, 1))
                for m in range(KD):
                    b = KD * q.par + m
                    dve.wait_ge(pe["dense"], q.count(KD, m + 1))
                    nc.vector.scalar_tensor_tensor(s[:, m % 2, :], dense_bank(q, m)[:], bias1[:, m:m + 1],
                                                   ranks[:, q.par, :], ALU.add, ALU.mult).then_inc(dense_free, 1)
                    dve.wait_ge(dense_free, q.count(KD, m + 1))
                    dve.wait_ge(in_x1[b], 16 * q.fill())
                    nc.vector.scalar_tensor_tensor(y_buf[b], s[:, m % 2, :], row_sel[:, m:m + 1], y_buf[b],
                                                   ALU.mult, ALU.add).then_inc(y_made, 1)
                    if m == 0 and after:
                        spread_hits(after)
                    if m == 1 and split:
                        rest(after)

            spread_hits(Tile(0, 0))
            rest(Tile(0, 1))
            dve.wait_ge(pe["rows"], 1)
            nc.vector.tensor_copy(row_sel, spare[:, 0:KD]).then_inc(rows_ready, 1)
            dve.wait_ge(rows_ready, 1)
            output(Tile(0, 0), Tile(0, 0), after=Tile(0, TILES - 1))
            output(Tile(0, TILES - 1), Tile(0, 1), after=Tile(0, 1))
            with dve.Fori(0, TILES // 2 - 2) as i:
                for k in (1, 2):
                    output(Tile(i, k), Tile(i, k + 1), after=Tile(i, k + 1), split=True)
            output(Tile(0, TILES - 3), Tile(0, TILES - 2), after=Tile(0, TILES - 2), split=True)
            output(Tile(0, TILES - 2), Tile(0, TILES - 1))

        @block.tensor
        def _(ten):
            def product(out, w, x, first=True, last=True):
                nc.tensor.matmul(out, w[0], x[0], start=first, stop=False, skip_group_check=True)
                nc.tensor.matmul(out, w[0], x[1], start=False, stop=False, skip_group_check=True)
                return nc.tensor.matmul(out, w[1], x[0], start=False, stop=last, skip_group_check=True)

            def cols(pr, a, b):
                return pr[0][:, a:b], pr[1][:, a:b]

            def chunk3(pr, k, a, b):
                return pr[0][:, k, a:b], pr[1][:, k, a:b]

            da, bd, act_p, x_p = (da_hi, da_lo), (bd_hi, bd_lo), (act_hi, act_lo), (x_hi, x_lo)
            xc_p, hw_p, base_p, a0_p, b0_p = (xc_hi, xc_lo), (hw_hi, hw_lo), (base_hi, base_lo), (a0_hi, a0_lo), (b0_hi, b0_lo)
            ad = (ad_hi, ad_lo)

            def product_packed(out, w, x, first, last):
                nc.tensor.matmul(out, w, x[0], start=first, stop=False, skip_group_check=True)
                return nc.tensor.matmul(out, w, x[1], start=False, stop=last, skip_group_check=True)

            def gate_up(t, c, q):
                ten.wait_ge(lo[("wg", "wu")[q]], t.count(FC, c + 1))
                wait(ten, (silu_done, prod_done)[q], t.count(FC, c))
                if c == 0 and q == 0:
                    ten.wait_ge(lo["x1"], t.count(KD, KD))
                bank_ = (p_gate, p_up)[q]
                w, x1 = (w_hi[q], w_lo[q]), (x1_hi[t.par], x1_lo[t.par])
                for k in range(KD):
                    product(bank_[:], cols(w, k * P, (k + 1) * P), chunk3(x1, k, 0, N), first=k == 0, last=False)
                ten.wait_ge(lo[("bg", "bu")[q]], t.count(FC, c + 1))
                if c == 0:
                    ten.wait_ge(lo["lora"], t.count(2, q + 1))
                for v in range(NW):
                    at = slice(v * WIN, (v + 1) * WIN)
                    mm = product(bank_[:, at], (b_hi[q][:, v, :], b_lo[q][:, v, :]),
                                 cols((gu_hi[q], gu_lo[q]), v * WIN, (v + 1) * WIN), first=False)
                mm.then_inc(pe[("gate", "up")[q]], 1)

            def down(t, c):
                ten.wait_ge(lo["act"], t.count(FC, c + 1))
                ten.wait_ge(lo["wd"], t.count(FC, c + 1))
                if c == 0:
                    wait(ten, d_act, t.count(1, 0))
                    wait(ten, d_dve, t.count(1, 0))
                    wait(ten, rank_made, t.count(1, 0))
                for m in range(KD):
                    product(p_d[m][:], cols((w_hi[DOWN], w_lo[DOWN]), m * P, (m + 1) * P), cols(act_p, 0, N),
                            first=c == 0, last=False)
                ten.wait_ge(lo["ad"], t.count(FC, c + 1))
                for v in range(NW):
                    w = [x[:, v * SPW:(v + 1) * SPW, :].rearrange("p s r -> p (s r)") for x in ad]
                    mm = product(p_rank[:, v * WIN:(v + 1) * WIN], w, cols(act_p, v * WIN, (v + 1) * WIN),
                                 first=c == 0 and v == 0, last=c == FC - 1)
                mm.then_inc(pe["down"], 1)

            def base_main(t, j):
                ten.wait_ge(lo["d"], 1)
                for k in range(KD):
                    product(front_bank(t, "base", j)[:], chunk3(base_p, k, j * P, (j + 1) * P),
                            chunk3(xc_p, k, 0, N), k == 0, False)

            def front(step, j, t):
                to = front_bank(t, step, j)
                if to is spare and not (t.first() and step == "cond"):
                    wait(ten, spare_free, t.count(SPARE, USE[step, j]))
                if step == "cond":
                    b, both, (x_h, x_l) = j // 2, mix_part(t, j // 2), x_part(t, j // 2)
                    ten.wait_ge(lo["x"], t.count(BLK, b + 1))
                    ten.wait_ge(lo["mix"], t.count(BLK, b + 1))
                    for i in range(KH):
                        feats = slice((j % 2 * KH + i) * P, (j % 2 * KH + i + 1) * P)
                        at = 2 * P * i
                        nc.tensor.matmul(to[:, at:at + 2 * P], x_h[:, feats], both, start=True, stop=False,
                                         skip_group_check=True)
                        mm = nc.tensor.matmul(to[:, at:at + P], x_l[:, feats], both[:, 0:P], start=False, stop=True,
                                              skip_group_check=True)
                elif step == "router":
                    ten.wait_ge(lo["const"], 4)
                    ten.wait_ge(lo["xc"], t.count(CONDS, CONDS))
                    for k in range(KD):
                        mm = product_packed(spare[0:2 * NR, :], rt[:, k, :], chunk3(xc_p, k, 0, N), k == 0, k == KD - 1)
                elif step == "turn":
                    passed(ten)
                    for b in range(BLK):
                        mm = nc.tensor.matmul(spare[:, b * NR:(b + 1) * NR], logit_t[:, b * P:(b + 1) * P], fold_rt[:],
                                              start=True, stop=True)
                elif step == "probs":
                    ten.wait_ge(chosen_done, t.count(1, 1))
                    passed(ten)
                    for b in range(BLK):
                        mm = nc.tensor.transpose(spare[0:2 * QUAD, b * P:(b + 1) * P],
                                                 cl[:, b, :], ident[:])
                elif step == "expand":
                    ten.wait_ge(spread_made, 1)
                    mm = nc.tensor.matmul(spare[:], spread[:].rearrange("n e r -> n (e r)"), probs_t,
                                          start=True, stop=True)
                elif step == "h":
                    for k in range(KD):
                        mm = product(to[:], chunk3(a0_p, k, 0, P), chunk3(xc_p, k, 0, N), k == 0, k == KD - 1)
                elif step == "base":
                    if not t.first():
                        base_main(t, j)
                    ten.wait_ge(lo["hw"], t.count(1, 1))
                    mm = product(to[:], cols(b0_p, j * P, (j + 1) * P), cols(hw_p, 0, N), False, True)
                elif step == "lora":
                    ten.wait_ge(lo["ag"], t.count(1, 1))
                    for v in range(NW):
                        for k in range(KD):
                            if j == 0 and v == 0:
                                ten.wait_ge(lo["x1"], t.count(KD, k + 1))
                            at = (v * 2 * KD + 2 * k + j) * P
                            mm = product(to[:, v * WIN:(v + 1) * WIN], cols(da, at, at + P),
                                         chunk3((x1_hi[t.par], x1_lo[t.par]), k, v * WIN, (v + 1) * WIN),
                                         k == 0, k == KD - 1)
                mm.then_inc(pe[step], 1)

            def serve(steps):
                for step, j, t in steps:
                    if step in ("gate", "up"):
                        gate_up(t, j, GATE if step == "gate" else UP)
                    elif step == "down" and t is not None:
                        down(t, j)
                    elif step == "early_h":
                        front("h", 0, t)
                    elif step == "early_base":
                        base_main(t, j)
                    elif (step, j) in USE and not (step == "h" and t.first()):
                        front(step, j, t)
                    elif step == "final":
                        ten.wait_ge(lo["rank"], t.count(1, 1))
                        ten.wait_ge(lo["bd"], t.count(1, 1))
                        for m in range(KD):
                            for v in range(NW):
                                w = [x[:, v, m * P:(m + 1) * P] for x in bd]
                                mm = product(p_d[m][:, v * WIN:(v + 1) * WIN], w,
                                             cols(x_p, v * WIN, (v + 1) * WIN), False, True)
                        mm.then_inc(pe["final"], 1)
                    elif step == "cluster":
                        ten.wait_ge(lo["d"], t.count(1, 2))
                        ten.wait_ge(spare_free, after_front(t))
                        for k in range(KD):
                            mm = product_packed(spare[:], ct[:, k, :], cols(da, k * N, (k + 1) * N),
                                                k == 0, k == KD - 1)
                        mm.then_inc(pe["cluster"], 1)
                    elif step == "cl_turn":
                        ten.wait_ge(spare_free, after_front(t) + 1)
                        passed(ten)
                        for b in range(BLK):
                            mm = nc.tensor.matmul(spare[:, b * CL:(b + 1) * CL], cl_t[:, b * P:(b + 1) * P],
                                                  fold_ct[:], start=True, stop=True)
                        mm.then_inc(pe["cl_turn"], 1)
                    elif step == "dense":
                        if j == 0:
                            ten.wait_ge(lo["dense"], 1)
                            ten.wait_ge(lo["ffn"], 1)
                        ten.wait_ge((silu_done, prod_done, rank_made, d_act)[j], (FC, FC, 1, 1)[j] * TILES)
                        dense(Tile(0, 0), Tile(0, 0), j)

            def dense(t, q, m):
                for k in range(KD):
                    at_home = t.fixed and t.k == TILES - 1
                    x = cols(da, k * N, (k + 1) * N) if at_home else chunk3((x1_hi[t.par], x1_lo[t.par]), k, 0, N)
                    mm = product(dense_bank(q, m)[:], chunk3(base_p, k, m * P, (m + 1) * P), x, k == 0, k == KD - 1)
                mm.then_inc(pe["dense"], 1)

            def hits(q):
                ten.wait_ge(hits_spread, q.count(1, 1))
                wait(ten, hits_copied, q.count(1, 0))
                for b in range(BLK):
                    mm = nc.tensor.matmul(spare[:, b * P:(b + 1) * P], hit_spread[:, b, :], ident_r,
                                          start=True, stop=True)
                mm.then_inc(pe["hits"], 1)

            t0 = Tile(0, 0)
            ten.wait_ge(pool_const, 5)
            serve(front_steps(t0))
            serve(seam_steps(None, t0))
            with ten.Fori(0, TILES // 2 - 1) as i:
                for k in range(2):
                    serve(body_steps(Tile(i, k), Tile(i, k + 1)))
            serve(body_steps(Tile(0, TILES - 2), Tile(0, TILES - 1)))
            serve(body_steps(Tile(0, TILES - 1), None))

            last, q0, q1 = Tile(0, TILES - 1), Tile(0, 0), Tile(0, 1)
            ten.wait_ge(d_dve, TILES)
            dense(last, q1, 0)
            dense(last, q1, 1)
            ten.wait_ge(sel_step, 1)
            ten.wait_ge(spare_free, SPARE * TILES + 2)
            nc.tensor.transpose(spare[0:CL, 0:P], best_1, ident[:]).then_inc(pe["best"], 1)
            dense(last, q1, 2)
            ten.wait_ge(sel_step, 5)
            for m in range(KD):
                mm = nc.tensor.matmul(spare[:, m:m + 1], onehot[:, m * P:(m + 1) * P], sel, start=True, stop=True)
            mm.then_inc(pe["rows"], 1)
            ten.wait_ge(rows_ready, 1)
            ten.wait_ge(identr_made, 1)
            hits(q0)
            ten.wait_ge(dense_free, 1)
            dense(last, q1, 3)
            hits(q1)

            def turn(t, q):
                ten.wait_ge(lo["dense"], t.count(1, 1))
                for m in range(KD):
                    if m < KD - 1:
                        ten.wait_ge(dense_free, q.count(KD, m + 2 - 2 * KD))
                    else:
                        ten.wait_ge(dense_free, q.count(KD, 0))
                    dense(t, q, m)
                    if m == 0:
                        hits(q)

            with ten.Fori(0, TILES // 2 - 1) as i:
                for k in (1, 2):
                    turn(Tile(i, k), Tile(i, k + 1))


def kernel(**inputs):
    import concourse.bacc as bacc
    from concourse.bass_utils import run_bass_kernel_spmd as run

    a = {k: np.asarray(v) for k, v in inputs.items()}

    def kmajor(w):
        return w.T.reshape(KD, P, -1).transpose(1, 0, 2).reshape(P, -1)

    def pad_f(w, axis):
        shape = list(w.shape)
        shape[axis] = FC * P
        full = np.zeros(shape, w.dtype)
        full[tuple(slice(0, n) for n in w.shape)] = w
        return full

    x = a["x"].reshape(TOKENS, D)
    router = np.zeros((NR, D), x.dtype)
    router[:NR - 1] = a["L0_ffn_router_W"]
    gate, up = (pad_f(a[n], 0).reshape(FC, P, KD, P).transpose(0, 3, 2, 1).reshape(FC, P, D)
                for n in ("L1_cond_W_gate", "L1_cond_W_up"))
    down = pad_f(a["L1_cond_W_down"], 1).reshape(D, FC, P).transpose(1, 2, 0)
    a_gu = np.stack([a["L1_cond_A_gate"][0], a["L1_cond_A_up"][0]])
    a_gu = a_gu.reshape(2, ADAPTERS, RANK, KD, P).transpose(1, 4, 3, 0, 2).reshape(ADAPTERS, P, -1)
    b_gu = pad_f(np.stack([a["L1_cond_B_gate"][0], a["L1_cond_B_up"][0]]), 2)
    b_gu = b_gu.reshape(2, ADAPTERS, FC, P, RANK).transpose(2, 1, 4, 0, 3).reshape(FC * ADAPTERS * RANK, 2 * P)
    a_dn = pad_f(a["L1_cond_A_down"][0], 2).reshape(ADAPTERS, RANK, FC, P).transpose(0, 3, 2, 1)
    subjects, loras = a["itok_B_0_30"], a["itok_B_2_6"]
    arrays = {
        "x_rows": x, "x_cols": x.T,
        "subj_rows": np.repeat(subjects.reshape(-1, SPB), SEQ, axis=1).T,
        "lora_rows": np.repeat(loras.reshape(-1, SPW), RANK, axis=1).T,
        "lora_index": loras.reshape(1, -1),
        "cond_w": a["L0_cond_weights"].reshape(-1, SEQ),
        "base_w": kmajor(a["L0_ffn_base_W"]), "base_b": a["L0_ffn_base_b"].reshape(KD, P).T,
        "router_w": kmajor(router), "router_b": a["L0_ffn_router_b"].reshape(1, -1),
        "a0": kmajor(a["L0_ffn_A"].reshape(-1, D)), "b0": a["L0_ffn_B"].transpose(0, 2, 1).reshape(-1, D),
        "expert_map": a["L0_ffn_expert_map"].reshape(-1, 1),
        "w1": np.stack([gate, up, down], axis=1),
        "a_gu": a_gu, "b_gu": b_gu, "a_dn": a_dn.reshape(ADAPTERS, P, -1),
        "b_dn": a["L1_cond_B_down"][0].transpose(0, 2, 1).reshape(-1, D),
        "ffn_w": kmajor(a["L1_ffn_weight"]), "ffn_b": a["L1_ffn_bias"].reshape(KD, P).T,
        "centroids": kmajor(a["L1_ffn_centroids"]), "assignments": a["L1_ffn_assignments"].reshape(1, -1),
    }
    arrays = {n: np.ascontiguousarray(v) for n, v in arrays.items()}
    nc = bacc.Bacc("TRN2", target_bir_lowering=False, num_devices=1)
    args = [nc.dram_tensor(n, v.shape, mybir.dt.from_np(v.dtype), kind="ExternalInput").ap() for n, v in arrays.items()]
    out = nc.dram_tensor("out_cols", (D, TOKENS), F32, kind="ExternalOutput").ap()
    adaln_ffn_kernel(nc, *args, out)
    got = run(nc, [arrays], core_ids=[0]).results[0]["out_cols"]
    return np.ascontiguousarray(got.T).reshape(BATCH, SEQ, D)
```
